# Optimizing a Trainium2 kernel written in Bass

```python
import numpy as np
import jax
import jax.numpy as jnp

def _softmax(x, axis=-1):
    return jax.nn.softmax(x, axis=axis)

def _gelu(x):
    return jax.nn.gelu(x, approximate=True)

def _silu(x):
    return jax.nn.silu(x)

def _sigmoid(x):
    return jax.nn.sigmoid(x)

def _layernorm(x, axis=-1, eps=1e-05):
    m = jnp.mean(x, axis=axis, keepdims=True)
    v = jnp.var(x, axis=axis, keepdims=True)
    return (x - m) / jnp.sqrt(v + eps)

def _scatter_add(tgt, idx, src, axis=0):
    return tgt.at[idx].add(src)

def _segment_sum(src, seg, n):
    return jax.ops.segment_sum(src, seg, n)
kernel_name = 'mk_adj_ffn_d2_adj_r2_dbea7a'

def setup_inputs(seed: int=0):
    np.random.seed(seed)
    _w = jnp.asarray

    def _rec_inputs():
        import jax
        import jax.numpy as jnp
        _gk = jax.random.key(seed)
        x = -0.0005207 + 1.001 * jax.random.normal(jax.random.fold_in(_gk, 1), (16, 512, 128), jnp.float32)
        _a = jax.random.bernoulli(jax.random.fold_in(_gk, 2), 0.03125, (16, 512, 512))
        adj = _a.astype(jnp.int32)
        return (x, adj)
    x, adj = _rec_inputs()

    def _L0_gnn_setup():
        import jax, jax.numpy as jnp
        import numpy as np
        DIM = 128
        HEADS = 8
        HEAD_DIM = DIM // HEADS
        DFF = 4 * DIM
        EPS = 1e-05

        def _layernorm(x, g, b):
            m = jnp.mean(x, axis=-1, keepdims=True)
            v = jnp.mean(jnp.square(x - m), axis=-1, keepdims=True)
            return (x - m) * jax.lax.rsqrt(v + EPS) * g + b
        key = jax.random.key(seed)
        ks = jax.random.split(key, 12)
        B, N = (8, 512)
        s = 1.0 / np.sqrt(DIM)
        x = jax.random.normal(ks[0], (B, N, DIM), dtype=jnp.float32)
        adj = jax.random.randint(ks[1], (B, N, N), 0, 2, dtype=jnp.int32)
        return {'x': x, 'adj': adj, 'Wqkv': jax.random.normal(ks[2], (3 * DIM, DIM), jnp.float32) * s, 'bqkv': jnp.zeros((3 * DIM,), jnp.float32), 'Wo': jax.random.normal(ks[3], (DIM, DIM), jnp.float32) * s, 'bo': jnp.zeros((DIM,), jnp.float32), 'ln1_g': jnp.ones((DIM,), jnp.float32), 'ln1_b': jnp.zeros((DIM,), jnp.float32), 'W1': jax.random.normal(ks[4], (DFF, DIM), jnp.float32) * s, 'b1': jnp.zeros((DFF,), jnp.float32), 'W2': jax.random.normal(ks[5], (DIM, DFF), jnp.float32) * (1.0 / np.sqrt(DFF)), 'b2': jnp.zeros((DIM,), jnp.float32), 'ln2_g': jnp.ones((DIM,), jnp.float32), 'ln2_b': jnp.zeros((DIM,), jnp.float32)}
    _L0_gnn_all = _L0_gnn_setup()
    _L0_gnn_in = {k: v for k, v in _L0_gnn_all.items() if k in ('Wqkv', 'bqkv', 'Wo', 'bo', 'ln1_g', 'ln1_b', 'W1', 'b1', 'W2', 'b2', 'ln2_g', 'ln2_b')}
    del _L0_gnn_all

    def _L0_ffn_setup():
        import jax, jax.numpy as jnp
        import numpy as np
        B, T, D, H, E = (16, 2048, 128, 256, 8)
        key = jax.random.key(seed)
        ks = jax.random.split(key, 5)
        x = jax.random.normal(ks[0], (B, T, D), dtype=jnp.float32)
        gate_w = jax.random.normal(ks[1], (D, E), dtype=jnp.float32) * 0.02
        gate_b = jnp.zeros((E,), dtype=jnp.float32)
        W1 = jax.random.normal(ks[2], (E, D, H), dtype=jnp.float32) * 0.02
        b1 = jnp.zeros((E, H), dtype=jnp.float32)
        W2 = jax.random.normal(ks[3], (E, H, D), dtype=jnp.float32) * 0.02
        b2 = jnp.zeros((E, D), dtype=jnp.float32)
        return {'x': x, 'gate_w': gate_w, 'gate_b': gate_b, 'W1': W1, 'b1': b1, 'W2': W2, 'b2': b2}
    _L0_ffn_all = _L0_ffn_setup()
    _L0_ffn_in = {k: v for k, v in _L0_ffn_all.items() if k in ('gate_w', 'gate_b', 'W1', 'b1', 'W2', 'b2')}
    del _L0_ffn_all

    def _L1_gnn_setup():
        import jax, jax.numpy as jnp
        import numpy as np
        B, N, D_IN, D_OUT, R = (8, 1024, 128, 128, 4)
        key = jax.random.key(seed)
        k1, k2, k3, k4 = jax.random.split(key, 4)
        x = jax.random.normal(k1, (B, N, D_IN), dtype=jnp.float32)
        adj = jnp.zeros((1,), dtype=jnp.float32)
        relation = jax.random.randint(k2, (B, N, N), 0, R + 1, dtype=jnp.int32)
        weight = jax.random.normal(k3, (R, D_IN, D_OUT), dtype=jnp.float32) * 0.05
        bias = jax.random.normal(k4, (D_OUT,), dtype=jnp.float32) * 0.05
        return {'x': x, 'adj': adj, 'relation': relation, 'weight': weight, 'bias': bias}
    _L1_gnn_all = _L1_gnn_setup()
    _L1_gnn_in = {k: v for k, v in _L1_gnn_all.items() if k in ('adj', 'weight', 'bias')}
    del _L1_gnn_all

    def _L1_ffn_setup():
        import jax, jax.numpy as jnp
        import numpy as np
        B, S, D, H, E, K = (8, 4096, 128, 512, 8, 2)
        key = jax.random.key(seed)
        ks = jax.random.split(key, 7)
        s_in = 1.0 / np.sqrt(D)
        s_hid = 1.0 / np.sqrt(H)
        return {'x': jax.random.normal(ks[0], (B, S, D), dtype=jnp.float32), 'Wg': jax.random.uniform(ks[1], (E, D), jnp.float32, -s_in, s_in), 'bg': jax.random.uniform(ks[2], (E,), jnp.float32, -s_in, s_in), 'W1': jax.random.uniform(ks[3], (E, H, D), jnp.float32, -s_in, s_in), 'b1': jax.random.uniform(ks[4], (E, H), jnp.float32, -s_in, s_in), 'W2': jax.random.uniform(ks[5], (E, D, H), jnp.float32, -s_hid, s_hid), 'b2': jax.random.uniform(ks[6], (E, D), jnp.float32, -s_hid, s_hid)}
    _L1_ffn_all = _L1_ffn_setup()
    _L1_ffn_in = {k: v for k, v in _L1_ffn_all.items() if k in ('Wg', 'bg', 'W1', 'b1', 'W2', 'b2')}
    del _L1_ffn_all
    return {'x': x, 'adj': adj, 'L0_gnn_Wqkv': _L0_gnn_in['Wqkv'], 'L0_gnn_bqkv': _L0_gnn_in['bqkv'], 'L0_gnn_Wo': _L0_gnn_in['Wo'], 'L0_gnn_bo': _L0_gnn_in['bo'], 'L0_gnn_ln1_g': _L0_gnn_in['ln1_g'], 'L0_gnn_ln1_b': _L0_gnn_in['ln1_b'], 'L0_gnn_W1': _L0_gnn_in['W1'], 'L0_gnn_b1': _L0_gnn_in['b1'], 'L0_gnn_W2': _L0_gnn_in['W2'], 'L0_gnn_b2': _L0_gnn_in['b2'], 'L0_gnn_ln2_g': _L0_gnn_in['ln2_g'], 'L0_gnn_ln2_b': _L0_gnn_in['ln2_b'], 'L0_ffn_gate_w': _L0_ffn_in['gate_w'], 'L0_ffn_gate_b': _L0_ffn_in['gate_b'], 'L0_ffn_W1': _L0_ffn_in['W1'], 'L0_ffn_b1': _L0_ffn_in['b1'], 'L0_ffn_W2': _L0_ffn_in['W2'], 'L0_ffn_b2': _L0_ffn_in['b2'], 'L1_gnn_adj': _L1_gnn_in['adj'], 'L1_gnn_weight': _L1_gnn_in['weight'], 'L1_gnn_bias': _L1_gnn_in['bias'], 'L1_ffn_Wg': _L1_ffn_in['Wg'], 'L1_ffn_bg': _L1_ffn_in['bg'], 'L1_ffn_W1': _L1_ffn_in['W1'], 'L1_ffn_b1': _L1_ffn_in['b1'], 'L1_ffn_W2': _L1_ffn_in['W2'], 'L1_ffn_b2': _L1_ffn_in['b2']}

def reference(x, adj, L0_gnn_Wqkv, L0_gnn_bqkv, L0_gnn_Wo, L0_gnn_bo, L0_gnn_ln1_g, L0_gnn_ln1_b, L0_gnn_W1, L0_gnn_b1, L0_gnn_W2, L0_gnn_b2, L0_gnn_ln2_g, L0_gnn_ln2_b, L0_ffn_gate_w, L0_ffn_gate_b, L0_ffn_W1, L0_ffn_b1, L0_ffn_W2, L0_ffn_b2, L1_gnn_adj, L1_gnn_weight, L1_gnn_bias, L1_ffn_Wg, L1_ffn_bg, L1_ffn_W1, L1_ffn_b1, L1_ffn_W2, L1_ffn_b2):
    import jax
    import jax.numpy as jnp

    def _L0_gnn_ref(x, adj, Wqkv, bqkv, Wo, bo, ln1_g, ln1_b, W1, b1, W2, b2, ln2_g, ln2_b):
        import jax, jax.numpy as jnp
        import numpy as np
        DIM = 128
        HEADS = 8
        HEAD_DIM = DIM // HEADS
        DFF = 4 * DIM
        EPS = 1e-05

        def _layernorm(x, g, b):
            m = jnp.mean(x, axis=-1, keepdims=True)
            v = jnp.mean(jnp.square(x - m), axis=-1, keepdims=True)
            return (x - m) * jax.lax.rsqrt(v + EPS) * g + b
        B, N, _ = x.shape
        eye = jnp.eye(N, dtype=bool)[None]
        allowed = (adj > 0) | (jnp.swapaxes(adj, 1, 2) > 0) | eye
        qkv = x @ Wqkv.T + bqkv
        q, k, v = jnp.split(qkv, 3, axis=-1)

        def heads(t):
            return t.reshape(B, N, HEADS, HEAD_DIM).transpose(0, 2, 1, 3)
        q, k, v = (heads(q), heads(k), heads(v))
        scale = 1.0 / np.sqrt(HEAD_DIM)
        scores = jnp.einsum('bhqd,bhkd->bhqk', q * scale, k)
        scores = jnp.where(allowed[:, None], scores, -jnp.inf)
        attn = jax.nn.softmax(scores, axis=-1)
        ctx = jnp.einsum('bhqk,bhkd->bhqd', attn, v)
        ctx = ctx.transpose(0, 2, 1, 3).reshape(B, N, DIM)
        attn_out = ctx @ Wo.T + bo
        x = _layernorm(x + attn_out, ln1_g, ln1_b)
        ff = jax.nn.relu(x @ W1.T + b1) @ W2.T + b2
        x = _layernorm(x + ff, ln2_g, ln2_b)
        return x

    def _L0_ffn_ref(x, gate_w, gate_b, W1, b1, W2, b2):
        import jax, jax.numpy as jnp
        import numpy as np
        B, T, D, H, E = (16, 2048, 128, 256, 8)
        Bb, Tt, Dd = x.shape
        Ee = gate_w.shape[1]
        xf = x.reshape(-1, Dd)
        N = xf.shape[0]
        logits = xf @ gate_w + gate_b
        probs = jax.nn.softmax(logits, axis=-1)
        top2_vals, top2_idx = jax.lax.top_k(probs, 2)
        cw = jnp.zeros((N, Ee), dtype=xf.dtype).at[jnp.arange(N)[:, None], top2_idx].add(top2_vals)

        def step(acc, params):
            w1, bb1, w2, bb2, we = params
            h = jax.nn.gelu(xf @ w1 + bb1, approximate=False)
            y = h @ w2 + bb2
            return (acc + we[:, None] * y, None)
        out, _ = jax.lax.scan(step, jnp.zeros_like(xf), (W1, b1, W2, b2, cw.T))
        return out.reshape(Bb, Tt, Dd)

    def _L1_gnn_ref(x, adj, relation, weight, bias):
        import jax, jax.numpy as jnp
        import numpy as np
        B, N, D_IN, D_OUT, R = (8, 1024, 128, 128, 4)
        rel_ids = jnp.arange(1, weight.shape[0] + 1, dtype=relation.dtype)
        masks = (relation[None] == rel_ids[:, None, None, None]).astype(x.dtype)
        h = jnp.einsum('rbnm,bmd->rbnd', masks, x)
        y = jnp.einsum('rbnd,rdo->bno', h, weight)
        return y + bias

    def _L1_ffn_ref(x, Wg, bg, W1, b1, W2, b2):
        import jax, jax.numpy as jnp
        import numpy as np
        B, S, D, H, E, K = (8, 4096, 128, 512, 8, 2)
        gate_scores = jnp.einsum('bsd,ed->bse', x, Wg) + bg
        topk_scores, topk_idx = jax.lax.top_k(gate_scores, K)
        topk_probs = jax.nn.softmax(topk_scores, axis=-1)
        combine = jnp.sum(topk_probs[..., None] * jax.nn.one_hot(topk_idx, E, dtype=x.dtype), axis=-2)
        out = jnp.zeros_like(x)
        for e in range(E):
            h = jax.nn.relu(jnp.einsum('bsd,hd->bsh', x, W1[e]) + b1[e])
            y = jnp.einsum('bsh,dh->bsd', h, W2[e]) + b2[e]
            out = out + combine[..., e:e + 1] * y
        return out
    x = x + _L0_gnn_ref(_layernorm(x, axis=-1), adj, L0_gnn_Wqkv, L0_gnn_bqkv, L0_gnn_Wo, L0_gnn_bo, L0_gnn_ln1_g, L0_gnn_ln1_b, L0_gnn_W1, L0_gnn_b1, L0_gnn_W2, L0_gnn_b2, L0_gnn_ln2_g, L0_gnn_ln2_b)
    x = x + _L0_ffn_ref(_layernorm(x, axis=-1), L0_ffn_gate_w, L0_ffn_gate_b, L0_ffn_W1, L0_ffn_b1, L0_ffn_W2, L0_ffn_b2)
    x = x + _L1_gnn_ref(_layernorm(x, axis=-1), L1_gnn_adj, adj, L1_gnn_weight, L1_gnn_bias)
    x = x + _L1_ffn_ref(_layernorm(x, axis=-1), L1_ffn_Wg, L1_ffn_bg, L1_ffn_W1, L1_ffn_b1, L1_ffn_W2, L1_ffn_b2)
    return x

_drawn_inputs = setup_inputs


def setup_inputs(seed=0):
    import zlib

    import numpy as np

    out = dict(_drawn_inputs(seed))
    spreads = {'L0_gnn_bqkv': (0.0, 0.1),
     'L0_gnn_bo': (0.0, 0.1),
     'L0_gnn_ln1_g': (1.0, 0.2),
     'L0_gnn_ln1_b': (0.0, 0.1),
     'L0_gnn_b1': (0.0, 0.1),
     'L0_gnn_b2': (0.0, 0.1),
     'L0_gnn_ln2_g': (1.0, 0.2),
     'L0_gnn_ln2_b': (0.0, 0.1),
     'L0_ffn_gate_b': (0.0, 0.553),
     'L0_ffn_b1': (0.0, 0.8),
     'L0_ffn_b2': (0.0, 0.374)}
    factors = {'L0_ffn_gate_w': 5.304,
     'L0_ffn_W1': 8.0,
     'L0_ffn_W2': 8.0,
     'L1_gnn_bias': 3.583,
     'L1_ffn_bg': 4.288,
     'L1_ffn_b1': 8.0,
     'L1_ffn_b2': 8.0}
    for name, (base, spread) in spreads.items():
        noise = np.random.default_rng([zlib.crc32(name.encode()), seed]).standard_normal(out[name].shape)
        drawn = base * np.exp(spread * noise) if base else spread * noise
        out[name] = jnp.asarray(drawn.astype(out[name].dtype))
    for name, factor in factors.items():
        out[name] = (out[name] * factor).astype(out[name].dtype)
    return out
```

```python
from contextlib import ExitStack

import concourse.bass as bass
from concourse import mybir

F32 = mybir.dt.float32
F32R = mybir.dt.float32r
BF16 = mybir.dt.bfloat16
I32 = mybir.dt.int32
U32 = mybir.dt.uint32
ALU = mybir.AluOpType
ACT = mybir.ActivationFunctionType
AX = mybir.AxisListType

P = 128
B, N, D = 16, 512, 128
NT = N // P
HEADS, HD = 8, 16
GROUPS, GH = 2, 4
NEG = -1.0e30
EPS = 1e-5
PAIRS = B // 2


class Semaphores:

    def __init__(self, c, nc):
        self.nc, self.all = nc, []
        c.callback(self.clear)

    def clear(self):
        self.nc.clear_and_free_semaphores(self.all)
        self.nc.all_engine_barrier()

    def __call__(self, name):
        self.all.append(self.nc.alloc_semaphore(name))
        return self.all[-1]


class Own:

    def __init__(self, eng, sem, turn, per):
        self.eng, self.sem, self.per, self.k = eng, sem, per, 0
        self.base = turn * per
        self.last = (sem, self.base + 1)

    def wait(self):
        self.eng.wait_ge(*self.last)

    def done(self, ins):
        self.k += 1
        self.last = (self.sem, self.base + (self.k + 1))
        ins.then_inc(self.sem, 1)

    def tell(self, ins, sem, value):
        self.last = (sem, value)
        ins.then_inc(sem, 1)

    def end(self):
        assert self.k == self.per, (self.k, self.per)


def bcast_rows(ap, n):
    return ap.partition_broadcast(n)


def gate(eng, sem, value, ticks):
    eng.wait_ge(sem, value)
    eng.sem_inc(ticks, 1)


class Norm:
    PER = 2 * NT + 2 * NT + 5 + 2 * NT

    def __init__(self, c, nc, fresh, name):
        sb = lambda n, s, d: c.enter_context(nc.sbuf_tensor(name + n, s, d))
        sem = lambda n: fresh(name + n)
        self.nc = nc
        self.stats = sb("stats", [P, 2, NT, 6], F32)
        self.mv = sb("mv", [P, 2, NT, 2], F32)
        self.std = sb("std", [P, 2, NT], F32)
        self.r = sb("r", [P, 2, NT], F32)
        self.s = sb("s", [P, 2, NT], F32)
        self.var_ready, self.std_ready = sem("var_ready"), sem("std_ready")

    def stats_of(self, own, src, h):
        own.wait()
        for t in range(NT):
            own.done(self.nc.vector.bn_stats(self.stats[:, h, t], src[:, t]))

    def variance(self, dve, own, nth, ticks):
        gate(dve, *own.last, ticks)
        for h in range(2):
            for t in range(NT):
                ins = self.nc.vector.bn_aggr(self.mv[:, h, t], self.stats[:, h, t])
                own.done(ins) if (h, t) != (1, NT - 1) else own.tell(ins, self.var_ready, nth + 1)

    def root(self, act, nth, eps):
        act.wait_ge(self.var_ready, nth + 1)
        self.nc.scalar.activation(self.std[:], self.mv[:, :, :, 1], ACT.Sqrt, bias=eps[:], scale=1.0).then_inc(self.std_ready, 1)

    def inverse(self, dve, own, nth):
        v, r, s = self.nc.vector, self.r, self.s
        dve.wait_ge(self.std_ready, nth + 1)
        own.done(v.reciprocal(r[:], self.std[:]))
        own.wait()
        own.done(v.tensor_tensor(s[:], r[:], r[:], ALU.mult))
        own.wait()
        own.done(v.scalar_tensor_tensor(out=s[:], in0=self.mv[:, :, :, 1], scalar=EPS, in1=s[:], op0=ALU.add, op1=ALU.mult))
        own.wait()
        own.done(v.tensor_scalar(s[:], s[:], -0.5, 1.5, ALU.mult, ALU.add))
        own.wait()
        own.done(v.tensor_tensor(r[:], r[:], s[:], ALU.mult))

    def apply(self, own, src, dst, h, last=None):
        own.wait()
        for t in range(NT):
            ins = self.nc.vector.tensor_scalar(dst[:, t], src[:, t], self.mv[:, h, t, 0:1], self.r[:, h, t:t + 1], ALU.subtract, ALU.mult)
            own.tell(ins, *last) if last and t == NT - 1 else own.done(ins)


def prepare(nc, x, adj, wqkv, bqkv, ident, identb, xn_d, qk_d, v_d, adjT_d, neg_d):
    with ExitStack() as c:
        sb = lambda n, s, d: c.enter_context(nc.sbuf_tensor("p_" + n, s, d))
        pb = lambda n, s, d: c.enter_context(nc.psum_tensor("p_" + n, s, d))
        fresh = Semaphores(c, nc)
        sem = lambda n: fresh("p_" + n)
        two = lambda n: [sem(n + "0"), sem(n + "1")]
        adj_i = sb("adj_i", [P, 2, NT, N], I32)
        adj_b = sb("adj_b", [P, 2, NT, N], BF16)
        adjT = sb("adjT", [P, 2, NT, N], BF16)
        neg = sb("neg", [P, 2, NT, N], BF16)
        wT = sb("wT", [P, 3 * D], F32)
        bqk = sb("bqk", [P, 2], F32)
        bqk_s = sb("bqk_s", [P, 2], F32)
        bv = sb("bv", [P, D], F32)
        eps = sb("eps", [P, 1], F32)
        closed = sb("closed", [P, NT, N], BF16)
        xn = sb("xn", [P, 2, NT, D], F32)
        xT = sb("xT", [P, 2, N], F32)
        qk = sb("qk", [P, 2, 2, N], F32)
        parts = sb("parts", [P, 2, 2, 2, N], F32R)
        va = sb("va", [P, 2, NT, HEADS, 32], F32)
        ps_x = pb("ps_x", [P, N], F32)
        ps_q = pb("ps_q", [P, N], F32)
        ps_k = pb("ps_k", [P, N], F32)
        ps_v = pb("ps_v", [P, N], F32)
        ps_a = [pb(f"ps_a{j}", [P, 1024], BF16) for j in range(NT)]

        weights_in = sem("weights_in")
        adj_in, x_in = two("adj_in"), two("x_in")
        adj_cast, adjT_ps, adjT_sb = sem("adj_cast"), sem("adjT_ps"), sem("adjT_sb")
        xn_ready = sem("xn")
        norm = Norm(c, nc, fresh, "p_n")
        sp_ticks, pool_ticks, dve_ticks = sem("sp_ticks"), sem("pool_ticks"), sem("dve_ticks")
        xT_ps, xT_sb, qk_ps, qk_sb, v_ps, v_sb = (sem(n) for n in ("xT_ps", "xT_sb", "qk_ps", "qk_sb", "v_ps", "v_sb"))
        parts_ready, neg_ready, consts = sem("parts"), sem("neg_ready"), sem("consts")
        parts_out, v_out, adjT_out, neg_out = two("parts_out"), two("v_out"), two("adjT_out"), two("neg_out")
        xn_out = two("xn_out")
        dve_own = sem("dve_own")

        with nc.Block() as block:
            @block.sync
            def _(sp):
                def load(b, h):
                    sp.dma_start(adj_i[:, h], adj[b].rearrange("(t p) m -> p t m", p=P)).then_inc(adj_in[h], 16)
                    sp.dma_start(xn[:, h], x[b].rearrange("(t p) d -> p t d", p=P)).then_inc(x_in[h], 16)

                def store(b, h):
                    gate(sp, xn_ready, b + 1, sp_ticks)
                    sp.dma_start(xn_d[b].rearrange("(t p) d -> p t d", p=P), xn[:, h]).then_inc(xn_out[h], 16)
                    gate(sp, v_sb, b + 2, sp_ticks)
                    sp.dma_start(v_d[b], va[:, h]).then_inc(v_out[h], 16)
                    gate(sp, parts_ready, b + 1, sp_ticks)
                    sp.dma_start(qk_d[b], parts[:, h].bitcast(F32)).then_inc(parts_out[h], 16)
                    gate(sp, adjT_sb, NT * (b + 2), sp_ticks)
                    sp.dma_start(adjT_d[b], adjT[:, h]).then_inc(adjT_out[h], 16)
                    gate(sp, neg_ready, b + 3, sp_ticks)
                    sp.dma_start(neg_d[b], neg[:, h]).then_inc(neg_out[h], 16)

                sp.dma_start(wT[:], wqkv).then_inc(weights_in, 16)
                sp.dma_start(bqk[:], bqkv[0:2 * D].rearrange("(a p) -> p a", p=P), allow_slow_non_contiguous=True).then_inc(weights_in, 16)
                sp.dma_start(bv[:], bcast_rows(bqkv[2 * D:3 * D], P)).then_inc(weights_in, 16)
                for h in range(2):
                    load(h, h)
                with sp.Fori(0, PAIRS - 1) as i:
                    for h in range(2):
                        store(i * 2 + h, h)
                        gate(sp, adj_cast, i * 2 + (h + 1), sp_ticks)
                        gate(sp, xn_out[h], i * 16 + 16, sp_ticks)
                        load(i * 2 + (h + 2), h)
                for h in range(2):
                    store(B - 2 + h, h)
                for h in range(2):
                    sp.wait_ge(xn_out[h], 16 * PAIRS)
                    for s in (parts_out, v_out, adjT_out, neg_out):
                        sp.wait_ge(s[h], 16 * (PAIRS + 1))

            @block.gpsimd
            def _(pool):
                nc.gpsimd.memset(eps[:], EPS).then_inc(consts, 1)
                nc.gpsimd.memset(va[:], 0.0).then_inc(consts, 1)
                pool.wait_ge(consts, 2)
                nc.gpsimd.memset(va[:, :, :, :, HD:HD + 1], 1.0).then_inc(consts, 1)
                for h in range(2):
                    for s in (parts_out, v_out, adjT_out, neg_out):
                        pool.sem_inc(s[h], 16)
                nc.gpsimd.memset(closed[:], NEG).then_inc(consts, 1)
                pool.wait_ge(consts, 4)
                nc.gpsimd.affine_select(out=closed[:], in_=closed[:], compare_op=ALU.not_equal, fill=0.0,
                                        base=0, pattern=[[P, NT], [-1, N]], channel_multiplier=1).then_inc(consts, 1)
                pool.sem_inc(neg_ready, 2)
                with pool.Fori(0, PAIRS) as i:
                    for h in range(2):
                        b = 2 * i + h
                        gate(pool, adj_in[h], i * 16 + 16, pool_ticks)
                        gate(pool, neg_ready, b + 1, pool_ticks)
                        nc.gpsimd.tensor_scalar(adj_b[:, h], adj_i[:, h], 0.0, 5.0, ALU.max, ALU.min).then_inc(adj_cast, 1)

            @block.scalar
            def _(act):
                act.wait_ge(consts, 5)
                act.wait_ge(weights_in, 48)
                nc.scalar.mul(bqk_s[:, 0:1], bqk[:, 0:1], 0.25).then_inc(consts, 1)
                act.wait_ge(consts, 6)
                act.sem_inc(adjT_sb, NT)
                act.sem_inc(xT_sb, 1)
                act.sem_inc(qk_sb, 2)
                with act.Fori(0, PAIRS) as i:
                    norm.root(act, i, eps)
                    for h in range(2):
                        b = 2 * i + h
                        act.wait_ge(adjT_out[h], 16 * i + 16)
                        for j in range(NT):
                            act.wait_ge(adjT_ps, NT * (b + 1) + (j + 1))
                            nc.scalar.copy(adjT[:, h, j], ps_a[j][:, 0:N]).then_inc(adjT_sb, 1)
                        act.wait_ge(xT_ps, b + 1)
                        nc.scalar.copy(xT[:, h], ps_x[:]).then_inc(xT_sb, 1)
                        act.wait_ge(qk_ps, 2 * b + 1)
                        nc.scalar.activation(qk[:, h, 0], ps_q[:], ACT.Identity, bias=bqk_s[:, 0:1], scale=0.25).then_inc(qk_sb, 1)
                        act.wait_ge(qk_ps, 2 * b + 2)
                        nc.scalar.activation(qk[:, h, 1], ps_k[:], ACT.Identity, bias=bqk[:, 1:2], scale=1.0).then_inc(qk_sb, 1)

            @block.vector
            def _(dve):
                PER = Norm.PER - 3 + 2 * 2
                dve.wait_ge(consts, 5)
                dve.wait_ge(weights_in, 48)
                dve.sem_inc(dve_own, 1)
                dve.sem_inc(v_sb, 1)
                with dve.Fori(0, PAIRS) as i:
                    own = Own(dve, dve_own, i, PER)
                    for h in range(2):
                        dve.wait_ge(x_in[h], 16 * i + 16)
                        norm.stats_of(own, xn[:, h], h)
                    norm.variance(dve, own, i, dve_ticks)
                    norm.inverse(dve, own, i)
                    for h in range(2):
                        norm.apply(own, xn[:, h], xn[:, h], h, (xn_ready, 2 * i + (h + 1)))
                    for h in range(2):
                        b = 2 * i + h
                        dve.wait_ge(adjT_sb, NT * (b + 2))
                        dve.wait_ge(neg_out[h], 16 * i + 16)
                        own.wait()
                        own.done(nc.vector.tensor_tensor(neg[:, h], adj_b[:, h], adjT[:, h], ALU.max))
                        own.wait()
                        own.tell(nc.vector.scalar_tensor_tensor(
                            out=neg[:, h].rearrange("p t m -> p (t m)"), in0=neg[:, h].rearrange("p t m -> p (t m)"), scalar=0.0,
                            in1=closed[:].rearrange("p t m -> p (t m)"), op0=ALU.is_le, op1=ALU.mult), neg_ready, b + 3)
                        dve.wait_ge(v_ps, b + 1)
                        dve.wait_ge(v_out[h], 16 * i + 16)
                        own.wait()
                        own.tell(nc.vector.tensor_tensor(
                            va[:, h, :, :, 0:HD], ps_v[:].rearrange("p (t h d) -> p t h d", t=NT, h=HEADS),
                            bv[:].rearrange("p (o h d) -> p o h d", o=1, h=HEADS).broadcast_to([P, NT, HEADS, HD]), ALU.add), v_sb, b + 2)
                        dve.wait_ge(qk_sb, 2 * b + 4)
                        dve.wait_ge(parts_out[h], 16 * i + 16)
                        own.wait()
                        own.done(nc.vector.tensor_copy(parts[:, h, 0], qk[:, h]))
                        own.wait()
                        own.tell(nc.vector.tensor_tensor(parts[:, h, 1], qk[:, h], parts[:, h, 0].bitcast(F32), ALU.subtract), parts_ready, b + 1)
                    own.end()

            @block.tensor
            def _(pe):
                pe.wait_ge(weights_in, 48)
                pe.sem_inc(adjT_ps, NT)
                with pe.Fori(0, PAIRS) as i:
                    for h in range(2):
                        b = 2 * i + h
                        pe.wait_ge(adj_cast, b + 1)
                        for j in range(NT):
                            pe.wait_ge(adjT_sb, NT * b + (j + 1))
                            for t in range(NT):
                                mm = nc.tensor.transpose(ps_a[j][:, t * P:(t + 1) * P], adj_b[:, h, t, j * P:(j + 1) * P], identb[:])
                            mm.then_inc(adjT_ps, 1)
                        pe.wait_ge(xn_ready, b + 1)
                        pe.wait_ge(xT_sb, b + 1)
                        for t in range(NT):
                            mm = nc.tensor.transpose(ps_x[:, t * P:(t + 1) * P], xn[:, h, t], ident[:])
                        mm.then_inc(xT_ps, 1)
                        pe.wait_ge(xT_sb, b + 2)
                        pe.wait_ge(qk_sb, 2 * b + 1)
                        nc.tensor.matmul(ps_q[:], wT[:, 0:D], xT[:, h], start=True, stop=True).then_inc(qk_ps, 1)
                        pe.wait_ge(qk_sb, 2 * b + 2)
                        nc.tensor.matmul(ps_k[:], wT[:, D:2 * D], xT[:, h], start=True, stop=True).then_inc(qk_ps, 1)
                        pe.wait_ge(v_sb, b + 1)
                        for t in range(NT):
                            mm = nc.tensor.matmul(ps_v[:, t * P:(t + 1) * P], xT[:, h, t * P:(t + 1) * P], wT[:, 2 * D:3 * D], start=True, stop=True)
                        mm.then_inc(v_ps, 1)


UNITS = B * GROUPS
AHEAD = 4
LOADS = 9
TILES = NT * GH
QK1_OF_SLOT = (6, 6, 4, 0)


def attend(nc, identf, identb, qk_d, v_d, neg_d, ctx_d):
    with ExitStack() as c:
        sb = lambda n, s, d: c.enter_context(nc.sbuf_tensor("a_" + n, s, d))
        pb = lambda n, s, d: c.enter_context(nc.psum_tensor("a_" + n, s, d))
        fresh = Semaphores(c, nc)
        sem = lambda n: fresh("a_" + n)
        many = lambda n: [sem(f"{n}{k}") for k in range(AHEAD)]
        SHIFT = 3 * HD
        qs = [sb(f"qs{k}", [P, GH, N], F32R) for k in range(AHEAD)]
        ks = [sb(f"ks{k}", [P, GH, N], F32R) for k in range(AHEAD)]
        nm = sb("nm", [P, AHEAD, NT, N], BF16)
        va = sb("va", [P, AHEAD, NT, GH, 32], F32)
        rows = sb("rows", [1, 2, GH * N], F32)
        junk = sb("junk", [P, 4, N], BF16)
        mx = sb("mx", [P, 2, TILES], F32)
        nmx = sb("nmx", [TILES, 2, P], F32R)
        pt = sb("pt", [P, 8, N], F32)
        ctx = sb("ctx", [P, 2, N], F32)
        s1 = [pb(f"s1_{k}", [P, N], F32) for k in range(2)]
        s2 = [pb(f"s2_{k}", [P, N], F32) for k in range(GH)]
        ps_c = pb("ps_c", [P, N], F32)
        ps_m = pb("ps_m", [P, N], F32)
        unit_in, shift_in = many("unit_in"), many("shift_in")
        ctx_out = [sem("ctx_out0"), sem("ctx_out1")]
        consts, s1_ps, max_done, mxT_ps, nmx_ready = (sem(n) for n in ("consts", "s1_ps", "max_done", "mxT_ps", "nmx_ready"))
        s2_ps, exp_done, pv_done, ctx_sb = (sem(n) for n in ("s2_ps", "exp_done", "pv_done", "ctx_sb"))
        sp_ticks, dve_ticks = sem("sp_ticks"), sem("dve_ticks")

        with nc.Block() as block:
            @block.sync
            def _(sp):
                def load(b, g, k, turn):
                    heads = slice(g * GH, (g + 1) * GH)
                    if turn is not None:
                        gate(sp, ctx_sb, turn, sp_ticks)
                    src = qk_d[b].rearrange("(h d) a q n -> d h a q n", d=HD)
                    for s, (qpart, kpart) in enumerate(((0, 0), (0, 1), (1, 0))):
                        at = slice(s * HD, (s + 1) * HD)
                        sp.dma_start(qs[k][at].bitcast(F32), src[:, heads, qpart, 0]).then_inc(unit_in[k], 16)
                        sp.dma_start(ks[k][at].bitcast(F32), src[:, heads, kpart, 1]).then_inc(unit_in[k], 16)
                    sp.dma_start(qs[k][SHIFT:SHIFT + 1].bitcast(F32).rearrange("p h n -> p (h n)"), rows[:, 0]).then_inc(unit_in[k], 16)
                    sp.dma_start(nm[:, k], neg_d[b]).then_inc(unit_in[k], 16)
                    sp.dma_start(va[:, k], v_d[b][:, :, heads]).then_inc(unit_in[k], 16)

                def shift(u, k):
                    gate(sp, nmx_ready, u + 1, sp_ticks)
                    sp.dma_start(qs[k][SHIFT:SHIFT + 1].bitcast(F32).rearrange("o h n -> o (h n)"), nmx[:, k % 2].bitcast(F32)).then_inc(shift_in[k], 16)

                def store(u, k):
                    gate(sp, ctx_sb, u + 2, sp_ticks)
                    sp.dma_start(ctx_d[u], ctx[:, k % 2]).then_inc(ctx_out[k % 2], 16)

                sp.wait_ge(consts, 2 * AHEAD + 2)
                for k in range(AHEAD):
                    sp.dma_start(ks[k][SHIFT:SHIFT + 1].bitcast(F32).rearrange("p h n -> p (h n)"), rows[:, 1]).then_inc(unit_in[k], 16)
                for k in range(3):
                    load(k // 2, k % 2, k, None)
                shift(0, 0)
                with sp.Fori(0, PAIRS - 1) as i:
                    for w in range(4):
                        load(2 * i + (w + 3) // 2, (w + 3) % 2, (w + 3) % 4, 4 * i + w + 1)
                        shift(4 * i + (w + 1), (w + 1) % 4)
                        store(4 * i + w, w)
                u = UNITS - 4
                for w in range(4):
                    if w == 0:
                        load(B - 1, 1, 3, u + 1)
                    if w < 3:
                        shift(u + w + 1, (w + 1) % 4)
                    store(u + w, w)
                for k in range(2):
                    sp.wait_ge(ctx_out[k], 16 * (UNITS // 2 + 1))

            @block.gpsimd
            def _(pool):
                nc.gpsimd.memset(rows[:, 0], 0.0).then_inc(consts, 1)
                nc.gpsimd.memset(rows[:, 1], 1.0).then_inc(consts, 1)
                for k in range(AHEAD):
                    nc.gpsimd.memset(qs[k][:].bitcast(F32), 0.0).then_inc(consts, 1)
                    nc.gpsimd.memset(ks[k][:].bitcast(F32), 0.0).then_inc(consts, 1)

            @block.scalar
            def _(act):
                def unit(i, w, last):
                    u = 4 * i + w
                    for kt in range(NT):
                        act.wait_ge(pv_done, 4 * u + (kt + 1))
                        for hh in range(GH):
                            m = 16 * u + (kt * GH + hh)
                            act.wait_ge(s2_ps, m + 1)
                            nc.scalar.activation(pt[:, (kt * GH + hh) % 8], s2[hh][:], ACT.Exp).then_inc(exp_done, 1)
                        if kt == 2 and not last:
                            k = (w + 1) % 4
                            act.wait_ge(mxT_ps, u + 2)
                            act.wait_ge(shift_in[(w + 3) % 4], shift_count(i, w))
                            nc.scalar.activation(nmx[:, k % 2], ps_m[0:TILES, 0:P], ACT.Copy, scale=-1.0).then_inc(nmx_ready, 1)

                def shift_count(i, w):
                    return 16 * i + (16 if w == 0 else 32)

                act.sem_inc(exp_done, 4)
                for k in range(AHEAD):
                    act.sem_inc(shift_in[k], 16)
                act.wait_ge(mxT_ps, 1)
                nc.scalar.activation(nmx[:, 0], ps_m[0:TILES, 0:P], ACT.Copy, scale=-1.0).then_inc(nmx_ready, 1)
                with act.Fori(0, PAIRS - 1) as i:
                    for w in range(4):
                        unit(i, w, False)
                for w in range(4):
                    unit(PAIRS - 1, w, w == 3)

            @block.vector
            def _(dve):
                def maxima(u, k, nth):
                    gate(dve, unit_in[k], nth, dve_ticks)
                    for j in range(TILES):
                        qt, hh = divmod(j, GH)
                        n = 16 * u + j
                        gate(dve, max_done, n + 1, dve_ticks)
                        gate(dve, s1_ps, n + 1, dve_ticks)
                        nc.vector.tensor_tensor_reduce(
                            out=junk[:, j % 4], in0=s1[j % 2][:], in1=nm[:, k, qt], scale=1.0, scalar=-3.0e38,
                            op0=ALU.add, op1=ALU.max, accum_out=mx[:, k % 2, hh * NT + qt:hh * NT + qt + 1]).then_inc(max_done, 1)

                def result(u, w, turn):
                    gate(dve, pv_done, 4 * u + 6, dve_ticks)
                    gate(dve, ctx_out[w % 2], turn, dve_ticks)
                    nc.vector.tensor_copy(ctx[:, w % 2], ps_c[:]).then_inc(ctx_sb, 1)

                dve.sem_inc(max_done, 4)
                dve.sem_inc(ctx_sb, 1)
                for k in range(2):
                    dve.sem_inc(ctx_out[k], 16)
                maxima(0, 0, 16 * (LOADS + 1))
                with dve.Fori(0, PAIRS - 1) as i:
                    for w in range(4):
                        k = (w + 1) % 4
                        maxima(4 * i + (w + 1), k, 16 * LOADS * i + 16 * (LOADS * (2 if w == 3 else 1) + 1))
                        result(4 * i + w, w, 32 * i + 16 * (w // 2 + 1))
                i = PAIRS - 1
                for w in range(4):
                    if w < 3:
                        maxima(4 * i + w + 1, w + 1, 16 * (LOADS * (i + 1) + 1))
                    result(4 * i + w, w, 32 * i + 16 * (w // 2 + 1))

            @block.tensor
            def _(pe):
                def by_query(u, k, js):
                    for j in js:
                        qt, hh = divmod(j, GH)
                        pe.wait_ge(max_done, 16 * u + (j + 3))
                        nc.tensor.matmul(s1[j % 2][:], qs[k][:, hh, qt * P:(qt + 1) * P], ks[k][:, hh], start=True, stop=True).then_inc(s1_ps, 1)

                def maxima_turned(u, k):
                    pe.wait_ge(max_done, 16 * u + 20)
                    pe.wait_ge(nmx_ready, u)
                    nc.tensor.transpose(ps_m[0:TILES, 0:P], mx[:, k % 2], identf[:]).then_inc(mxT_ps, 1)

                def by_key(u, k, kt):
                    for hh in range(GH):
                        pe.wait_ge(exp_done, 16 * u + (kt * GH + hh + 1))
                        nc.tensor.matmul(s2[hh][:], ks[k][:, hh, kt * P:(kt + 1) * P], qs[k][:, hh], start=True, stop=False)
                        nc.tensor.matmul(s2[hh][:], identb[:], nm[:, k, kt], start=False, stop=True).then_inc(s2_ps, 1)

                def values(u, k, kt):
                    if kt == 0:
                        pe.wait_ge(ctx_sb, u + 1)
                    for hh in range(GH):
                        pe.wait_ge(exp_done, 16 * u + (kt * GH + hh + 5))
                        mm = nc.tensor.matmul(ps_c[32 * hh:32 * hh + 32, :], va[:, k, kt, hh], pt[:, (kt * GH + hh) % 8],
                                              start=(kt == 0), stop=(kt == NT - 1))
                    mm.then_inc(pv_done, 1)

                def unit(i, w, last, nth):
                    u, k = 4 * i + w, (w + 1) % 4
                    pe.wait_ge(shift_in[w], 16 * i + 32)
                    if not last:
                        pe.wait_ge(unit_in[k], nth)
                    js = list(range(TILES))
                    for kt in range(NT):
                        by_key(u, w, kt)
                        if not last:
                            by_query(u + 1, k, [js.pop(0) for _ in range(QK1_OF_SLOT[kt])])
                        if kt >= 1:
                            values(u, w, kt - 1)
                        if kt == 2 and not last:
                            maxima_turned(u + 1, k)
                    values(u, w, NT - 1)

                pe.sem_inc(pv_done, 2)
                pe.wait_ge(unit_in[0], 16 * (LOADS + 1))
                by_query(0, 0, range(TILES))
                pe.wait_ge(max_done, 20)
                nc.tensor.transpose(ps_m[0:TILES, 0:P], mx[:, 0], identf[:]).then_inc(mxT_ps, 1)
                with pe.Fori(0, PAIRS - 1) as i:
                    for w in range(4):
                        unit(i, w, False, 16 * LOADS * i + 16 * (LOADS * (2 if w == 3 else 1) + 1))
                for w in range(4):
                    unit(PAIRS - 1, w, w == 3, 16 * (LOADS * PAIRS + 1))


E_ = 8
TILE = 512
CAP = B * N + TILE
ROWS = E_ * CAP + 2 * TILE
LAST = ROWS - TILE
MOE_TILES = 2 * B * N // TILE + E_


def wide(ap, shape):
    return ap.rearrange("p (o d) -> p o d", o=1).broadcast_to(shape)


class Router:

    def __init__(self, c, nc, fresh, name, gate_w, gate_b, xs_d, identf):
        sb = lambda n, s, d: c.enter_context(nc.sbuf_tensor(name + n, s, d))
        sem = lambda n: fresh(name + n)
        self.nc, self.gate_w, self.gate_b, self.xs_d, self.identf = nc, gate_w, gate_b, xs_d, identf
        self.gw = sb("gw", [P, E_], F32)
        self.gb = sb("gb", [P, E_], F32)
        self.xT = sb("xT", [P, 2, N], F32)
        self.lg = sb("lg", [P, 2, NT, E_], F32)
        self.top = sb("top", [P, 2, NT, E_], F32)
        self.ix = sb("ix", [P, 2, NT, E_], U32)
        self.ixf = sb("ixf", [P, 2, 2, NT], F32)
        self.iota = sb("iota", [P, E_], F32)
        self.iota_i = sb("iota_i", [P, E_], I32)
        self.hot = sb("hot", [P, 2, 2, NT, E_], F32)
        self.both = sb("both", [P, 2, NT, E_], BF16)
        self.pos = sb("pos", [P, 2, NT, E_], F32)
        self.pick = sb("pick", [P, 2, 2, NT, E_], F32)
        self.slot = sb("slot", [P, 2, 2, NT], F32)
        self.slot_i = sb("slot_i", [P, 2, 2, NT], I32)
        self.before = sb("before", [P, P], BF16)
        self.ones = sb("ones", [P, P], BF16)
        self.consts, self.gxT_ps, self.gxT_sb = sem("consts"), sem("gxT_ps"), sem("gxT_sb")
        self.lg_ps, self.chosen, self.rank_ps, self.slots = sem("lg_ps"), sem("chosen"), sem("rank_ps"), sem("slots")
        self.sent, self.gone, self.ticks = sem("sent"), sem("gone"), sem("ticks")
        self.PER = 2 + 8 + 7 + 1 + 6

    def load(self, sp, done):
        sp.dma_start(self.gw[:], self.gate_w).then_inc(done, 16)
        sp.dma_start(self.gb[:], bcast_rows(self.gate_b, P)).then_inc(done, 16)

    def pool_start(self, pool, base):
        nc = self.nc
        nc.gpsimd.memset(self.ones[:], 1.0).then_inc(self.consts, 1)
        nc.gpsimd.memset(self.before[:], 1.0).then_inc(self.consts, 1)
        nc.gpsimd.iota(self.iota_i[:], pattern=[[1, E_]], base=0, channel_multiplier=0).then_inc(self.consts, 1)
        pool.wait_ge(self.consts, 3)
        nc.gpsimd.affine_select(out=self.before[:], in_=self.before[:], compare_op=ALU.is_gt, fill=0.0,
                                base=0, pattern=[[1, P]], channel_multiplier=-1).then_inc(self.consts, 1)
        nc.gpsimd.tensor_copy(self.iota[:], self.iota_i[:]).then_inc(self.consts, 1)
        pool.wait_ge(self.consts, 5)
        nc.gpsimd.tensor_scalar(base[:], self.iota[:], float(CAP), None, ALU.mult).then_inc(self.consts, 1)
        pool.sem_inc(self.gone, 2)

    def pool_send(self, pool, h, i, b, rows):
        gate(pool, self.slots, b + 3, self.ticks)
        for k in range(2):
            for t in range(NT):
                self.nc.gpsimd.indirect_dma_start(
                    self.xs_d, bass.IndirectOffsetOnAxis(self.slot_i[:, h, k, t:t + 1], 0), rows[:, t], None).then_inc(self.sent, 16)
        gate(pool, self.sent, 16 * 2 * NT * (b + 1), self.ticks)
        pool.sem_inc(self.gone, 1)

    def pe_turn(self, pe, h, b, rows, ready, value, ps):
        pe.wait_ge(ready, value)
        for t in range(NT):
            mm = self.nc.tensor.transpose(ps[:, t * P:(t + 1) * P], rows[:, t], self.identf[:])
        mm.then_inc(self.gxT_ps, 1)

    def act_turn(self, act, h, b, ps):
        act.wait_ge(self.gxT_ps, b + 1)
        self.nc.scalar.copy(self.xT[:, h], ps[:]).then_inc(self.gxT_sb, 1)

    def pe_logits(self, pe, h, b, ps):
        pe.wait_ge(self.gxT_sb, b + 1)
        for t in range(NT):
            mm = self.nc.tensor.matmul(ps[:, t * E_:(t + 1) * E_], self.xT[:, h, t * P:(t + 1) * P], self.gw[:], start=True, stop=True)
        mm.then_inc(self.lg_ps, 1)

    def dve_choose(self, dve, own, h, b, ps, gaps_out):
        nc, lg, top = self.nc, self.lg[:, h], self.top[:, h]
        gate(dve, self.lg_ps, b + 1, self.ticks_dve)
        own.wait()
        own.done(nc.vector.tensor_tensor(lg, ps[:, 0:NT * E_].rearrange("p (t e) -> p t e", t=NT), wide(self.gb[:], [P, NT, E_]), ALU.add))
        gate(dve, *own.last, self.ticks_dve)
        for t in range(NT):
            own.done(nc.vector.max(top[:, t], lg[:, t]))
        gate(dve, *own.last, self.ticks_dve)
        for t in range(NT):
            own.done(nc.vector.max_index(self.ix[:, h, t], top[:, t], lg[:, t]))
        own.wait()
        own.done(nc.vector.tensor_copy(self.ixf[:, h], self.ix[:, h, :, 0:2].rearrange("p t k -> p k t")))
        own.wait()
        for k in range(2):
            own.done(nc.vector.tensor_tensor(self.hot[:, h, k], wide(self.iota[:], [P, NT, E_]),
                                             self.ixf[:, h, k].rearrange("p (t o) -> p t o", o=1).broadcast_to([P, NT, E_]), ALU.is_equal))
        own.wait()
        own.tell(nc.vector.tensor_tensor(self.both[:, h], self.hot[:, h, 0], self.hot[:, h, 1], ALU.add), self.chosen, b + 1)
        own.done(nc.vector.tensor_tensor(gaps_out, top, top[:, :, 0:1].broadcast_to([P, NT, E_]), ALU.subtract))

    def pe_rank(self, pe, h, b, ps):
        pe.wait_ge(self.chosen, b + 1)
        at = NT * E_
        for t in range(NT):
            for s in range(t + 1):
                self.nc.tensor.matmul(ps[:, at + t * E_:at + (t + 1) * E_], (self.before if s == t else self.ones)[:], self.both[:, h, s],
                                      start=(s == 0), stop=(s == t))
        for s in range(NT):
            mm = self.nc.tensor.matmul(ps[:, 2 * at:2 * at + E_], self.ones[:], self.both[:, h, s], start=(s == 0), stop=(s == NT - 1))
        mm.then_inc(self.rank_ps, 1)

    def dve_slots(self, dve, own, h, i, b, ps, base, keep):
        nc, at = self.nc, NT * E_
        gate(dve, self.rank_ps, b + 1, self.ticks_dve)
        own.wait()
        own.done(nc.vector.tensor_tensor(self.pos[:, h], ps[:, at:2 * at].rearrange("p (t e) -> p t e", t=NT), wide(base[:], [P, NT, E_]), ALU.add))
        own.wait()
        own.done(nc.vector.tensor_tensor(base[:], base[:], ps[:, 2 * at:2 * at + E_], ALU.add))
        for k in range(2):
            own.done(nc.vector.tensor_tensor(self.pick[:, h, k], self.hot[:, h, k], self.pos[:, h], ALU.mult))
        own.wait()
        own.done(nc.vector.tensor_reduce(self.slot[:, h], self.pick[:, h], AX.X, ALU.add))
        gate(dve, self.gone, b + 1, self.ticks_dve)
        own.wait()
        own.done(nc.vector.tensor_copy(keep, self.slot[:, h].rearrange("p k t -> p (k t)")))
        own.tell(nc.vector.tensor_copy(self.slot_i[:, h], self.slot[:, h]), self.slots, b + 3)


def after_attention(nc, x, xn_d, ctx_d, wo, bo, g1, c1, w1, b1, w2, b2, g2, c2, identf, route, x1_d, base, gaps, slots):
    with ExitStack() as c:
        sb = lambda n, s, d: c.enter_context(nc.sbuf_tensor("f_" + n, s, d))
        pb = lambda n, s, d: c.enter_context(nc.psum_tensor("f_" + n, s, d))
        fresh = Semaphores(c, nc)
        sem = lambda n: fresh("f_" + n)
        FC = 4
        ctx = sb("ctx", [P, 2, GROUPS, N], F32)
        xn = sb("xn", [P, 2, NT, D], F32)
        x0 = sb("x0", [P, 2, NT, D], F32)
        woT, w1T, w2T = sb("woT", [P, D], F32), sb("w1T", [P, FC * P], F32), sb("w2T", [P, FC, D], F32)
        b1c = sb("b1c", [P, FC], F32)
        rows = {n: sb(n, [P, D], F32) for n in ("bo", "g1", "c1", "b2", "g2", "c2")}
        eps = sb("eps", [P, 1], F32)
        rd = sb("rd", [P, 2, GROUPS, NT, GH], F32)
        cn = sb("cn", [P, 2, NT, D], F32)
        cT = sb("cT", [P, 2, N], F32)
        y = sb("y", [P, 2, NT, D], F32)
        yT = sb("yT", [P, 2, N], F32)
        hT = sb("hT", [P, 2, FC, N], F32)
        z = sb("z", [P, 2, NT, D], F32)
        x1 = sb("x1", [P, 2, NT, D], F32)
        xo = sb("xo", [P, 2, NT, D], F32)
        banks = [[pb(f"b{h}{n}", [P, N], F32) for n in range(4)] for h in range(2)]
        weights_in, consts = sem("weights_in"), sem("consts")
        ctx_in, xn_in, x_in = ([sem(n + "0"), sem(n + "1")] for n in ("ctx_in", "xn_in", "x_in"))
        ctxT_ps, cn_ready, cnT_ps, cT_sb, o_ps, y_ready = (sem(n) for n in ("ctxT_ps", "cn_ready", "cnT_ps", "cT_sb", "o_ps", "y_ready"))
        yT_ps, yT_sb, ff1_ps, hT_sb, ff2_ps, x1_ready, xo_ready = (sem(n) for n in ("yT_ps", "yT_sb", "ff1_ps", "hT_sb", "ff2_ps", "x1_ready", "xo_ready"))
        x1_out = [sem("x1_out0"), sem("x1_out1")]
        dve_own, dve_ticks, sp_ticks = sem("dve_own"), sem("dve_ticks"), sem("sp_ticks")
        n1, n2, n3 = (Norm(c, nc, fresh, f"f_n{k}") for k in range(3))
        r = Router(c, nc, fresh, "f_r", *route, identf)
        r.ticks_dve = dve_ticks
        halves = (0, 1)
        NW = 11

        with nc.Block() as block:
            @block.sync
            def _(sp):
                def load(b, h):
                    sp.dma_start(ctx[:, h], ctx_d[bass.ds(b * 2, 2) if not isinstance(b, int) else slice(2 * b, 2 * b + 2)].rearrange("g p n -> p g n")).then_inc(ctx_in[h], 16)
                    sp.dma_start(xn[:, h], xn_d[b].rearrange("(t p) d -> p t d", p=P)).then_inc(xn_in[h], 16)
                    sp.dma_start(x0[:, h], x[b].rearrange("(t p) d -> p t d", p=P)).then_inc(x_in[h], 16)

                def store(b, h):
                    gate(sp, x1_ready, b + 1, sp_ticks)
                    sp.dma_start(x1_d[b].rearrange("(t p) d -> p t d", p=P), x1[:, h]).then_inc(x1_out[h], 16)

                for t_, src in ((woT[:], wo), (w1T[:], w1), (w2T[:], w2)):
                    sp.dma_start(t_, src).then_inc(weights_in, 16)
                sp.dma_start(b1c[:], b1.rearrange("(a p) -> p a", p=P), allow_slow_non_contiguous=True).then_inc(weights_in, 16)
                for n, src in (("bo", bo), ("g1", g1), ("c1", c1), ("b2", b2), ("g2", g2), ("c2", c2)):
                    sp.dma_start(rows[n][:], bcast_rows(src, P)).then_inc(weights_in, 16)
                r.load(sp, weights_in)
                for h in halves:
                    load(h, h)
                with sp.Fori(0, PAIRS - 1) as i:
                    for h in halves:
                        store(2 * i + h, h)
                        load(2 * i + (h + 2), h)
                for h in halves:
                    store(B - 2 + h, h)
                for h in halves:
                    sp.wait_ge(x1_out[h], 16 * (PAIRS + 1))

            @block.gpsimd
            def _(pool):
                nc.gpsimd.memset(eps[:], EPS).then_inc(consts, 1)
                r.pool_start(pool, base)
                with pool.Fori(0, PAIRS) as i:
                    for h in halves:
                        r.pool_send(pool, h, i, 2 * i + h, xo[:, h])

            @block.scalar
            def _(act):
                act.wait_ge(consts, 1)
                act.wait_ge(weights_in, 16 * 12)
                for h in halves:
                    act.sem_inc(x1_out[h], 16)
                with act.Fori(0, PAIRS) as i:
                    for h in halves:
                        act.wait_ge(cnT_ps, 2 * i + (h + 1))
                        nc.scalar.copy(cT[:, h], banks[h][0][:]).then_inc(cT_sb, 1)
                    n1.root(act, i, eps)
                    for h in halves:
                        act.wait_ge(yT_ps, 2 * i + (h + 1))
                        nc.scalar.copy(yT[:, h], banks[h][0][:]).then_inc(yT_sb, 1)
                    for h in halves:
                        for f in range(FC):
                            act.wait_ge(ff1_ps, FC * (2 * i + h) + (f + 1))
                            nc.scalar.activation(hT[:, h, f], banks[h][2 + f % 2][:], ACT.Relu, bias=b1c[:, f:f + 1]).then_inc(hT_sb, 1)
                    n2.root(act, i, eps)
                    n3.root(act, i, eps)
                    for h in halves:
                        r.act_turn(act, h, 2 * i + h, banks[h][0])

            @block.vector
            def _(dve):
                PER = 140
                dve.wait_ge(r.consts, 6)
                dve.wait_ge(weights_in, 16 * 12)
                dve.sem_inc(dve_own, 1)
                dve.sem_inc(r.slots, 2)
                v = nc.vector
                with dve.Fori(0, PAIRS) as i:
                    own = Own(dve, dve_own, i, PER)
                    full = [P, NT, D]
                    for h in halves:
                        b = 2 * i + h
                        for g in range(GROUPS):
                            src = banks[h][g][:].rearrange("p (t h d) -> p t h d", t=NT, h=GH)
                            dve.wait_ge(ctxT_ps, 2 * b + (g + 1))
                            own.done(v.reciprocal(rd[:, h, g], src[:, :, :, HD]))
                            own.wait()
                            ins = v.tensor_tensor(cn[:, h, :, g * 64:(g + 1) * 64].rearrange("p t (h d) -> p t h d", h=GH), src[:, :, :, 0:HD],
                                                  rd[:, h, g].rearrange("p t (h o) -> p t h o", o=1).broadcast_to([P, NT, GH, HD]), ALU.mult)
                            own.done(ins) if g == 0 else own.tell(ins, cn_ready, b + 1)
                    for h in halves:
                        b = 2 * i + h
                        dve.wait_ge(xn_in[h], 16 * i + 16)
                        dve.wait_ge(o_ps, b + 1)
                        own.done(v.tensor_tensor(y[:, h], banks[h][1][:].rearrange("p (t d) -> p t d", t=NT), wide(rows["bo"][:], full), ALU.add))
                        own.wait()
                        own.done(v.tensor_tensor(y[:, h], y[:, h], xn[:, h], ALU.add))
                        n1.stats_of(own, y[:, h], h)
                    n1.variance(dve, own, i, dve_ticks)
                    n1.inverse(dve, own, i)
                    for h in halves:
                        b = 2 * i + h
                        n1.apply(own, y[:, h], y[:, h], h)
                        own.wait()
                        own.done(v.tensor_tensor(y[:, h], y[:, h], wide(rows["g1"][:], full), ALU.mult))
                        own.wait()
                        own.tell(v.tensor_tensor(y[:, h], y[:, h], wide(rows["c1"][:], full), ALU.add), y_ready, b + 1)
                    for h in halves:
                        b = 2 * i + h
                        dve.wait_ge(ff2_ps, b + 1)
                        own.done(v.tensor_tensor(z[:, h], banks[h][1][:].rearrange("p (t d) -> p t d", t=NT), wide(rows["b2"][:], full), ALU.add))
                        own.wait()
                        own.done(v.tensor_tensor(z[:, h], z[:, h], y[:, h], ALU.add))
                        n2.stats_of(own, z[:, h], h)
                    n2.variance(dve, own, i, dve_ticks)
                    n2.inverse(dve, own, i)
                    for h in halves:
                        b = 2 * i + h
                        n2.apply(own, z[:, h], z[:, h], h)
                        own.wait()
                        own.done(v.tensor_tensor(z[:, h], z[:, h], wide(rows["g2"][:], full), ALU.mult))
                        own.wait()
                        own.done(v.tensor_tensor(z[:, h], z[:, h], wide(rows["c2"][:], full), ALU.add))
                        dve.wait_ge(x_in[h], 16 * i + 16)
                        dve.wait_ge(x1_out[h], 16 * i + 16)
                        own.wait()
                        own.tell(v.tensor_tensor(x1[:, h], x0[:, h], z[:, h], ALU.add), x1_ready, b + 1)
                        n3.stats_of(own, x1[:, h], h)
                    n3.variance(dve, own, i, dve_ticks)
                    n3.inverse(dve, own, i)
                    for h in halves:
                        b = 2 * i + h
                        dve.wait_ge(r.gone, b + 1)
                        n3.apply(own, x1[:, h], xo[:, h], h, (xo_ready, b + 1))
                    for h in halves:
                        b = 2 * i + h
                        r.dve_choose(dve, own, h, b, banks[h][1], gaps[:, bass.ds(b * NT, NT), :])
                    for h in halves:
                        b = 2 * i + h
                        r.dve_slots(dve, own, h, i, b, banks[h][1], base, slots[:, bass.ds(b * (2 * NT), 2 * NT)])
                    own.end()

            @block.tensor
            def _(pe):
                pe.wait_ge(weights_in, 16 * 12)
                pe.wait_ge(r.consts, 6)
                with pe.Fori(0, PAIRS) as i:
                    for h in halves:
                        b = 2 * i + h
                        pe.wait_ge(ctx_in[h], 16 * i + 16)
                        pe.wait_ge(r.slots, b + 1)
                        for g in range(GROUPS):
                            for t in range(NT):
                                mm = nc.tensor.transpose(banks[h][g][:, t * P:(t + 1) * P], ctx[:, h, g, t * P:(t + 1) * P], identf[:])
                            mm.then_inc(ctxT_ps, 1)
                    for h in halves:
                        pe.wait_ge(cn_ready, 2 * i + (h + 1))
                        for t in range(NT):
                            mm = nc.tensor.transpose(banks[h][0][:, t * P:(t + 1) * P], cn[:, h, t], identf[:])
                        mm.then_inc(cnT_ps, 1)
                    for h in halves:
                        pe.wait_ge(cT_sb, 2 * i + (h + 1))
                        for t in range(NT):
                            mm = nc.tensor.matmul(banks[h][1][:, t * P:(t + 1) * P], cT[:, h, t * P:(t + 1) * P], woT[:], start=True, stop=True)
                        mm.then_inc(o_ps, 1)
                    for h in halves:
                        pe.wait_ge(y_ready, 2 * i + (h + 1))
                        for t in range(NT):
                            mm = nc.tensor.transpose(banks[h][0][:, t * P:(t + 1) * P], y[:, h, t], identf[:])
                        mm.then_inc(yT_ps, 1)
                    for h in halves:
                        b = 2 * i + h
                        pe.wait_ge(yT_sb, b + 1)
                        for f in range(FC):
                            if f >= 2:
                                pe.wait_ge(hT_sb, FC * b + (f - 1))
                            nc.tensor.matmul(banks[h][2 + f % 2][:], w1T[:, f * P:(f + 1) * P], yT[:, h], start=True, stop=True).then_inc(ff1_ps, 1)
                    for h in halves:
                        b = 2 * i + h
                        pe.wait_ge(hT_sb, FC * b + FC)
                        for t in range(NT):
                            for f in range(FC):
                                mm = nc.tensor.matmul(banks[h][1][:, t * P:(t + 1) * P], hT[:, h, f, t * P:(t + 1) * P], w2T[:, f], start=(f == 0), stop=(f == FC - 1))
                        mm.then_inc(ff2_ps, 1)
                    for h in halves:
                        r.pe_turn(pe, h, 2 * i + h, xo[:, h], xo_ready, 2 * i + (h + 1), banks[h][0])
                    for h in halves:
                        r.pe_logits(pe, h, 2 * i + h, banks[h][1])
                    for h in halves:
                        r.pe_rank(pe, h, 2 * i + h, banks[h][1])


def experts(nc, name, hc, func, base, xs_d, pack_d, y_d, slots, identf):
    H = hc * P
    W1, W2, B1, B2 = 0, H, 2 * H, 2 * H + hc
    WIDTH = 2 * H + hc + D
    PASTS = MOE_TILES * E_
    with ExitStack() as c:
        sb = lambda n, s, d: c.enter_context(nc.sbuf_tensor(name + n, s, d))
        pb = lambda n, s, d: c.enter_context(nc.psum_tensor(name + n, s, d))
        fresh = Semaphores(c, nc)
        sem = lambda n: fresh(name + n)
        two = lambda n: [sem(n + "0"), sem(n + "1")]
        K = B * N // TILE
        iota_e, iota_k, iota_j = sb("iota_e", [P, E_], I32), sb("iota_k", [P, K], I32), sb("iota_j", [P, MOE_TILES], I32)
        iota_l, spare, idle = sb("iota_l", [P, MOE_TILES], I32), sb("spare", [P, MOE_TILES], F32), sb("idle", [P, MOE_TILES], F32)
        caps, steps, js = sb("caps", [P, E_], F32), sb("steps", [P, K], F32), sb("js", [P, MOE_TILES], F32)
        ones = sb("ones", [P, E_], F32)
        count, need, upto = sb("count", [P, E_], F32), sb("need", [P, E_], F32), sb("upto", [P, E_], F32)
        over = sb("over", [P, E_, K], F32)
        past = sb("past", [P, 2, MOE_TILES, E_], F32)
        sums = sb("sums", [P, 2, MOE_TILES], F32)
        row = sb("row", [P, 2, MOE_TILES], F32)
        table = sb("table", [P, 2, MOE_TILES], I32)
        ends = sb("ends", [P, E_], I32)
        shift = sb("shift", [P, E_ - 1], F32)
        slot = sb("slot", [P, B * 2 * NT], F32)
        behind = sb("behind", [P, B * 2 * NT, E_ - 1], F32)
        moved = sb("moved", [P, B * 2 * NT], F32)
        zeros = sb("zeros", [P, TILE], F32)
        pack = sb("pack", [P, 2, WIDTH], F32)
        xs = sb("xs", [P, 2, NT, D], F32)
        xT = sb("xT", [P, 2, TILE], F32)
        hT = sb("hT", [P, 2, hc, TILE], F32)
        ys = sb("ys", [P, 2, NT, D], F32)
        ps_x = [pb(f"ps_x{h}", [P, TILE], F32) for h in range(2)]
        ps_h = [pb(f"ps_h{h}", [P, TILE], F32) for h in range(4)]
        ps_y = [pb(f"ps_y{h}", [P, TILE], F32) for h in range(2)]
        consts, dve_own, tables, zeroed = sem("consts"), sem("dve_own"), sem("tables"), sem("zeroed")
        x_in, w_in, y_out = two("x_in"), two("w_in"), two("y_out")
        xT_ps, xT_sb, h_ps, h_sb, y_ps, y_sb = (sem(n) for n in ("xT_ps", "xT_sb", "h_ps", "h_sb", "y_ps", "y_sb"))
        ticks, sp_ticks = sem("ticks"), sem("sp_ticks")
        tile_at = lambda d, at: d[bass.ds(at, TILE), :].rearrange("(p t) d -> p (t d)", p=P)
        flat = lambda a: a.rearrange("p t d -> p (t d)")

        with nc.Block() as block:
            @block.gpsimd
            def _(pool):
                g = nc.gpsimd
                g.iota(iota_e[:], pattern=[[CAP, E_]], base=0, channel_multiplier=0).then_inc(consts, 1)
                g.iota(iota_k[:], pattern=[[TILE, K]], base=0, channel_multiplier=0).then_inc(consts, 1)
                g.iota(iota_j[:], pattern=[[1, MOE_TILES]], base=0, channel_multiplier=0).then_inc(consts, 1)
                g.iota(iota_l[:], pattern=[[0, MOE_TILES // 2], [TILE, 2]], base=0, channel_multiplier=0).then_inc(consts, 1)
                g.memset(ones[:], 1.0).then_inc(consts, 1)
                g.memset(zeros[:], 0.0).then_inc(consts, 1)
                pool.wait_ge(consts, 6)
                pool.wait_ge(tables, 1)
                for e in range(E_ + 2):
                    at = E_ * CAP + (e - E_) * TILE if e >= E_ else g.value_load(ends[0:1, e:e + 1], min_val=0, max_val=E_ * CAP)
                    g.dma_start(tile_at(xs_d, at), zeros[:]).then_inc(zeroed, 16)
                pool.wait_ge(zeroed, 16 * (E_ + 2))

                def load(j, h):
                    e = g.value_load(table[0:1, 0, bass.ds(j, 1)], min_val=0, max_val=E_ - 1)
                    g.dma_start(pack[:, h], pack_d[e]).then_inc(w_in[h], 16)
                    at = g.value_load(table[0:1, 1, bass.ds(j, 1)], min_val=0, max_val=LAST)
                    g.dma_start(flat(xs[:, h]), tile_at(xs_d, at)).then_inc(x_in[h], 16)

                for h in range(2):
                    load(h, h)
                with pool.Fori(0, MOE_TILES // 2 - 1) as i:
                    for h in range(2):
                        gate(pool, y_sb, 2 * i + (h + 1), ticks)
                        load(2 * i + (h + 2), h)

            @block.sync
            def _(sp):
                for h in range(2):
                    sp.sem_inc(y_out[h], 16)
                with sp.Fori(0, MOE_TILES // 2) as i:
                    for h in range(2):
                        gate(sp, y_sb, 2 * i + (h + 1), sp_ticks)
                        sp.dma_start(tile_at(y_d, (2 * i + h) * TILE), flat(ys[:, h])).then_inc(y_out[h], 16)
                for h in range(2):
                    sp.wait_ge(y_out[h], 16 * (MOE_TILES // 2 + 1))

            @block.vector
            def _(dve):
                v = nc.vector
                dve.wait_ge(consts, 6)
                dve.sem_inc(dve_own, 1)
                own = Own(dve, dve_own, 0, 0)
                for dst, src in ((caps, iota_e), (steps, iota_k), (js, iota_j), (spare, iota_l)):
                    own.done(v.tensor_copy(dst[:], src[:]))
                own.done(v.tensor_copy(ends[:], base[:]))
                own.wait()
                own.done(v.tensor_tensor(count[:], base[:], caps[:], ALU.subtract))
                own.wait()
                own.done(v.tensor_tensor(over[:], count[:].rearrange("p (e o) -> p e o", o=1).broadcast_to([P, E_, K]), wide(steps[:], [P, E_, K]), ALU.is_gt))
                own.wait()
                own.done(v.tensor_reduce(need[:], over[:], AX.X, ALU.add))
                own.wait()
                own.done(v.tensor_tensor_scan(upto[:], ones[:], need[:], 0.0, ALU.mult, ALU.add))
                own.wait()
                each = [P, MOE_TILES, E_]
                own.done(v.tensor_tensor(past[:, 0], js[:].rearrange("p (j o) -> p j o", o=1).broadcast_to(each), wide(upto[:], each), ALU.is_ge))
                own.wait()
                own.done(v.tensor_tensor(past[:, 1], past[:, 0], wide(need[:], each), ALU.mult))
                own.wait()
                own.done(v.tensor_reduce(sums[:], past[:], AX.X, ALU.add))
                own.wait()
                own.done(v.tensor_tensor(row[:, 1], js[:], sums[:, 1], ALU.subtract))
                own.wait()
                own.done(v.tensor_scalar(row[:, 1], row[:, 1], float(TILE), None, ALU.mult))
                own.wait()
                own.done(v.scalar_tensor_tensor(out=row[:, 1], in0=sums[:, 0], scalar=float(CAP), in1=row[:, 1], op0=ALU.mult, op1=ALU.add))
                own.wait()
                own.done(v.tensor_scalar(idle[:], sums[:, 0], float(E_), float(ROWS), ALU.is_ge, ALU.mult))
                own.done(v.tensor_scalar(spare[:], spare[:], float(E_ * CAP), None, ALU.add))
                own.wait()
                own.done(v.tensor_tensor(row[:, 1], row[:, 1], idle[:], ALU.add))
                own.wait()
                own.done(v.tensor_tensor(row[:, 1], row[:, 1], spare[:], ALU.min))
                own.done(v.tensor_scalar(row[:, 0], sums[:, 0], float(E_ - 1), None, ALU.min))
                own.wait()
                own.tell(v.tensor_copy(table[:], row[:]), tables, 1)

                own.done(v.tensor_copy(slot[:], slots[:]))
                own.done(v.tensor_scalar(shift[:], need[:, 0:E_ - 1], float(TILE), float(-CAP), ALU.mult, ALU.add))
                own.wait()
                each = [P, B * 2 * NT, E_ - 1]
                own.done(v.tensor_tensor(behind[:], slot[:].rearrange("p (s o) -> p s o", o=1).broadcast_to(each), wide(caps[:, 1:E_], each), ALU.is_ge))
                own.wait()
                own.done(v.tensor_tensor(behind[:], behind[:], wide(shift[:], each), ALU.mult))
                own.wait()
                own.done(v.tensor_reduce(moved[:], behind[:], AX.X, ALU.add))
                own.wait()
                own.done(v.tensor_tensor(slots[:], slot[:], moved[:], ALU.add))

                def turned(j, h, i):
                    dve.wait_ge(xT_ps, j + 1)
                    v.tensor_copy(xT[:, h], ps_x[h][:]).then_inc(xT_sb, 1)

                def result(j, h, i):
                    dve.wait_ge(y_out[h], 16 * i + 16)
                    dve.wait_ge(y_ps, j + 1)
                    v.tensor_tensor(ys[:, h], ps_y[h][:].rearrange("p (t d) -> p t d", t=NT), wide(pack[:, h, B2:B2 + D], [P, NT, D]), ALU.add).then_inc(y_sb, 1)

                for h in range(2):
                    turned(h, h, 0)
                with dve.Fori(0, MOE_TILES // 2 - 1) as i:
                    for h in range(2):
                        result(2 * i + h, h, i)
                        turned(2 * i + (h + 2), h, i)
                for h in range(2):
                    result(MOE_TILES - 2 + h, h, MOE_TILES // 2 - 1)

            @block.scalar
            def _(act):
                act.sem_inc(h_sb, 4)
                with act.Fori(0, MOE_TILES // 2) as i:
                    for h in range(2):
                        for f in range(hc):
                            n = hc * h + f
                            act.wait_ge(h_ps, 2 * hc * i + (n + 1))
                            nc.scalar.activation(hT[:, h, f], ps_h[n % 4][:], func, bias=pack[:, h, B1 + f:B1 + f + 1]).then_inc(h_sb, 1)

            @block.tensor
            def _(pe):
                def turn(j, h, i):
                    pe.wait_ge(x_in[h], 16 * i + 16)
                    for t in range(NT):
                        mm = nc.tensor.transpose(ps_x[h][:, t * P:(t + 1) * P], xs[:, h, t], identf[:])
                    mm.then_inc(xT_ps, 1)

                def up(j, h, i):
                    pe.wait_ge(w_in[h], 16 * i + 16)
                    pe.wait_ge(xT_sb, j + 1)
                    for f in range(hc):
                        pe.wait_ge(h_sb, hc * j + (f + 1))
                        nc.tensor.matmul(ps_h[(hc * h + f) % 4][:], pack[:, h, W1 + f * P:W1 + (f + 1) * P], xT[:, h], start=True, stop=True).then_inc(h_ps, 1)

                def down(j, h):
                    pe.wait_ge(h_sb, hc * j + (hc + 4))
                    for t in range(NT):
                        for f in range(hc):
                            mm = nc.tensor.matmul(ps_y[h][:, t * P:(t + 1) * P], hT[:, h, f, t * P:(t + 1) * P], pack[:, h, W2 + f * D:W2 + (f + 1) * D],
                                                  start=(f == 0), stop=(f == hc - 1))
                    mm.then_inc(y_ps, 1)

                for h in range(2):
                    turn(h, h, 0)
                up(0, 0, 0)
                with pe.Fori(0, MOE_TILES // 2 - 1) as i:
                    up(2 * i + 1, 1, i)
                    down(2 * i, 0)
                    turn(2 * i + 2, 0, i + 1)
                    up(2 * i + 2, 0, i + 1)
                    down(2 * i + 1, 1)
                    turn(2 * i + 3, 1, i + 1)
                i = MOE_TILES // 2 - 1
                up(2 * i + 1, 1, i)
                down(2 * i, 0)
                down(2 * i + 1, 1)


class Gather:

    def __init__(self, c, nc, fresh, name, y_d, gaps, slots, among):
        sb = lambda n, s, d: c.enter_context(nc.sbuf_tensor(name + n, s, d))
        sem = lambda n: fresh(name + n)
        self.nc, self.y_d, self.gaps, self.slots, self.among = nc, y_d, gaps, slots, among
        self.e = sb("e", [P, B * NT, E_], F32)
        self.total = sb("total", [P, B * NT], F32)
        self.inv = sb("inv", [P, B * NT], F32)
        self.w = sb("w", [P, B * NT, 2], F32)
        self.wh = sb("wh", [P, 2, NT, 2], F32)
        self.ix = sb("ix", [P, 2, 2 * NT], I32)
        self.y = sb("y", [P, 2, 2, NT, D], F32)
        self.ix_ready, self.exps, self.ticks = sem("ix_ready"), sem("exps"), sem("ticks")
        self.came = [sem("came0"), sem("came1")]
        self.ix_own = sem("ix_own")
        self.taken = sem("taken")

    def act_start(self, act):
        self.nc.scalar.activation(self.e[:], self.gaps[:], ACT.Exp).then_inc(self.exps, 1)

    def dve_start(self, dve, own):
        v, full = self.nc.vector, [P, B * NT, 2]
        dve.sem_inc(self.taken, 2)
        dve.wait_ge(self.exps, 1)
        own.done(v.tensor_reduce(self.total[:], self.e[:, :, 0:self.among], AX.X, ALU.add))
        own.wait()
        own.done(v.reciprocal(self.inv[:], self.total[:]))
        own.wait()
        own.done(v.tensor_tensor(self.w[:], self.e[:, :, 0:2], self.inv[:].rearrange("p (t o) -> p t o", o=1).broadcast_to(full), ALU.mult))
        own.wait()

    def pool_bring(self, pool, h, b):
        g = self.nc.gpsimd
        gate(pool, self.taken, b + 1, self.ticks)
        g.tensor_copy(self.ix[:, h], self.slots[:, bass.ds(b * (2 * NT), 2 * NT)]).then_inc(self.ix_ready, 1)
        gate(pool, self.ix_ready, b + 1, self.ticks)
        for k in range(2):
            for t in range(NT):
                g.indirect_dma_start(self.y[:, h, k, t], None, self.y_d, bass.IndirectOffsetOnAxis(self.ix[:, h, k * NT + t:k * NT + t + 1], 0)).then_inc(self.came[h], 16)

    def dve_add(self, dve, own, h, i, b, x):
        v = self.nc.vector
        own.wait()
        own.done(v.tensor_copy(self.wh[:, h], self.w[:, bass.ds(b * NT, NT), :]))
        gate(dve, self.came[h], 16 * 2 * NT * (i + 1), self.ticks_dve)
        for k in range(2):
            own.wait()
            for t in range(NT):
                ins = v.scalar_tensor_tensor(out=x[:, t], in0=self.y[:, h, k, t], scalar=self.wh[:, h, t, k:k + 1], in1=x[:, t], op0=ALU.mult, op1=ALU.add)
                own.tell(ins, self.taken, b + 3) if (k, t) == (1, NT - 1) else own.done(ins)


R_ = 4
PARTS = 3


def relations(nc, x1_d, adjT_d, y_d, weight, bias, identf, route, x2_d, base, gaps, slots):
    with ExitStack() as c:
        sb = lambda n, s, d: c.enter_context(nc.sbuf_tensor("g_" + n, s, d))
        pb = lambda n, s, d: c.enter_context(nc.psum_tensor("g_" + n, s, d))
        fresh = Semaphores(c, nc)
        sem = lambda n: fresh("g_" + n)
        x1 = sb("x1", [P, 2, NT, D], F32)
        xn = sb("xn", [P, 2, NT, D], F32)
        xo = sb("xo", [P, 2, NT, D], F32)
        aT = sb("aT", [P, 2, NT, N], BF16)
        mask = sb("mask", [P, 2, R_, NT, N], BF16)
        wr = sb("wr", [P, R_ * D], F32)
        bc = sb("bc", [P, 1], F32)
        eps = sb("eps", [P, 1], F32)
        xT = sb("xT", [P, 2, N], F32)
        part = sb("part", [P, 2, PARTS, NT, R_ * D], BF16)
        rest = sb("rest", [P, 2, NT, R_ * D], F32)
        oT = sb("oT", [P, 2, N], F32)
        banks = [[pb(f"b{h}{n}", [P, N], F32) for n in range(4)] for h in range(2)]
        weights_in, consts = sem("weights_in"), sem("consts")
        x_in, a_in, x2_out = ([sem(n + "0"), sem(n + "1")] for n in ("x_in", "a_in", "x2_out"))
        xn_ready, xT_ps, xT_sb, xw_ps, high_sb, rest_sb, mid_sb, parts_sb = (
            sem(n) for n in ("xn_ready", "xT_ps", "xT_sb", "xw_ps", "high_sb", "rest_sb", "mid_sb", "parts_sb"))
        masks, oT_ps, oT_sb, o_ps, x2_ready, xo_ready = (sem(n) for n in ("masks", "oT_ps", "oT_sb", "o_ps", "x2_ready", "xo_ready"))
        dve_own, dve_ticks, sp_ticks = sem("dve_own"), sem("dve_ticks"), sem("sp_ticks")
        n1, n2 = (Norm(c, nc, fresh, f"g_n{k}") for k in range(2))
        new_gaps, new_slots = gaps[1], slots[1]
        r = Router(c, nc, fresh, "g_r", *route, identf)
        q = Gather(c, nc, fresh, "g_q", y_d, gaps[0], slots[0], E_)
        r.ticks_dve = q.ticks_dve = dve_ticks
        halves = (0, 1)

        with nc.Block() as block:
            @block.sync
            def _(sp):
                def load(b, h):
                    sp.dma_start(x1[:, h], x1_d[b].rearrange("(t p) d -> p t d", p=P)).then_inc(x_in[h], 16)
                    sp.dma_start(aT[:, h], adjT_d[b]).then_inc(a_in[h], 16)

                def store(b, h):
                    gate(sp, x2_ready, b + 1, sp_ticks)
                    sp.dma_start(x2_d[b].rearrange("(t p) d -> p t d", p=P), x1[:, h]).then_inc(x2_out[h], 16)

                sp.dma_start(wr[:].rearrange("p (r o) -> p r o", r=R_), weight.rearrange("r d o -> d r o")).then_inc(weights_in, 16)
                sp.dma_start(bc[:], bias.rearrange("(p a) -> p a", a=1), allow_slow_non_contiguous=True).then_inc(weights_in, 16)
                r.load(sp, weights_in)
                for h in halves:
                    load(h, h)
                with sp.Fori(0, PAIRS - 1) as i:
                    for h in halves:
                        store(2 * i + h, h)
                        gate(sp, x2_out[h], 16 * i + 16, sp_ticks)
                        gate(sp, xo_ready, 2 * i + (h + 1), sp_ticks)
                        load(2 * i + (h + 2), h)
                for h in halves:
                    store(B - 2 + h, h)
                for h in halves:
                    sp.wait_ge(x2_out[h], 16 * PAIRS)

            @block.gpsimd
            def _(pool):
                nc.gpsimd.memset(eps[:], EPS).then_inc(consts, 1)
                r.pool_start(pool, base)
                for h in halves:
                    q.pool_bring(pool, h, h)
                with pool.Fori(0, PAIRS - 1) as i:
                    for h in halves:
                        q.pool_bring(pool, h, 2 * i + (h + 2))
                    for h in halves:
                        r.pool_send(pool, h, i, 2 * i + h, xo[:, h])
                for h in halves:
                    r.pool_send(pool, h, PAIRS - 1, B - 2 + h, xo[:, h])

            @block.scalar
            def _(act):
                q.act_start(act)
                act.wait_ge(consts, 1)
                act.wait_ge(weights_in, 16 * 4)
                with act.Fori(0, PAIRS) as i:
                    n1.root(act, i, eps)
                    for h in halves:
                        act.wait_ge(xT_ps, 2 * i + (h + 1))
                        nc.scalar.copy(xT[:, h], banks[h][0][:]).then_inc(xT_sb, 1)
                    for h in halves:
                        for t in range(NT):
                            act.wait_ge(xw_ps, NT * (2 * i + h) + (t + 1))
                            nc.scalar.copy(part[:, h, 0, t], banks[h][2 + t % 2][:]).then_inc(high_sb, 1)
                            act.wait_ge(rest_sb, NT * (2 * i + h) + (t + 3))
                            nc.scalar.copy(part[:, h, 1, t], rest[:, h, t]).then_inc(mid_sb, 1)
                    for h in halves:
                        act.wait_ge(oT_ps, 2 * i + (h + 1))
                        nc.scalar.activation(oT[:, h], banks[h][1][:], ACT.Identity, bias=bc[:], scale=1.0).then_inc(oT_sb, 1)
                    n2.root(act, i, eps)
                    for h in halves:
                        r.act_turn(act, h, 2 * i + h, banks[h][0])

            @block.vector
            def _(dve):
                PER = 112
                v = nc.vector
                dve.wait_ge(r.consts, 6)
                dve.wait_ge(weights_in, 16 * 4)
                dve.sem_inc(dve_own, 1)
                dve.sem_inc(r.slots, 2)
                dve.sem_inc(rest_sb, 2)
                first = Own(dve, q.ix_own, 0, 3)
                dve.sem_inc(q.ix_own, 1)
                q.dve_start(dve, first)
                with dve.Fori(0, PAIRS) as i:
                    own = Own(dve, dve_own, i, PER)
                    for h in halves:
                        b = 2 * i + h
                        gate(dve, x_in[h], 16 * i + 16, dve_ticks)
                        q.dve_add(dve, own, h, i, b, x1[:, h])
                        n1.stats_of(own, x1[:, h], h)
                    n1.variance(dve, own, i, dve_ticks)
                    n1.inverse(dve, own, i)
                    for h in halves:
                        n1.apply(own, x1[:, h], xn[:, h], h, (xn_ready, 2 * i + (h + 1)))
                    for h in halves:
                        gate(dve, a_in[h], 16 * i + 16, dve_ticks)
                        for k in range(R_):
                            ins = v.tensor_scalar(mask[:, h, k], aT[:, h], float(k + 1), None, ALU.is_equal)
                            own.tell(ins, masks, 2 * i + (h + 1)) if k == R_ - 1 else own.done(ins)
                    for h in halves:
                        for t in range(NT):
                            n = NT * (2 * i + h) + t
                            dve.wait_ge(high_sb, n + 1)
                            own.tell(v.tensor_tensor(rest[:, h, t], banks[h][2 + t % 2][:], part[:, h, 0, t], ALU.subtract), rest_sb, n + 3)
                            dve.wait_ge(mid_sb, n + 1)
                            own.tell(v.tensor_tensor(part[:, h, 2, t], rest[:, h, t], part[:, h, 1, t], ALU.subtract), parts_sb, n + 1)
                    for h in halves:
                        b = 2 * i + h
                        dve.wait_ge(o_ps, b + 1)
                        own.tell(v.tensor_tensor(x1[:, h], x1[:, h], banks[h][0][:].rearrange("p (t d) -> p t d", t=NT), ALU.add), x2_ready, b + 1)
                        n2.stats_of(own, x1[:, h], h)
                    n2.variance(dve, own, i, dve_ticks)
                    n2.inverse(dve, own, i)
                    for h in halves:
                        b = 2 * i + h
                        dve.wait_ge(r.gone, b + 1)
                        n2.apply(own, x1[:, h], xo[:, h], h, (xo_ready, b + 1))
                    for h in halves:
                        b = 2 * i + h
                        r.dve_choose(dve, own, h, b, banks[h][1], new_gaps[:, bass.ds(b * NT, NT), :])
                    for h in halves:
                        b = 2 * i + h
                        r.dve_slots(dve, own, h, i, b, banks[h][1], base, new_slots[:, bass.ds(b * (2 * NT), 2 * NT)])
                    own.end()

            @block.tensor
            def _(pe):
                pe.wait_ge(weights_in, 16 * 4)
                pe.wait_ge(r.consts, 6)
                with pe.Fori(0, PAIRS) as i:
                    for h in halves:
                        b = 2 * i + h
                        pe.wait_ge(xn_ready, b + 1)
                        for t in range(NT):
                            mm = nc.tensor.transpose(banks[h][0][:, t * P:(t + 1) * P], xn[:, h, t], identf[:])
                        mm.then_inc(xT_ps, 1)
                    for h in halves:
                        b = 2 * i + h
                        pe.wait_ge(xT_sb, b + 1)
                        for t in range(NT):
                            pe.wait_ge(rest_sb, NT * b + (t + 1))
                            nc.tensor.matmul(banks[h][2 + t % 2][:], xT[:, h, t * P:(t + 1) * P], wr[:], start=True, stop=True).then_inc(xw_ps, 1)
                    for h in halves:
                        b = 2 * i + h
                        pe.wait_ge(masks, b + 1)
                        pe.wait_ge(r.slots, b + 1)
                        for t in range(NT):
                            pe.wait_ge(parts_sb, NT * b + (t + 1))
                            for k in range(R_):
                                for s in range(PARTS):
                                    mm = nc.tensor.matmul(banks[h][1][:], part[:, h, s, t, k * D:(k + 1) * D], mask[:, h, k, t],
                                                          start=(t, k, s) == (0, 0, 0), stop=(t, k, s) == (NT - 1, R_ - 1, PARTS - 1))
                        mm.then_inc(oT_ps, 1)
                    for h in halves:
                        b = 2 * i + h
                        pe.wait_ge(oT_sb, b + 1)
                        for t in range(NT):
                            mm = nc.tensor.transpose(banks[h][0][:, t * P:(t + 1) * P], oT[:, h, t * P:(t + 1) * P], identf[:])
                        mm.then_inc(o_ps, 1)
                    for h in halves:
                        r.pe_turn(pe, h, 2 * i + h, xo[:, h], xo_ready, 2 * i + (h + 1), banks[h][0])
                    for h in halves:
                        r.pe_logits(pe, h, 2 * i + h, banks[h][1])
                    for h in halves:
                        r.pe_rank(pe, h, 2 * i + h, banks[h][1])


def finish(nc, x2_d, y_d, gaps, slots, out):
    with ExitStack() as c:
        fresh = Semaphores(c, nc)
        sem = lambda n: fresh("z_" + n)
        x2 = c.enter_context(nc.sbuf_tensor("z_x2", [P, 2, NT, D], F32))
        x_in, out_done = ([sem(n + "0"), sem(n + "1")] for n in ("x_in", "out_done"))
        dve_own, dve_ticks, sp_ticks = sem("dve_own"), sem("dve_ticks"), sem("sp_ticks")
        q = Gather(c, nc, fresh, "z_q", y_d, gaps, slots, 2)
        q.ticks_dve = dve_ticks
        halves = (0, 1)

        with nc.Block() as block:
            @block.sync
            def _(sp):
                def load(b, h):
                    sp.dma_start(x2[:, h], x2_d[b].rearrange("(t p) d -> p t d", p=P)).then_inc(x_in[h], 16)

                def store(b, h, nth):
                    gate(sp, q.taken, b + 3, sp_ticks)
                    sp.dma_start(out[b].rearrange("(t p) d -> p t d", p=P), x2[:, h]).then_inc(out_done[h], 16)
                    gate(sp, out_done[h], nth, sp_ticks)

                for h in halves:
                    load(h, h)
                with sp.Fori(0, PAIRS - 1) as i:
                    for h in halves:
                        store(2 * i + h, h, 16 * i + 16)
                        load(2 * i + (h + 2), h)
                for h in halves:
                    store(B - 2 + h, h, 16 * PAIRS)

            @block.gpsimd
            def _(pool):
                with pool.Fori(0, PAIRS) as i:
                    for h in halves:
                        q.pool_bring(pool, h, 2 * i + h)

            @block.scalar
            def _(act):
                q.act_start(act)

            @block.vector
            def _(dve):
                dve.sem_inc(q.ix_own, 1)
                q.dve_start(dve, Own(dve, q.ix_own, 0, 3))
                dve.sem_inc(dve_own, 1)
                with dve.Fori(0, PAIRS) as i:
                    own = Own(dve, dve_own, i, 2 * 2 * NT)
                    for h in halves:
                        gate(dve, x_in[h], 16 * i + 16, dve_ticks)
                        q.dve_add(dve, own, h, i, 2 * i + h, x2[:, h])
                    own.end()


def build(nc, x, adj, wqkv, bqkv, wo, bo, g1, c1, w1, b1, w2, b2, g2, c2, gate0_w, gate0_b, pack0,
          rel_w, rel_b, gate1_w, gate1_b, pack1, out):
    dram = lambda n, s, d=F32: nc.dram_tensor(n, s, d, kind="Internal").ap()
    xn_d, x1_d, x2_d = (dram(n, (B, N, D)) for n in ("xn_d", "x1_d", "x2_d"))
    qk_d = dram("qk_d", (B, P, 2, 2, N))
    v_d = dram("v_d", (B, P, NT, HEADS, 32))
    adjT_d, neg_d = dram("adjT_d", (B, P, NT, N), BF16), dram("neg_d", (B, P, NT, N), BF16)
    ctx_d = dram("ctx_d", (UNITS, P, N))
    xs_d = [dram(f"xs{k}_d", (ROWS, D)) for k in range(2)]
    y_d = [dram(f"y{k}_d", (MOE_TILES * TILE, D)) for k in range(2)]
    with ExitStack() as c:
        sb = lambda n, s, d: c.enter_context(nc.sbuf_tensor(n, s, d))
        identf, identb = sb("identf", [P, P], F32), sb("identb", [P, P], BF16)
        base = [sb(f"base{k}", [P, E_], F32) for k in range(2)]
        gaps = [sb(f"gaps{k}", [P, B * NT, E_], F32) for k in range(2)]
        slots = [sb(f"slots{k}", [P, B * 2 * NT], I32) for k in range(2)]
        made = c.enter_context(nc.semaphore("made"))
        with nc.Block() as block:
            @block.gpsimd
            def _(pool):
                nc.gpsimd.memset(identf[:], 0.0).then_inc(made, 1)
                nc.gpsimd.memset(identb[:], 0.0).then_inc(made, 1)
                pool.wait_ge(made, 2)
                for m in (identf, identb):
                    nc.gpsimd.affine_select(out=m[:], in_=m[:], compare_op=ALU.not_equal, fill=1.0,
                                            base=0, pattern=[[-1, P]], channel_multiplier=1).then_inc(made, 1)
                pool.wait_ge(made, 4)
        prepare(nc, x, adj, wqkv, bqkv, identf, identb, xn_d, qk_d, v_d, adjT_d, neg_d)
        attend(nc, identf, identb, qk_d, v_d, neg_d, ctx_d)
        after_attention(nc, x, xn_d, ctx_d, wo, bo, g1, c1, w1, b1, w2, b2, g2, c2, identf,
                        (gate0_w, gate0_b, xs_d[0]), x1_d, base[0], gaps[0], slots[0])
        experts(nc, "e0_", 2, ACT.Gelu, base[0], xs_d[0], pack0, y_d[0], slots[0], identf)
        relations(nc, x1_d, adjT_d, y_d[0], rel_w, rel_b, identf, (gate1_w, gate1_b, xs_d[1]), x2_d, base[1], gaps, slots)
        experts(nc, "e1_", 4, ACT.Relu, base[1], xs_d[1], pack1, y_d[1], slots[1], identf)
        finish(nc, x2_d, y_d[1], gaps[1], slots[1], out)


def kernel(**inputs):
    import numpy as np
    import concourse.bacc as bacc
    from concourse.bass_utils import run_bass_kernel_spmd

    a = {k: np.asarray(v) for k, v in inputs.items()}

    def pack(w1, b1, w2, b2):
        e, d, h = w1.shape
        c = h // P
        return np.concatenate([w1, w2.reshape(e, c, P, d).transpose(0, 2, 1, 3).reshape(e, P, h),
                               b1.reshape(e, c, P).transpose(0, 2, 1), np.broadcast_to(b2[:, None, :], (e, P, d))], axis=-1)

    arrays = {
        "x": a["x"], "adj": a["adj"],
        "wqkv": a["L0_gnn_Wqkv"].T, "bqkv": a["L0_gnn_bqkv"], "wo": a["L0_gnn_Wo"].T, "bo": a["L0_gnn_bo"],
        "g1": a["L0_gnn_ln1_g"], "c1": a["L0_gnn_ln1_b"], "w1": a["L0_gnn_W1"].T, "b1": a["L0_gnn_b1"],
        "w2": a["L0_gnn_W2"].T.reshape(4, P, D).transpose(1, 0, 2), "b2": a["L0_gnn_b2"],
        "g2": a["L0_gnn_ln2_g"], "c2": a["L0_gnn_ln2_b"],
        "gate0_w": a["L0_ffn_gate_w"], "gate0_b": a["L0_ffn_gate_b"],
        "pack0": pack(a["L0_ffn_W1"], a["L0_ffn_b1"], a["L0_ffn_W2"], a["L0_ffn_b2"]),
        "rel_w": a["L1_gnn_weight"], "rel_b": a["L1_gnn_bias"],
        "gate1_w": a["L1_ffn_Wg"].T, "gate1_b": a["L1_ffn_bg"],
        "pack1": pack(a["L1_ffn_W1"].transpose(0, 2, 1), a["L1_ffn_b1"], a["L1_ffn_W2"].transpose(0, 2, 1), a["L1_ffn_b2"]),
    }
    nc = bacc.Bacc("TRN2", target_bir_lowering=False, num_devices=1)
    given, args = {}, []
    for name, v in arrays.items():
        given[name] = np.ascontiguousarray(v)
        args.append(nc.dram_tensor(name, v.shape, mybir.dt.from_np(v.dtype), kind="ExternalInput").ap())
    out = nc.dram_tensor("out", (B, N, D), F32, kind="ExternalOutput").ap()
    build(nc, *args, out)
    result = run_bass_kernel_spmd(nc, [given], core_ids=[0])
    return result.results[0]["out"]
```

```python
from contextlib import ExitStack

import concourse.bass as bass
from concourse import mybir

F32 = mybir.dt.float32
F32R = mybir.dt.float32r
BF16 = mybir.dt.bfloat16
I32 = mybir.dt.int32
U32 = mybir.dt.uint32
ALU = mybir.AluOpType
ACT = mybir.ActivationFunctionType
AX = mybir.AxisListType

P = 128
B, N, D = 16, 512, 128
NT = N // P
HEADS, HD = 8, 16
GROUPS, GH = 2, 4
NEG = -1.0e30
EPS = 1e-5
PAIRS = B // 2


class Semaphores:

    def __init__(self, c, nc):
        self.nc, self.all = nc, []
        c.callback(self.clear)

    def clear(self):
        self.nc.clear_and_free_semaphores(self.all)
        self.nc.all_engine_barrier()

    def __call__(self, name):
        self.all.append(self.nc.alloc_semaphore(name))
        return self.all[-1]


class Own:

    def __init__(self, eng, sem, turn, per):
        self.eng, self.sem, self.per, self.k = eng, sem, per, 0
        self.base = turn * per
        self.last = (sem, self.base + 1)

    def wait(self):
        self.eng.wait_ge(*self.last)

    def done(self, ins):
        self.k += 1
        self.last = (self.sem, self.base + (self.k + 1))
        ins.then_inc(self.sem, 1)

    def tell(self, ins, sem, value):
        self.last = (sem, value)
        ins.then_inc(sem, 1)

    def end(self):
        assert self.k == self.per, (self.k, self.per)


def bcast_rows(ap, n):
    return ap.partition_broadcast(n)


def gate(eng, sem, value, ticks):
    eng.wait_ge(sem, value)
    eng.sem_inc(ticks, 1)


class Norm:
    PER = 2 * NT + 2 * NT + 5 + 2 * NT

    def __init__(self, c, nc, fresh, name):
        sb = lambda n, s, d: c.enter_context(nc.sbuf_tensor(name + n, s, d))
        sem = lambda n: fresh(name + n)
        self.nc = nc
        self.stats = sb("stats", [P, 2, NT, 6], F32)
        self.mv = sb("mv", [P, 2, NT, 2], F32)
        self.std = sb("std", [P, 2, NT], F32)
        self.r = sb("r", [P, 2, NT], F32)
        self.s = sb("s", [P, 2, NT], F32)
        self.var_ready, self.std_ready = sem("var_ready"), sem("std_ready")

    def stats_of(self, own, src, h):
        own.wait()
        for t in range(NT):
            own.done(self.nc.vector.bn_stats(self.stats[:, h, t], src[:, t]))

    def variance(self, dve, own, nth, ticks):
        gate(dve, *own.last, ticks)
        for h in range(2):
            for t in range(NT):
                ins = self.nc.vector.bn_aggr(self.mv[:, h, t], self.stats[:, h, t])
                own.done(ins) if (h, t) != (1, NT - 1) else own.tell(ins, self.var_ready, nth + 1)

    def root(self, act, nth, eps):
        act.wait_ge(self.var_ready, nth + 1)
        self.nc.scalar.activation(self.std[:], self.mv[:, :, :, 1], ACT.Sqrt, bias=eps[:], scale=1.0).then_inc(self.std_ready, 1)

    def inverse(self, dve, own, nth):
        v, r, s = self.nc.vector, self.r, self.s
        dve.wait_ge(self.std_ready, nth + 1)
        own.done(v.reciprocal(r[:], self.std[:]))
        own.wait()
        own.done(v.tensor_tensor(s[:], r[:], r[:], ALU.mult))
        own.wait()
        own.done(v.scalar_tensor_tensor(out=s[:], in0=self.mv[:, :, :, 1], scalar=EPS, in1=s[:], op0=ALU.add, op1=ALU.mult))
        own.wait()
        own.done(v.tensor_scalar(s[:], s[:], -0.5, 1.5, ALU.mult, ALU.add))
        own.wait()
        own.done(v.tensor_tensor(r[:], r[:], s[:], ALU.mult))

    def apply(self, own, src, dst, h, last=None):
        own.wait()
        for t in range(NT):
            ins = self.nc.vector.tensor_scalar(dst[:, t], src[:, t], self.mv[:, h, t, 0:1], self.r[:, h, t:t + 1], ALU.subtract, ALU.mult)
            own.tell(ins, *last) if last and t == NT - 1 else own.done(ins)


def prepare(nc, x, adj, wqkv, bqkv, ident, identb, xn_d, qk_d, v_d, adjT_d, neg_d):
    with ExitStack() as c:
        sb = lambda n, s, d: c.enter_context(nc.sbuf_tensor("p_" + n, s, d))
        pb = lambda n, s, d: c.enter_context(nc.psum_tensor("p_" + n, s, d))
        fresh = Semaphores(c, nc)
        sem = lambda n: fresh("p_" + n)
        two = lambda n: [sem(n + "0"), sem(n + "1")]
        adj_i = sb("adj_i", [P, 2, NT, N], I32)
        adj_b = sb("adj_b", [P, 2, NT, N], BF16)
        adjT = sb("adjT", [P, 2, NT, N], BF16)
        neg = sb("neg", [P, 2, NT, N], BF16)
        wT = sb("wT", [P, 3 * D], F32)
        bqk = sb("bqk", [P, 2], F32)
        bqk_s = sb("bqk_s", [P, 2], F32)
        bv = sb("bv", [P, D], F32)
        eps = sb("eps", [P, 1], F32)
        closed = sb("closed", [P, NT, N], BF16)
        xn = sb("xn", [P, 2, NT, D], F32)
        xT = sb("xT", [P, 2, N], F32)
        qk = sb("qk", [P, 2, 2, N], F32)
        parts = sb("parts", [P, 2, 2, 2, N], F32R)
        va = sb("va", [P, 2, NT, HEADS, 32], F32)
        ps_x = pb("ps_x", [P, N], F32)
        ps_q = pb("ps_q", [P, N], F32)
        ps_k = pb("ps_k", [P, N], F32)
        ps_v = pb("ps_v", [P, N], F32)
        ps_a = [pb(f"ps_a{j}", [P, 1024], BF16) for j in range(NT)]

        weights_in = sem("weights_in")
        adj_in, x_in = two("adj_in"), two("x_in")
        adj_cast, adjT_ps, adjT_sb = sem("adj_cast"), sem("adjT_ps"), sem("adjT_sb")
        xn_ready = sem("xn")
        norm = Norm(c, nc, fresh, "p_n")
        sp_ticks, pool_ticks, dve_ticks = sem("sp_ticks"), sem("pool_ticks"), sem("dve_ticks")
        xT_ps, xT_sb, qk_ps, qk_sb, v_ps, v_sb = (sem(n) for n in ("xT_ps", "xT_sb", "qk_ps", "qk_sb", "v_ps", "v_sb"))
        parts_ready, neg_ready, consts = sem("parts"), sem("neg_ready"), sem("consts")
        parts_out, v_out, adjT_out, neg_out = two("parts_out"), two("v_out"), two("adjT_out"), two("neg_out")
        xn_out = two("xn_out")
        dve_own = sem("dve_own")

        with nc.Block() as block:
            @block.sync
            def _(sp):
                def load(b, h):
                    sp.dma_start(adj_i[:, h], adj[b].rearrange("(t p) m -> p t m", p=P)).then_inc(adj_in[h], 16)
                    sp.dma_start(xn[:, h], x[b].rearrange("(t p) d -> p t d", p=P)).then_inc(x_in[h], 16)

                def store(b, h):
                    gate(sp, xn_ready, b + 1, sp_ticks)
                    sp.dma_start(xn_d[b].rearrange("(t p) d -> p t d", p=P), xn[:, h]).then_inc(xn_out[h], 16)
                    gate(sp, v_sb, b + 2, sp_ticks)
                    sp.dma_start(v_d[b], va[:, h]).then_inc(v_out[h], 16)
                    gate(sp, parts_ready, b + 1, sp_ticks)
                    sp.dma_start(qk_d[b], parts[:, h].bitcast(F32)).then_inc(parts_out[h], 16)
                    gate(sp, adjT_sb, NT * (b + 2), sp_ticks)
                    sp.dma_start(adjT_d[b], adjT[:, h]).then_inc(adjT_out[h], 16)
                    gate(sp, neg_ready, b + 3, sp_ticks)
                    sp.dma_start(neg_d[b], neg[:, h]).then_inc(neg_out[h], 16)

                sp.dma_start(wT[:], wqkv).then_inc(weights_in, 16)
                sp.dma_start(bqk[:], bqkv[0:2 * D].rearrange("(a p) -> p a", p=P), allow_slow_non_contiguous=True).then_inc(weights_in, 16)
                sp.dma_start(bv[:], bcast_rows(bqkv[2 * D:3 * D], P)).then_inc(weights_in, 16)
                for h in range(2):
                    load(h, h)
                with sp.Fori(0, PAIRS - 1) as i:
                    for h in range(2):
                        store(i * 2 + h, h)
                        gate(sp, adj_cast, i * 2 + (h + 1), sp_ticks)
                        gate(sp, xn_out[h], i * 16 + 16, sp_ticks)
                        load(i * 2 + (h + 2), h)
                for h in range(2):
                    store(B - 2 + h, h)
                for h in range(2):
                    sp.wait_ge(xn_out[h], 16 * PAIRS)
                    for s in (parts_out, v_out, adjT_out, neg_out):
                        sp.wait_ge(s[h], 16 * (PAIRS + 1))

            @block.gpsimd
            def _(pool):
                nc.gpsimd.memset(eps[:], EPS).then_inc(consts, 1)
                nc.gpsimd.memset(va[:], 0.0).then_inc(consts, 1)
                pool.wait_ge(consts, 2)
                nc.gpsimd.memset(va[:, :, :, :, HD:HD + 1], 1.0).then_inc(consts, 1)
                for h in range(2):
                    for s in (parts_out, v_out, adjT_out, neg_out):
                        pool.sem_inc(s[h], 16)
                nc.gpsimd.memset(closed[:], NEG).then_inc(consts, 1)
                pool.wait_ge(consts, 4)
                nc.gpsimd.affine_select(out=closed[:], in_=closed[:], compare_op=ALU.not_equal, fill=0.0,
                                        base=0, pattern=[[P, NT], [-1, N]], channel_multiplier=1).then_inc(consts, 1)
                pool.sem_inc(neg_ready, 2)
                with pool.Fori(0, PAIRS) as i:
                    for h in range(2):
                        b = 2 * i + h
                        gate(pool, adj_in[h], i * 16 + 16, pool_ticks)
                        gate(pool, neg_ready, b + 1, pool_ticks)
                        nc.gpsimd.tensor_scalar(adj_b[:, h], adj_i[:, h], 0.0, 5.0, ALU.max, ALU.min).then_inc(adj_cast, 1)

            @block.scalar
            def _(act):
                act.wait_ge(consts, 5)
                act.wait_ge(weights_in, 48)
                nc.scalar.mul(bqk_s[:, 0:1], bqk[:, 0:1], 0.25).then_inc(consts, 1)
                act.wait_ge(consts, 6)
                act.sem_inc(adjT_sb, NT)
                act.sem_inc(xT_sb, 1)
                act.sem_inc(qk_sb, 2)
                with act.Fori(0, PAIRS) as i:
                    norm.root(act, i, eps)
                    for h in range(2):
                        b = 2 * i + h
                        act.wait_ge(adjT_out[h], 16 * i + 16)
                        for j in range(NT):
                            act.wait_ge(adjT_ps, NT * (b + 1) + (j + 1))
                            nc.scalar.copy(adjT[:, h, j], ps_a[j][:, 0:N]).then_inc(adjT_sb, 1)
                        act.wait_ge(xT_ps, b + 1)
                        nc.scalar.copy(xT[:, h], ps_x[:]).then_inc(xT_sb, 1)
                        act.wait_ge(qk_ps, 2 * b + 1)
                        nc.scalar.activation(qk[:, h, 0], ps_q[:], ACT.Identity, bias=bqk_s[:, 0:1], scale=0.25).then_inc(qk_sb, 1)
                        act.wait_ge(qk_ps, 2 * b + 2)
                        nc.scalar.activation(qk[:, h, 1], ps_k[:], ACT.Identity, bias=bqk[:, 1:2], scale=1.0).then_inc(qk_sb, 1)

            @block.vector
            def _(dve):
                PER = Norm.PER - 3 + 2 * 2
                dve.wait_ge(consts, 5)
                dve.wait_ge(weights_in, 48)
                dve.sem_inc(dve_own, 1)
                dve.sem_inc(v_sb, 1)
                with dve.Fori(0, PAIRS) as i:
                    own = Own(dve, dve_own, i, PER)
                    for h in range(2):
                        dve.wait_ge(x_in[h], 16 * i + 16)
                        norm.stats_of(own, xn[:, h], h)
                    norm.variance(dve, own, i, dve_ticks)
                    norm.inverse(dve, own, i)
                    for h in range(2):
                        norm.apply(own, xn[:, h], xn[:, h], h, (xn_ready, 2 * i + (h + 1)))
                    for h in range(2):
                        b = 2 * i + h
                        dve.wait_ge(adjT_sb, NT * (b + 2))
                        dve.wait_ge(neg_out[h], 16 * i + 16)
                        own.wait()
                        own.done(nc.vector.tensor_tensor(neg[:, h], adj_b[:, h], adjT[:, h], ALU.max))
                        own.wait()
                        own.tell(nc.vector.scalar_tensor_tensor(
                            out=neg[:, h].rearrange("p t m -> p (t m)"), in0=neg[:, h].rearrange("p t m -> p (t m)"), scalar=0.0,
                            in1=closed[:].rearrange("p t m -> p (t m)"), op0=ALU.is_le, op1=ALU.mult), neg_ready, b + 3)
                        dve.wait_ge(v_ps, b + 1)
                        dve.wait_ge(v_out[h], 16 * i + 16)
                        own.wait()
                        own.tell(nc.vector.tensor_tensor(
                            va[:, h, :, :, 0:HD], ps_v[:].rearrange("p (t h d) -> p t h d", t=NT, h=HEADS),
                            bv[:].rearrange("p (o h d) -> p o h d", o=1, h=HEADS).broadcast_to([P, NT, HEADS, HD]), ALU.add), v_sb, b + 2)
                        dve.wait_ge(qk_sb, 2 * b + 4)
                        dve.wait_ge(parts_out[h], 16 * i + 16)
                        own.wait()
                        own.done(nc.vector.tensor_copy(parts[:, h, 0], qk[:, h]))
                        own.wait()
                        own.tell(nc.vector.tensor_tensor(parts[:, h, 1], qk[:, h], parts[:, h, 0].bitcast(F32), ALU.subtract), parts_ready, b + 1)
                    own.end()

            @block.tensor
            def _(pe):
                pe.wait_ge(weights_in, 48)
                pe.sem_inc(adjT_ps, NT)
                with pe.Fori(0, PAIRS) as i:
                    for h in range(2):
                        b = 2 * i + h
                        pe.wait_ge(adj_cast, b + 1)
                        for j in range(NT):
                            pe.wait_ge(adjT_sb, NT * b + (j + 1))
                            for t in range(NT):
                                mm = nc.tensor.transpose(ps_a[j][:, t * P:(t + 1) * P], adj_b[:, h, t, j * P:(j + 1) * P], identb[:])
                            mm.then_inc(adjT_ps, 1)
                        pe.wait_ge(xn_ready, b + 1)
                        pe.wait_ge(xT_sb, b + 1)
                        for t in range(NT):
                            mm = nc.tensor.transpose(ps_x[:, t * P:(t + 1) * P], xn[:, h, t], ident[:])
                        mm.then_inc(xT_ps, 1)
                        pe.wait_ge(xT_sb, b + 2)
                        pe.wait_ge(qk_sb, 2 * b + 1)
                        nc.tensor.matmul(ps_q[:], wT[:, 0:D], xT[:, h], start=True, stop=True).then_inc(qk_ps, 1)
                        pe.wait_ge(qk_sb, 2 * b + 2)
                        nc.tensor.matmul(ps_k[:], wT[:, D:2 * D], xT[:, h], start=True, stop=True).then_inc(qk_ps, 1)
                        pe.wait_ge(v_sb, b + 1)
                        for t in range(NT):
                            mm = nc.tensor.matmul(ps_v[:, t * P:(t + 1) * P], xT[:, h, t * P:(t + 1) * P], wT[:, 2 * D:3 * D], start=True, stop=True)
                        mm.then_inc(v_ps, 1)


UNITS = B * GROUPS
AHEAD = 4
LOADS = 9
TILES = NT * GH


def attend(nc, identf, identb, qk_d, v_d, neg_d, ctx_d, packs):
    with ExitStack() as c:
        sb = lambda n, s, d: c.enter_context(nc.sbuf_tensor("a_" + n, s, d))
        pb = lambda n, s, d: c.enter_context(nc.psum_tensor("a_" + n, s, d))
        fresh = Semaphores(c, nc)
        sem = lambda n: fresh("a_" + n)
        many = lambda n: [sem(f"{n}{k}") for k in range(AHEAD)]
        SHIFT = 3 * HD
        qs = [sb(f"qs{k}", [P, GH, N], F32R) for k in range(AHEAD)]
        ks = [sb(f"ks{k}", [P, GH, N], F32R) for k in range(AHEAD)]
        nm = sb("nm", [P, AHEAD, NT, N], BF16)
        va = sb("va", [P, AHEAD, NT, GH, 32], F32)
        rows = sb("rows", [1, 2, GH * N], F32)
        junk = sb("junk", [P, 4, N], BF16)
        mx = sb("mx", [P, 2, TILES], F32)
        nmx = sb("nmx", [TILES, 2, P], F32R)
        pt = sb("pt", [P, 8, N], F32)
        ctx = sb("ctx", [P, 2, N], F32)
        WIDE = 2 * P * max(hc for _, _, hc in packs)
        w_raw, w_high, w_low = sb("w_raw", [P, WIDE + 8], F32), sb("w_high", [P, WIDE], F32R), sb("w_low", [P, WIDE], F32R)
        nothing = sb("nothing", [P, WIDE], F32)
        w_zeros, w_came, w_split, w_gone, w_ticks = (sem(n) for n in ("w_zeros", "w_came", "w_split", "w_gone", "w_ticks"))
        s1 = [pb(f"s1_{k}", [P, N], F32) for k in range(2)]
        s2 = [pb(f"s2_{k}", [P, N], F32) for k in range(GH)]
        ps_c = pb("ps_c", [P, N], F32)
        ps_m = pb("ps_m", [P, N], F32)
        unit_in, shift_in = many("unit_in"), many("shift_in")
        ctx_out = [sem("ctx_out0"), sem("ctx_out1")]
        consts, s1_ps, max_done, mxT_ps, nmx_ready = (sem(n) for n in ("consts", "s1_ps", "max_done", "mxT_ps", "nmx_ready"))
        s2_ps, exp_done, pv_done, ctx_sb = (sem(n) for n in ("s2_ps", "exp_done", "pv_done", "ctx_sb"))
        sp_ticks, dve_ticks, q_zeros, k_zeros = (sem(n) for n in ("sp_ticks", "dve_ticks", "q_zeros", "k_zeros"))

        with nc.Block() as block:
            @block.sync
            def _(sp):
                def load(b, g, k, turn):
                    heads = slice(g * GH, (g + 1) * GH)
                    if turn is not None:
                        gate(sp, ctx_sb, turn, sp_ticks)
                    src = qk_d[b].rearrange("(h d) a q n -> d h a q n", d=HD)
                    for s, (qpart, kpart) in enumerate(((0, 0), (0, 1), (1, 0))):
                        at = slice(s * HD, (s + 1) * HD)
                        sp.dma_start(qs[k][at].bitcast(F32), src[:, heads, qpart, 0]).then_inc(unit_in[k], 16)
                        sp.dma_start(ks[k][at].bitcast(F32), src[:, heads, kpart, 1]).then_inc(unit_in[k], 16)
                    sp.dma_start(qs[k][SHIFT:SHIFT + 1].bitcast(F32).rearrange("p h n -> p (h n)"), rows[:, 0]).then_inc(unit_in[k], 16)
                    sp.dma_start(nm[:, k], neg_d[b]).then_inc(unit_in[k], 16)
                    sp.dma_start(va[:, k], v_d[b][:, :, heads]).then_inc(unit_in[k], 16)

                def shift(u, k):
                    gate(sp, nmx_ready, u + 1, sp_ticks)
                    sp.dma_start(qs[k][SHIFT:SHIFT + 1].bitcast(F32).rearrange("o h n -> o (h n)"), nmx[:, k % 2].bitcast(F32)).then_inc(shift_in[k], 16)

                def store(u, k):
                    gate(sp, ctx_sb, u + 2, sp_ticks)
                    sp.dma_start(ctx_d[u], ctx[:, k % 2]).then_inc(ctx_out[k % 2], 16)

                sp.wait_ge(consts, 2)
                for k in range(AHEAD):
                    sp.wait_ge(q_zeros, k + 1)
                    sp.wait_ge(k_zeros, k + 1)
                    sp.dma_start(ks[k][SHIFT:SHIFT + 1].bitcast(F32).rearrange("p h n -> p (h n)"), rows[:, 1]).then_inc(unit_in[k], 16)
                    if k < 3:
                        load(k // 2, k % 2, k, None)
                shift(0, 0)
                shift(1, 1)
                with sp.Fori(0, PAIRS - 1) as i:
                    for w in range(4):
                        load(2 * i + (w + 3) // 2, (w + 3) % 2, (w + 3) % 4, 4 * i + w + 1)
                        shift(4 * i + (w + 2), (w + 2) % 4)
                        store(4 * i + w, w)
                u = UNITS - 4
                for w in range(4):
                    if w == 0:
                        load(B - 1, 1, 3, u + 1)
                    if w < 2:
                        shift(u + w + 2, w + 2)
                    store(u + w, w)
                for k in range(2):
                    sp.wait_ge(ctx_out[k], 16 * (UNITS // 2 + 1))

            @block.gpsimd
            def _(pool):
                nc.gpsimd.memset(rows[:, 0], 0.0).then_inc(consts, 1)
                nc.gpsimd.memset(rows[:, 1], 1.0).then_inc(consts, 1)
                for k in range(AHEAD):
                    nc.gpsimd.memset(qs[k][:].bitcast(F32), 0.0).then_inc(q_zeros, 1)
                nc.gpsimd.memset(nothing[:], 0.0).then_inc(w_zeros, 1)
                pool.wait_ge(w_zeros, 1)
                for n, (given, parts, hc) in enumerate(packs):
                    split_weights(pool, nc, w_raw, w_high, w_low, nothing, given, parts, w_came, w_split, (w_gone, w_ticks), hc, E_ * n)

            @block.scalar
            def _(act):
                def unit(i, w, last):
                    u = 4 * i + w
                    for kt in range(NT):
                        act.wait_ge(pv_done, 4 * u + (kt + 1))
                        for hh in range(GH):
                            m = 16 * u + (kt * GH + hh)
                            act.wait_ge(s2_ps, m + 1)
                            nc.scalar.activation(pt[:, (kt * GH + hh) % 8], s2[hh][:], ACT.Exp).then_inc(exp_done, 1)
                    if not last:
                        negated(u + 2, w % 2, i, w)

                def negated(u, k, i, w):
                    act.wait_ge(mxT_ps, u + 1)
                    act.wait_ge(shift_in[w], 16 * i + 32)
                    nc.scalar.activation(nmx[:, k], ps_m[0:TILES, 0:P], ACT.Copy, scale=-1.0).then_inc(nmx_ready, 1)

                act.sem_inc(exp_done, 4)
                for k in range(AHEAD):
                    act.sem_inc(shift_in[k], 16)
                for k in range(2):
                    act.wait_ge(mxT_ps, k + 1)
                    nc.scalar.activation(nmx[:, k], ps_m[0:TILES, 0:P], ACT.Copy, scale=-1.0).then_inc(nmx_ready, 1)
                with act.Fori(0, PAIRS - 1) as i:
                    for w in range(4):
                        unit(i, w, False)
                for w in range(4):
                    unit(PAIRS - 1, w, w >= 2)

            @block.vector
            def _(dve):
                def maxima(u, k, nth):
                    gate(dve, unit_in[k], nth, dve_ticks)
                    for j in range(TILES):
                        qt, hh = divmod(j, GH)
                        n = 16 * u + j
                        gate(dve, max_done, n + 1, dve_ticks)
                        gate(dve, s1_ps, n + 1, dve_ticks)
                        nc.vector.tensor_tensor_reduce(
                            out=junk[:, j % 4], in0=s1[j % 2][:], in1=nm[:, k, qt], scale=1.0, scalar=-3.0e38,
                            op0=ALU.add, op1=ALU.max, accum_out=mx[:, k % 2, hh * NT + qt:hh * NT + qt + 1]).then_inc(max_done, 1)

                def result(u, w, turn):
                    gate(dve, pv_done, 4 * u + 6, dve_ticks)
                    gate(dve, ctx_out[w % 2], turn, dve_ticks)
                    nc.vector.tensor_copy(ctx[:, w % 2], ps_c[:]).then_inc(ctx_sb, 1)

                for k in range(AHEAD):
                    nc.vector.memset(ks[k][:].bitcast(F32), 0.0).then_inc(k_zeros, 1)
                dve.sem_inc(max_done, 4)
                dve.sem_inc(ctx_sb, 1)
                for k in range(2):
                    dve.sem_inc(ctx_out[k], 16)
                for k in range(2):
                    maxima(k, k, 16 * (LOADS + 1))
                with dve.Fori(0, PAIRS - 1) as i:
                    for w in range(4):
                        maxima(4 * i + (w + 2), (w + 2) % 4, 16 * LOADS * i + 16 * (LOADS * (2 if w >= 2 else 1) + 1))
                        result(4 * i + w, w, 32 * i + 16 * (w // 2 + 1))
                i = PAIRS - 1
                for w in range(4):
                    if w < 2:
                        maxima(4 * i + w + 2, w + 2, 16 * (LOADS * (i + 1) + 1))
                    result(4 * i + w, w, 32 * i + 16 * (w // 2 + 1))

            @block.tensor
            def _(pe):
                def by_query(u, k, j):
                    qt, hh = divmod(j, GH)
                    pe.wait_ge(max_done, 16 * u + (j + 3))
                    nc.tensor.matmul(s1[j % 2][:], qs[k][:, hh, qt * P:(qt + 1) * P], ks[k][:, hh], start=True, stop=True).then_inc(s1_ps, 1)

                def maxima_turned(u, k):
                    pe.wait_ge(max_done, 16 * u + 20)
                    pe.wait_ge(nmx_ready, u)
                    nc.tensor.transpose(ps_m[0:TILES, 0:P], mx[:, k % 2], identf[:]).then_inc(mxT_ps, 1)

                def by_key(u, k, kt, hh):
                    pe.wait_ge(exp_done, 16 * u + (kt * GH + hh + 1))
                    nc.tensor.matmul(s2[hh][:], ks[k][:, hh, kt * P:(kt + 1) * P], qs[k][:, hh], start=True, stop=False)
                    nc.tensor.matmul(s2[hh][:], identb[:], nm[:, k, kt], start=False, stop=True).then_inc(s2_ps, 1)

                def values(u, k, kt, hh):
                    if (kt, hh) == (0, 0):
                        pe.wait_ge(ctx_sb, u + 1)
                    pe.wait_ge(exp_done, 16 * u + (kt * GH + hh + 5))
                    mm = nc.tensor.matmul(ps_c[32 * hh:32 * hh + 32, :], va[:, k, kt, hh], pt[:, (kt * GH + hh) % 8],
                                          start=(kt == 0), stop=(kt == NT - 1))
                    if hh == GH - 1:
                        mm.then_inc(pv_done, 1)

                def unit(i, w, last, nth):
                    u, k = 4 * i + w, (w + 2) % 4
                    pe.wait_ge(shift_in[w], 16 * i + 32)
                    if not last:
                        pe.wait_ge(unit_in[k], nth)
                    for kt in range(NT):
                        for hh in range(GH):
                            by_key(u, w, kt, hh)
                            if not last:
                                by_query(u + 2, k, kt * GH + hh)
                        if kt >= 1:
                            for hh in range(GH):
                                values(u, w, kt - 1, hh)
                    if not last:
                        maxima_turned(u + 2, k)
                    for hh in range(GH):
                        values(u, w, NT - 1, hh)

                pe.sem_inc(pv_done, 2)
                for u in range(2):
                    pe.wait_ge(unit_in[u], 16 * (LOADS + 1))
                    for j in range(TILES):
                        by_query(u, u, j)
                    pe.wait_ge(max_done, 16 * u + 20)
                    if u > 0:
                        pe.wait_ge(nmx_ready, u)
                    nc.tensor.transpose(ps_m[0:TILES, 0:P], mx[:, u], identf[:]).then_inc(mxT_ps, 1)
                with pe.Fori(0, PAIRS - 1) as i:
                    for w in range(4):
                        unit(i, w, False, 16 * LOADS * i + 16 * (LOADS * (2 if w >= 2 else 1) + 1))
                for w in range(4):
                    unit(PAIRS - 1, w, w >= 2, 16 * (LOADS * PAIRS + 1))


E_ = 8
TILE = 512
CAP = B * N + TILE
ROWS = E_ * CAP + 2 * TILE
LAST = ROWS - TILE
MOE_TILES = 2 * B * N // TILE + E_


def wide(ap, shape):
    return ap.rearrange("p (o d) -> p o d", o=1).broadcast_to(shape)


class Router:

    def __init__(self, c, nc, fresh, name, gate_w, gate_b, xs_d, identf):
        sb = lambda n, s, d: c.enter_context(nc.sbuf_tensor(name + n, s, d))
        sem = lambda n: fresh(name + n)
        self.nc, self.gate_w, self.gate_b, self.xs_d, self.identf = nc, gate_w, gate_b, xs_d, identf
        self.gw = sb("gw", [P, E_], F32)
        self.gb = sb("gb", [P, E_], F32)
        self.xT = sb("xT", [P, 2, N], F32)
        self.lg = sb("lg", [P, 2, NT, E_], F32)
        self.top = sb("top", [P, 2, NT, E_], F32)
        self.ix = sb("ix", [P, 2, NT, E_], U32)
        self.ixf = sb("ixf", [P, 2, 2, NT], F32)
        self.iota = sb("iota", [P, E_], F32)
        self.iota_i = sb("iota_i", [P, E_], I32)
        self.hot = sb("hot", [P, 2, 2, NT, E_], F32)
        self.both = sb("both", [P, 2, NT, E_], BF16)
        self.pos = sb("pos", [P, 2, NT, E_], F32)
        self.pick = sb("pick", [P, 2, 2, NT, E_], F32)
        self.slot = sb("slot", [P, 2, 2, NT], F32)
        self.slot_i = sb("slot_i", [P, 2, 2, NT], I32)
        self.before = sb("before", [P, P], BF16)
        self.ones = sb("ones", [P, P], BF16)
        self.consts, self.gxT_ps, self.gxT_sb = sem("consts"), sem("gxT_ps"), sem("gxT_sb")
        self.lg_ps, self.chosen, self.rank_ps, self.slots = sem("lg_ps"), sem("chosen"), sem("rank_ps"), sem("slots")
        self.sent, self.gone, self.ticks = sem("sent"), sem("gone"), sem("ticks")
        self.PER = 2 + 8 + 7 + 1 + 6

    def load(self, sp, done):
        sp.dma_start(self.gw[:], self.gate_w).then_inc(done, 16)
        sp.dma_start(self.gb[:], bcast_rows(self.gate_b, P)).then_inc(done, 16)

    def pool_start(self, pool, base):
        nc = self.nc
        nc.gpsimd.memset(self.ones[:], 1.0).then_inc(self.consts, 1)
        nc.gpsimd.memset(self.before[:], 1.0).then_inc(self.consts, 1)
        nc.gpsimd.iota(self.iota_i[:], pattern=[[1, E_]], base=0, channel_multiplier=0).then_inc(self.consts, 1)
        pool.wait_ge(self.consts, 3)
        nc.gpsimd.affine_select(out=self.before[:], in_=self.before[:], compare_op=ALU.is_gt, fill=0.0,
                                base=0, pattern=[[1, P]], channel_multiplier=-1).then_inc(self.consts, 1)
        nc.gpsimd.tensor_copy(self.iota[:], self.iota_i[:]).then_inc(self.consts, 1)
        pool.wait_ge(self.consts, 5)
        nc.gpsimd.tensor_scalar(base[:], self.iota[:], float(CAP), None, ALU.mult).then_inc(self.consts, 1)
        pool.sem_inc(self.gone, 2)

    def pool_send(self, pool, h, i, b, rows):
        gate(pool, self.slots, b + 3, self.ticks)
        for k in range(2):
            for t in range(NT):
                self.nc.gpsimd.indirect_dma_start(
                    self.xs_d, bass.IndirectOffsetOnAxis(self.slot_i[:, h, k, t:t + 1], 0), rows[:, t], None).then_inc(self.sent, 16)
        gate(pool, self.sent, 16 * 2 * NT * (b + 1), self.ticks)
        pool.sem_inc(self.gone, 1)

    def pe_turn(self, pe, h, b, rows, ready, value, ps):
        pe.wait_ge(ready, value)
        for t in range(NT):
            mm = self.nc.tensor.transpose(ps[:, t * P:(t + 1) * P], rows[:, t], self.identf[:])
        mm.then_inc(self.gxT_ps, 1)

    def act_turn(self, act, h, b, ps):
        act.wait_ge(self.gxT_ps, b + 1)
        self.nc.scalar.copy(self.xT[:, h], ps[:]).then_inc(self.gxT_sb, 1)

    def pe_logits(self, pe, h, b, ps):
        pe.wait_ge(self.gxT_sb, b + 1)
        for t in range(NT):
            mm = self.nc.tensor.matmul(ps[:, t * E_:(t + 1) * E_], self.xT[:, h, t * P:(t + 1) * P], self.gw[:], start=True, stop=True)
        mm.then_inc(self.lg_ps, 1)

    def dve_choose(self, dve, own, h, b, ps, gaps_out):
        nc, lg, top = self.nc, self.lg[:, h], self.top[:, h]
        gate(dve, self.lg_ps, b + 1, self.ticks_dve)
        own.wait()
        own.done(nc.vector.tensor_tensor(lg, ps[:, 0:NT * E_].rearrange("p (t e) -> p t e", t=NT), wide(self.gb[:], [P, NT, E_]), ALU.add))
        gate(dve, *own.last, self.ticks_dve)
        for t in range(NT):
            own.done(nc.vector.max(top[:, t], lg[:, t]))
        gate(dve, *own.last, self.ticks_dve)
        for t in range(NT):
            own.done(nc.vector.max_index(self.ix[:, h, t], top[:, t], lg[:, t]))
        own.wait()
        own.done(nc.vector.tensor_copy(self.ixf[:, h], self.ix[:, h, :, 0:2].rearrange("p t k -> p k t")))
        own.wait()
        for k in range(2):
            own.done(nc.vector.tensor_tensor(self.hot[:, h, k], wide(self.iota[:], [P, NT, E_]),
                                             self.ixf[:, h, k].rearrange("p (t o) -> p t o", o=1).broadcast_to([P, NT, E_]), ALU.is_equal))
        own.wait()
        own.tell(nc.vector.tensor_tensor(self.both[:, h], self.hot[:, h, 0], self.hot[:, h, 1], ALU.add), self.chosen, b + 1)
        own.done(nc.vector.tensor_tensor(gaps_out, top, top[:, :, 0:1].broadcast_to([P, NT, E_]), ALU.subtract))

    def pe_rank(self, pe, h, b, ps):
        pe.wait_ge(self.chosen, b + 1)
        at = NT * E_
        for t in range(NT):
            for s in range(t + 1):
                self.nc.tensor.matmul(ps[:, at + t * E_:at + (t + 1) * E_], (self.before if s == t else self.ones)[:], self.both[:, h, s],
                                      start=(s == 0), stop=(s == t))
        for s in range(NT):
            mm = self.nc.tensor.matmul(ps[:, 2 * at:2 * at + E_], self.ones[:], self.both[:, h, s], start=(s == 0), stop=(s == NT - 1))
        mm.then_inc(self.rank_ps, 1)

    def dve_slots(self, dve, own, h, i, b, ps, base, keep):
        nc, at = self.nc, NT * E_
        gate(dve, self.rank_ps, b + 1, self.ticks_dve)
        own.wait()
        own.done(nc.vector.tensor_tensor(self.pos[:, h], ps[:, at:2 * at].rearrange("p (t e) -> p t e", t=NT), wide(base[:], [P, NT, E_]), ALU.add))
        own.wait()
        own.done(nc.vector.tensor_tensor(base[:], base[:], ps[:, 2 * at:2 * at + E_], ALU.add))
        for k in range(2):
            own.done(nc.vector.tensor_tensor(self.pick[:, h, k], self.hot[:, h, k], self.pos[:, h], ALU.mult))
        own.wait()
        own.done(nc.vector.tensor_reduce(self.slot[:, h], self.pick[:, h], AX.X, ALU.add))
        gate(dve, self.gone, b + 1, self.ticks_dve)
        own.wait()
        own.done(nc.vector.tensor_copy(keep, self.slot[:, h].rearrange("p k t -> p (k t)")))
        own.tell(nc.vector.tensor_copy(self.slot_i[:, h], self.slot[:, h]), self.slots, b + 3)


def after_attention(nc, x, xn_d, ctx_d, wo, bo, g1, c1, w1, b1, w2, b2, g2, c2, identf, route, x1_d, base, gaps, slots):
    with ExitStack() as c:
        sb = lambda n, s, d: c.enter_context(nc.sbuf_tensor("f_" + n, s, d))
        pb = lambda n, s, d: c.enter_context(nc.psum_tensor("f_" + n, s, d))
        fresh = Semaphores(c, nc)
        sem = lambda n: fresh("f_" + n)
        FC = 4
        ctx = sb("ctx", [P, 2, GROUPS, N], F32)
        xn = sb("xn", [P, 2, NT, D], F32)
        x0 = sb("x0", [P, 2, NT, D], F32)
        woT, w1T, w2T = sb("woT", [P, D], F32), sb("w1T", [P, FC * P], F32), sb("w2T", [P, FC, D], F32)
        b1c = sb("b1c", [P, FC], F32)
        rows = {n: sb(n, [P, D], F32) for n in ("bo", "g1", "c1", "b2", "g2", "c2")}
        eps = sb("eps", [P, 1], F32)
        rd = sb("rd", [P, 2, GROUPS, NT, GH], F32)
        cn = sb("cn", [P, 2, NT, D], F32)
        cT = sb("cT", [P, 2, N], F32)
        y = sb("y", [P, 2, NT, D], F32)
        yT = sb("yT", [P, 2, N], F32)
        hT = sb("hT", [P, 2, FC, N], F32)
        z = sb("z", [P, 2, NT, D], F32)
        x1 = sb("x1", [P, 2, NT, D], F32)
        xo = sb("xo", [P, 2, NT, D], F32)
        banks = [[pb(f"b{h}{n}", [P, N], F32) for n in range(4)] for h in range(2)]
        weights_in, consts = sem("weights_in"), sem("consts")
        ctx_in, xn_in, x_in = ([sem(n + "0"), sem(n + "1")] for n in ("ctx_in", "xn_in", "x_in"))
        ctxT_ps, cn_ready, cnT_ps, cT_sb, o_ps, y_ready = (sem(n) for n in ("ctxT_ps", "cn_ready", "cnT_ps", "cT_sb", "o_ps", "y_ready"))
        yT_ps, yT_sb, ff1_ps, hT_sb, ff2_ps, x1_ready, xo_ready = (sem(n) for n in ("yT_ps", "yT_sb", "ff1_ps", "hT_sb", "ff2_ps", "x1_ready", "xo_ready"))
        x1_out = [sem("x1_out0"), sem("x1_out1")]
        dve_own, dve_ticks, sp_ticks = sem("dve_own"), sem("dve_ticks"), sem("sp_ticks")
        n1, n2, n3 = (Norm(c, nc, fresh, f"f_n{k}") for k in range(3))
        r = Router(c, nc, fresh, "f_r", *route, identf)
        r.ticks_dve = dve_ticks
        halves = (0, 1)
        NW = 11

        with nc.Block() as block:
            @block.sync
            def _(sp):
                def load(b, h):
                    sp.dma_start(ctx[:, h], ctx_d[bass.ds(b * 2, 2) if not isinstance(b, int) else slice(2 * b, 2 * b + 2)].rearrange("g p n -> p g n")).then_inc(ctx_in[h], 16)
                    sp.dma_start(xn[:, h], xn_d[b].rearrange("(t p) d -> p t d", p=P)).then_inc(xn_in[h], 16)
                    sp.dma_start(x0[:, h], x[b].rearrange("(t p) d -> p t d", p=P)).then_inc(x_in[h], 16)

                def store(b, h):
                    gate(sp, x1_ready, b + 1, sp_ticks)
                    sp.dma_start(x1_d[b].rearrange("(t p) d -> p t d", p=P), x1[:, h]).then_inc(x1_out[h], 16)

                for t_, src in ((woT[:], wo), (w1T[:], w1), (w2T[:], w2)):
                    sp.dma_start(t_, src).then_inc(weights_in, 16)
                sp.dma_start(b1c[:], b1.rearrange("(a p) -> p a", p=P), allow_slow_non_contiguous=True).then_inc(weights_in, 16)
                for n, src in (("bo", bo), ("g1", g1), ("c1", c1), ("b2", b2), ("g2", g2), ("c2", c2)):
                    sp.dma_start(rows[n][:], bcast_rows(src, P)).then_inc(weights_in, 16)
                r.load(sp, weights_in)
                for h in halves:
                    load(h, h)
                with sp.Fori(0, PAIRS - 1) as i:
                    for h in halves:
                        store(2 * i + h, h)
                        load(2 * i + (h + 2), h)
                for h in halves:
                    store(B - 2 + h, h)
                for h in halves:
                    sp.wait_ge(x1_out[h], 16 * (PAIRS + 1))

            @block.gpsimd
            def _(pool):
                nc.gpsimd.memset(eps[:], EPS).then_inc(consts, 1)
                r.pool_start(pool, base)
                with pool.Fori(0, PAIRS) as i:
                    for h in halves:
                        r.pool_send(pool, h, i, 2 * i + h, xo[:, h])

            @block.scalar
            def _(act):
                act.wait_ge(consts, 1)
                act.wait_ge(weights_in, 16 * 12)
                for h in halves:
                    act.sem_inc(x1_out[h], 16)
                with act.Fori(0, PAIRS) as i:
                    for h in halves:
                        act.wait_ge(cnT_ps, 2 * i + (h + 1))
                        nc.scalar.copy(cT[:, h], banks[h][0][:]).then_inc(cT_sb, 1)
                    n1.root(act, i, eps)
                    for h in halves:
                        act.wait_ge(yT_ps, 2 * i + (h + 1))
                        nc.scalar.copy(yT[:, h], banks[h][0][:]).then_inc(yT_sb, 1)
                    for h in halves:
                        for f in range(FC):
                            act.wait_ge(ff1_ps, FC * (2 * i + h) + (f + 1))
                            nc.scalar.activation(hT[:, h, f], banks[h][2 + f % 2][:], ACT.Relu, bias=b1c[:, f:f + 1]).then_inc(hT_sb, 1)
                    n2.root(act, i, eps)
                    n3.root(act, i, eps)
                    for h in halves:
                        r.act_turn(act, h, 2 * i + h, banks[h][0])

            @block.vector
            def _(dve):
                PER = 140
                dve.wait_ge(r.consts, 6)
                dve.wait_ge(weights_in, 16 * 12)
                dve.sem_inc(dve_own, 1)
                dve.sem_inc(r.slots, 2)
                v = nc.vector
                with dve.Fori(0, PAIRS) as i:
                    own = Own(dve, dve_own, i, PER)
                    full = [P, NT, D]
                    for h in halves:
                        b = 2 * i + h
                        for g in range(GROUPS):
                            src = banks[h][g][:].rearrange("p (t h d) -> p t h d", t=NT, h=GH)
                            dve.wait_ge(ctxT_ps, 2 * b + (g + 1))
                            own.done(v.reciprocal(rd[:, h, g], src[:, :, :, HD]))
                            own.wait()
                            ins = v.tensor_tensor(cn[:, h, :, g * 64:(g + 1) * 64].rearrange("p t (h d) -> p t h d", h=GH), src[:, :, :, 0:HD],
                                                  rd[:, h, g].rearrange("p t (h o) -> p t h o", o=1).broadcast_to([P, NT, GH, HD]), ALU.mult)
                            own.done(ins) if g == 0 else own.tell(ins, cn_ready, b + 1)
                    for h in halves:
                        b = 2 * i + h
                        dve.wait_ge(xn_in[h], 16 * i + 16)
                        dve.wait_ge(o_ps, b + 1)
                        own.done(v.tensor_tensor(y[:, h], banks[h][1][:].rearrange("p (t d) -> p t d", t=NT), wide(rows["bo"][:], full), ALU.add))
                        own.wait()
                        own.done(v.tensor_tensor(y[:, h], y[:, h], xn[:, h], ALU.add))
                        n1.stats_of(own, y[:, h], h)
                    n1.variance(dve, own, i, dve_ticks)
                    n1.inverse(dve, own, i)
                    for h in halves:
                        b = 2 * i + h
                        n1.apply(own, y[:, h], y[:, h], h)
                        own.wait()
                        own.done(v.tensor_tensor(y[:, h], y[:, h], wide(rows["g1"][:], full), ALU.mult))
                        own.wait()
                        own.tell(v.tensor_tensor(y[:, h], y[:, h], wide(rows["c1"][:], full), ALU.add), y_ready, b + 1)
                    for h in halves:
                        b = 2 * i + h
                        dve.wait_ge(ff2_ps, b + 1)
                        own.done(v.tensor_tensor(z[:, h], banks[h][1][:].rearrange("p (t d) -> p t d", t=NT), wide(rows["b2"][:], full), ALU.add))
                        own.wait()
                        own.done(v.tensor_tensor(z[:, h], z[:, h], y[:, h], ALU.add))
                        n2.stats_of(own, z[:, h], h)
                    n2.variance(dve, own, i, dve_ticks)
                    n2.inverse(dve, own, i)
                    for h in halves:
                        b = 2 * i + h
                        n2.apply(own, z[:, h], z[:, h], h)
                        own.wait()
                        own.done(v.tensor_tensor(z[:, h], z[:, h], wide(rows["g2"][:], full), ALU.mult))
                        own.wait()
                        own.done(v.tensor_tensor(z[:, h], z[:, h], wide(rows["c2"][:], full), ALU.add))
                        dve.wait_ge(x_in[h], 16 * i + 16)
                        dve.wait_ge(x1_out[h], 16 * i + 16)
                        own.wait()
                        own.tell(v.tensor_tensor(x1[:, h], x0[:, h], z[:, h], ALU.add), x1_ready, b + 1)
                        n3.stats_of(own, x1[:, h], h)
                    n3.variance(dve, own, i, dve_ticks)
                    n3.inverse(dve, own, i)
                    for h in halves:
                        b = 2 * i + h
                        dve.wait_ge(r.gone, b + 1)
                        n3.apply(own, x1[:, h], xo[:, h], h, (xo_ready, b + 1))
                    for h in halves:
                        b = 2 * i + h
                        r.dve_choose(dve, own, h, b, banks[h][1], gaps[:, bass.ds(b * NT, NT), :])
                    for h in halves:
                        b = 2 * i + h
                        r.dve_slots(dve, own, h, i, b, banks[h][1], base, slots[:, bass.ds(b * (2 * NT), 2 * NT)])
                    own.end()

            @block.tensor
            def _(pe):
                pe.wait_ge(weights_in, 16 * 12)
                pe.wait_ge(r.consts, 6)
                with pe.Fori(0, PAIRS) as i:
                    for h in halves:
                        b = 2 * i + h
                        pe.wait_ge(ctx_in[h], 16 * i + 16)
                        pe.wait_ge(r.slots, b + 1)
                        for g in range(GROUPS):
                            for t in range(NT):
                                mm = nc.tensor.transpose(banks[h][g][:, t * P:(t + 1) * P], ctx[:, h, g, t * P:(t + 1) * P], identf[:])
                            mm.then_inc(ctxT_ps, 1)
                    for h in halves:
                        pe.wait_ge(cn_ready, 2 * i + (h + 1))
                        for t in range(NT):
                            mm = nc.tensor.transpose(banks[h][0][:, t * P:(t + 1) * P], cn[:, h, t], identf[:])
                        mm.then_inc(cnT_ps, 1)
                    for h in halves:
                        pe.wait_ge(cT_sb, 2 * i + (h + 1))
                        for t in range(NT):
                            mm = nc.tensor.matmul(banks[h][1][:, t * P:(t + 1) * P], cT[:, h, t * P:(t + 1) * P], woT[:], start=True, stop=True)
                        mm.then_inc(o_ps, 1)
                    for h in halves:
                        pe.wait_ge(y_ready, 2 * i + (h + 1))
                        for t in range(NT):
                            mm = nc.tensor.transpose(banks[h][0][:, t * P:(t + 1) * P], y[:, h, t], identf[:])
                        mm.then_inc(yT_ps, 1)
                    for h in halves:
                        b = 2 * i + h
                        pe.wait_ge(yT_sb, b + 1)
                        for f in range(FC):
                            if f >= 2:
                                pe.wait_ge(hT_sb, FC * b + (f - 1))
                            nc.tensor.matmul(banks[h][2 + f % 2][:], w1T[:, f * P:(f + 1) * P], yT[:, h], start=True, stop=True).then_inc(ff1_ps, 1)
                    for h in halves:
                        b = 2 * i + h
                        pe.wait_ge(hT_sb, FC * b + FC)
                        for t in range(NT):
                            for f in range(FC):
                                mm = nc.tensor.matmul(banks[h][1][:, t * P:(t + 1) * P], hT[:, h, f, t * P:(t + 1) * P], w2T[:, f], start=(f == 0), stop=(f == FC - 1))
                        mm.then_inc(ff2_ps, 1)
                    for h in halves:
                        r.pe_turn(pe, h, 2 * i + h, xo[:, h], xo_ready, 2 * i + (h + 1), banks[h][0])
                    for h in halves:
                        r.pe_logits(pe, h, 2 * i + h, banks[h][1])
                    for h in halves:
                        r.pe_rank(pe, h, 2 * i + h, banks[h][1])


def experts(nc, name, hc, func, base, xs_d, pack_d, y_d, slots, identf):
    H = hc * P
    LOW = 2 * H
    W1, W2, B1, B2 = 0, H, 4 * H, 4 * H + hc
    WIDTH = 4 * H + hc + 1
    DEEP = 4
    TURNS = MOE_TILES // 4 - 1
    with ExitStack() as c:
        sb = lambda n, s, d: c.enter_context(nc.sbuf_tensor(name + n, s, d))
        pb = lambda n, s, d: c.enter_context(nc.psum_tensor(name + n, s, d))
        fresh = Semaphores(c, nc)
        sem = lambda n: fresh(name + n)
        two = lambda n: [sem(n + "0"), sem(n + "1")]
        K = B * N // TILE
        iota_e, iota_k, iota_j = sb("iota_e", [P, E_], I32), sb("iota_k", [P, K], I32), sb("iota_j", [P, MOE_TILES], I32)
        iota_l, spare, idle = sb("iota_l", [P, MOE_TILES], I32), sb("spare", [P, MOE_TILES], F32), sb("idle", [P, MOE_TILES], F32)
        caps, steps, js = sb("caps", [P, E_], F32), sb("steps", [P, K], F32), sb("js", [P, MOE_TILES], F32)
        ones = sb("ones", [P, E_], F32)
        count, need, upto = sb("count", [P, E_], F32), sb("need", [P, E_], F32), sb("upto", [P, E_], F32)
        over = sb("over", [P, E_, K], F32)
        past = sb("past", [P, 2, MOE_TILES, E_], F32)
        sums = sb("sums", [P, 2, MOE_TILES], F32)
        row = sb("row", [P, 2, MOE_TILES], F32)
        table = sb("table", [P, 2, MOE_TILES], I32)
        ends = sb("ends", [P, E_], I32)
        shift = sb("shift", [P, E_ - 1], F32)
        slot = sb("slot", [P, B * 2 * NT], F32)
        behind = sb("behind", [P, B * 2 * NT, E_ - 1], F32)
        moved = sb("moved", [P, B * 2 * NT], F32)
        zeros = sb("zeros", [P, TILE], F32)
        pack = [sb(f"pack{k}", [P, WIDTH], F32R) for k in range(DEEP)]
        xs = sb("xs", [P, DEEP, NT, D], F32)
        xT = sb("xT", [P, 2, 2, TILE], F32R)
        h_full = sb("h_full", [P, 2, hc, TILE], F32)
        h_high, h_low = sb("h_high", [P, 2, hc, TILE], F32R), sb("h_low", [P, 2, hc, TILE], F32R)
        yT = sb("yT", [P, 2, TILE], F32)
        ys = sb("ys", [P, 2, NT, D], F32)
        ps_x, ps_b = pb("ps_x", [P, TILE], F32), pb("ps_b", [P, TILE], F32)
        ps_h = [pb(f"ps_h{h}", [P, TILE], F32) for h in range(4)]
        ps_y = [pb(f"ps_y{h}", [P, TILE], F32) for h in range(2)]
        consts, dve_own, tables, zeroed = sem("consts"), sem("dve_own"), sem("tables"), sem("zeroed")
        x_in, w_in, y_out = [sem(f"x_in{k}") for k in range(DEEP)], [sem(f"w_in{k}") for k in range(DEEP)], two("y_out")
        xT_ps, xT_high, xT_sb, h_ps, h_sb, low_sb = (sem(n) for n in ("xT_ps", "xT_high", "xT_sb", "h_ps", "h_sb", "low_sb"))
        y_ps, yT_sb, back_ps, y_sb = (sem(n) for n in ("y_ps", "yT_sb", "back_ps", "y_sb"))
        ticks, sp_ticks = sem("ticks"), sem("sp_ticks")
        tile_at = lambda d, at: d[bass.ds(at, TILE), :].rearrange("(p t) d -> p (t d)", p=P)
        flat = lambda a: a.rearrange("p t d -> p (t d)")

        with nc.Block() as block:
            @block.gpsimd
            def _(pool):
                g = nc.gpsimd
                g.iota(iota_e[:], pattern=[[CAP, E_]], base=0, channel_multiplier=0).then_inc(consts, 1)
                g.iota(iota_k[:], pattern=[[TILE, K]], base=0, channel_multiplier=0).then_inc(consts, 1)
                g.iota(iota_j[:], pattern=[[1, MOE_TILES]], base=0, channel_multiplier=0).then_inc(consts, 1)
                g.iota(iota_l[:], pattern=[[0, MOE_TILES // 2], [TILE, 2]], base=0, channel_multiplier=0).then_inc(consts, 1)
                g.memset(ones[:], 1.0).then_inc(consts, 1)
                g.memset(zeros[:], 0.0).then_inc(consts, 1)
                pool.wait_ge(consts, 6)
                pool.wait_ge(tables, 1)
                for e in range(E_ + 2):
                    at = E_ * CAP + (e - E_) * TILE if e >= E_ else g.value_load(ends[0:1, e:e + 1], min_val=0, max_val=E_ * CAP)
                    g.dma_start(tile_at(xs_d, at), zeros[:]).then_inc(zeroed, 16)
                pool.wait_ge(zeroed, 16 * (E_ + 2))

                def load(i, c):
                    k = c % DEEP
                    e = g.value_load(table[0:1, 0, bass.ds(4 * i + c, 1)], min_val=0, max_val=E_ - 1)
                    g.dma_start(pack[k][:].bitcast(F32), pack_d[e]).then_inc(w_in[k], 16)
                    at = g.value_load(table[0:1, 1, bass.ds(4 * i + c, 1)], min_val=0, max_val=LAST)
                    g.dma_start(flat(xs[:, k]), tile_at(xs_d, at)).then_inc(x_in[k], 16)

                for c in range(DEEP):
                    load(0, c)
                with pool.Fori(0, MOE_TILES // DEEP - 1) as i:
                    for c in range(DEEP):
                        gate(pool, yT_sb, 4 * i + (c + 1), ticks)
                        load(i, c + DEEP)

            @block.sync
            def _(sp):
                for h in range(2):
                    sp.sem_inc(y_out[h], 16)
                with sp.Fori(0, MOE_TILES // 2) as i:
                    for h in range(2):
                        gate(sp, y_sb, 2 * i + (h + 2), sp_ticks)
                        sp.dma_start(tile_at(y_d, (2 * i + h) * TILE), flat(ys[:, h])).then_inc(y_out[h], 16)
                for h in range(2):
                    sp.wait_ge(y_out[h], 16 * (MOE_TILES // 2 + 1))

            @block.vector
            def _(dve):
                v = nc.vector
                dve.wait_ge(consts, 6)
                dve.sem_inc(dve_own, 1)
                own = Own(dve, dve_own, 0, 0)
                for dst, src in ((caps, iota_e), (steps, iota_k), (js, iota_j), (spare, iota_l)):
                    own.done(v.tensor_copy(dst[:], src[:]))
                own.done(v.tensor_copy(ends[:], base[:]))
                own.wait()
                own.done(v.tensor_tensor(count[:], base[:], caps[:], ALU.subtract))
                own.wait()
                own.done(v.tensor_tensor(over[:], count[:].rearrange("p (e o) -> p e o", o=1).broadcast_to([P, E_, K]), wide(steps[:], [P, E_, K]), ALU.is_gt))
                own.wait()
                own.done(v.tensor_reduce(need[:], over[:], AX.X, ALU.add))
                own.wait()
                own.done(v.tensor_tensor_scan(upto[:], ones[:], need[:], 0.0, ALU.mult, ALU.add))
                own.wait()
                each = [P, MOE_TILES, E_]
                own.done(v.tensor_tensor(past[:, 0], js[:].rearrange("p (j o) -> p j o", o=1).broadcast_to(each), wide(upto[:], each), ALU.is_ge))
                own.wait()
                own.done(v.tensor_tensor(past[:, 1], past[:, 0], wide(need[:], each), ALU.mult))
                own.wait()
                own.done(v.tensor_reduce(sums[:], past[:], AX.X, ALU.add))
                own.wait()
                own.done(v.tensor_tensor(row[:, 1], js[:], sums[:, 1], ALU.subtract))
                own.wait()
                own.done(v.tensor_scalar(row[:, 1], row[:, 1], float(TILE), None, ALU.mult))
                own.wait()
                own.done(v.scalar_tensor_tensor(out=row[:, 1], in0=sums[:, 0], scalar=float(CAP), in1=row[:, 1], op0=ALU.mult, op1=ALU.add))
                own.wait()
                own.done(v.tensor_scalar(idle[:], sums[:, 0], float(E_), float(ROWS), ALU.is_ge, ALU.mult))
                own.done(v.tensor_scalar(spare[:], spare[:], float(E_ * CAP), None, ALU.add))
                own.wait()
                own.done(v.tensor_tensor(row[:, 1], row[:, 1], idle[:], ALU.add))
                own.wait()
                own.done(v.tensor_tensor(row[:, 1], row[:, 1], spare[:], ALU.min))
                own.done(v.tensor_scalar(row[:, 0], sums[:, 0], float(E_ - 1), None, ALU.min))
                own.wait()
                own.tell(v.tensor_copy(table[:], row[:]), tables, 1)

                own.done(v.tensor_copy(slot[:], slots[:]))
                own.done(v.tensor_scalar(shift[:], need[:, 0:E_ - 1], float(TILE), float(-CAP), ALU.mult, ALU.add))
                own.wait()
                each = [P, B * 2 * NT, E_ - 1]
                own.done(v.tensor_tensor(behind[:], slot[:].rearrange("p (s o) -> p s o", o=1).broadcast_to(each), wide(caps[:, 1:E_], each), ALU.is_ge))
                own.wait()
                own.done(v.tensor_tensor(behind[:], behind[:], wide(shift[:], each), ALU.mult))
                own.wait()
                own.done(v.tensor_reduce(moved[:], behind[:], AX.X, ALU.add))
                own.wait()
                own.done(v.tensor_tensor(slots[:], slot[:], moved[:], ALU.add))

                def turned(i, c):
                    j, h = 4 * i + c, c % 2
                    dve.wait_ge(xT_ps, j + 1)
                    v.tensor_copy(xT[:, h, 0], ps_x[:]).then_inc(xT_high, 1)
                    dve.wait_ge(xT_high, j + 1)
                    v.tensor_tensor(xT[:, h, 1], ps_x[:], xT[:, h, 0].bitcast(F32), ALU.subtract).then_inc(xT_sb, 1)

                def low(i, c, f):
                    j, h = 4 * i + c, c % 2
                    dve.wait_ge(h_sb, 4 * hc * i + (hc * c + f + 5))
                    v.tensor_tensor(h_low[:, h, f], h_full[:, h, f], h_high[:, h, f].bitcast(F32), ALU.subtract).then_inc(low_sb, 1)

                def result(i, c):
                    j, h = 4 * i + c, c % 2
                    dve.wait_ge(y_out[h], 32 * i + 16 * (c // 2 + 1))
                    dve.wait_ge(back_ps, j + 1)
                    v.tensor_copy(ys[:, h], ps_b[:].rearrange("p (t d) -> p t d", t=NT)).then_inc(y_sb, 1)

                def step(i, c, last=MOE_TILES):
                    if c + 1 < last:
                        for f in range(hc - 1):
                            low(i, c + 1, f)
                    if c + 2 < last:
                        turned(i, c + 2)
                    if c + 1 < last:
                        low(i, c + 1, hc - 1)
                    if not (isinstance(i, int) and i == 0 and c == 0):
                        result(i, c - 1)

                dve.sem_inc(y_sb, 1)
                turned(0, 0)
                turned(0, 1)
                for f in range(hc):
                    low(0, 0, f)
                step(0, 0)
                with dve.Fori(0, TURNS) as i:
                    for c in range(1, 5):
                        step(i, c)
                for c in range(1, 4):
                    step(TURNS, c, 4)
                result(TURNS, 3)

            @block.scalar
            def _(act):
                def hidden(i, c):
                    j, h = 4 * i + c, c % 2
                    act.wait_ge(y_ps, j + 1)
                    for f in range(hc):
                        n = hc * c + f
                        act.wait_ge(h_ps, 4 * hc * i + (n + 1))
                        bias = pack[c % DEEP][:, B1 + f:B1 + f + 1].bitcast(F32)
                        nc.scalar.activation(h_high[:, h, f], ps_h[n % 4][:], func, bias=bias)
                        nc.scalar.activation(h_full[:, h, f], ps_h[n % 4][:], func, bias=bias).then_inc(h_sb, 1)

                def biased(i, c):
                    j, h = 4 * i + c, c % 2
                    act.wait_ge(y_ps, j + 3)
                    nc.scalar.activation(yT[:, h], ps_y[h][:], ACT.Identity, bias=pack[c % DEEP][:, B2:B2 + 1].bitcast(F32)).then_inc(yT_sb, 1)

                act.sem_inc(h_sb, 4)
                hidden(0, 0)
                hidden(0, 1)
                biased(0, 0)
                with act.Fori(0, TURNS) as i:
                    for c in range(1, 5):
                        hidden(i, c + 1)
                        biased(i, c)
                for c in range(1, 4):
                    if c < 3:
                        hidden(TURNS, c + 1)
                    biased(TURNS, c)

            @block.tensor
            def _(pe):
                def turn(i, c):
                    k = c % DEEP
                    pe.wait_ge(x_in[k], 16 * (i + (c // DEEP + 1)))
                    if not (isinstance(i, int) and i == 0 and c == 0):
                        pe.wait_ge(xT_sb, 4 * i + c)
                    for t in range(NT):
                        mm = nc.tensor.transpose(ps_x[:, t * P:(t + 1) * P], xs[:, k, t], identf[:])
                    mm.then_inc(xT_ps, 1)

                def products(out, weights, at, rows, start, stop):
                    high, low = weights[:, at:at + P], weights[:, LOW + at:LOW + at + P]
                    nc.tensor.matmul(out, high, rows[0], start=start, stop=False)
                    nc.tensor.matmul(out, high, rows[1], start=False, stop=False)
                    return nc.tensor.matmul(out, low, rows[0], start=False, stop=stop)

                def up(i, c):
                    k, h = c % DEEP, c % 2
                    pe.wait_ge(w_in[k], 16 * (i + (c // DEEP + 1)))
                    pe.wait_ge(xT_sb, 4 * i + (c + 1))
                    for f in range(hc):
                        n = hc * c + f
                        pe.wait_ge(h_sb, 4 * hc * i + (n + 1))
                        products(ps_h[n % 4][:], pack[k], W1 + f * P, (xT[:, h, 0], xT[:, h, 1]), True, True).then_inc(h_ps, 1)

                def down(i, c):
                    k, h = c % DEEP, c % 2
                    for f in range(hc):
                        pe.wait_ge(low_sb, 4 * hc * i + (hc * c + f + 1))
                        mm = products(ps_y[h][:], pack[k], W2 + f * P, (h_high[:, h, f], h_low[:, h, f]), f == 0, f == hc - 1)
                    mm.then_inc(y_ps, 1)

                def back(i, c):
                    h = c % 2
                    pe.wait_ge(yT_sb, 4 * i + (c + 1))
                    pe.wait_ge(y_sb, 4 * i + (c + 1))
                    for t in range(NT):
                        mm = nc.tensor.transpose(ps_b[:, t * P:(t + 1) * P], yT[:, h, t * P:(t + 1) * P], identf[:])
                    mm.then_inc(back_ps, 1)

                pe.sem_inc(y_ps, 2)
                turn(0, 0)
                turn(0, 1)
                up(0, 0)
                up(0, 1)
                turn(0, 2)
                down(0, 0)
                with pe.Fori(0, TURNS) as i:
                    for c in range(1, 5):
                        up(i, c + 1)
                        turn(i, c + 2)
                        back(i, c - 1)
                        down(i, c)
                for c in range(1, 4):
                    if c < 3:
                        up(TURNS, c + 1)
                    if c < 2:
                        turn(TURNS, c + 2)
                    back(TURNS, c - 1)
                    down(TURNS, c)
                back(TURNS, 3)


def split_weights(pool, nc, raw, high, low, rest, pack_in, pack_out, came, split, gone, hc, first):
    H2 = 2 * hc * P
    with pool.Fori(0, E_) as e:
        nc.gpsimd.dma_start(raw[:, 0:H2 + hc + 1], pack_in[e]).then_inc(came, 16)
        pool.wait_ge(came, 16 * e + (16 * first + 16))
        nc.gpsimd.tensor_tensor(high[:, 0:H2], raw[:, 0:H2], rest[:, 0:H2], ALU.add).then_inc(split, 1)
        pool.wait_ge(split, 2 * e + (2 * first + 1))
        nc.gpsimd.tensor_tensor(low[:, 0:H2], raw[:, 0:H2], high[:, 0:H2].bitcast(F32), ALU.subtract).then_inc(split, 1)
        gate(pool, split, 2 * e + (2 * first + 2), gone[1])
        nc.gpsimd.dma_start(pack_out[e][:, 0:H2], high[:, 0:H2].bitcast(F32)).then_inc(gone[0], 16)
        nc.gpsimd.dma_start(pack_out[e][:, H2:2 * H2], low[:, 0:H2].bitcast(F32)).then_inc(gone[0], 16)
        nc.gpsimd.dma_start(pack_out[e][:, 2 * H2:2 * H2 + hc + 1], raw[:, H2:H2 + hc + 1]).then_inc(gone[0], 16)
        gate(pool, gone[0], 48 * e + (48 * first + 48), gone[1])


class Gather:

    def __init__(self, c, nc, fresh, name, y_d, gaps, slots, among):
        sb = lambda n, s, d: c.enter_context(nc.sbuf_tensor(name + n, s, d))
        sem = lambda n: fresh(name + n)
        self.nc, self.y_d, self.gaps, self.slots, self.among = nc, y_d, gaps, slots, among
        self.e = sb("e", [P, B * NT, E_], F32)
        self.total = sb("total", [P, B * NT], F32)
        self.inv = sb("inv", [P, B * NT], F32)
        self.w = sb("w", [P, B * NT, 2], F32)
        self.wh = sb("wh", [P, 2, NT, 2], F32)
        self.ix = sb("ix", [P, 2, 2 * NT], I32)
        self.y = sb("y", [P, 2, 2, NT, D], F32)
        self.ix_ready, self.exps, self.ticks = sem("ix_ready"), sem("exps"), sem("ticks")
        self.came = [sem("came0"), sem("came1")]
        self.ix_own = sem("ix_own")
        self.taken = sem("taken")

    def act_start(self, act):
        self.nc.scalar.activation(self.e[:], self.gaps[:], ACT.Exp).then_inc(self.exps, 1)

    def dve_start(self, dve, own):
        v, full = self.nc.vector, [P, B * NT, 2]
        dve.sem_inc(self.taken, 2)
        dve.wait_ge(self.exps, 1)
        own.done(v.tensor_reduce(self.total[:], self.e[:, :, 0:self.among], AX.X, ALU.add))
        own.wait()
        own.done(v.reciprocal(self.inv[:], self.total[:]))
        own.wait()
        own.done(v.tensor_tensor(self.w[:], self.e[:, :, 0:2], self.inv[:].rearrange("p (t o) -> p t o", o=1).broadcast_to(full), ALU.mult))
        own.wait()

    def pool_bring(self, pool, h, b):
        g = self.nc.gpsimd
        gate(pool, self.taken, b + 1, self.ticks)
        g.tensor_copy(self.ix[:, h], self.slots[:, bass.ds(b * (2 * NT), 2 * NT)]).then_inc(self.ix_ready, 1)
        gate(pool, self.ix_ready, b + 1, self.ticks)
        for k in range(2):
            for t in range(NT):
                g.indirect_dma_start(self.y[:, h, k, t], None, self.y_d, bass.IndirectOffsetOnAxis(self.ix[:, h, k * NT + t:k * NT + t + 1], 0)).then_inc(self.came[h], 16)

    def dve_add(self, dve, own, h, i, b, x):
        v = self.nc.vector
        own.wait()
        own.done(v.tensor_copy(self.wh[:, h], self.w[:, bass.ds(b * NT, NT), :]))
        gate(dve, self.came[h], 16 * 2 * NT * (i + 1), self.ticks_dve)
        for k in range(2):
            own.wait()
            for t in range(NT):
                ins = v.scalar_tensor_tensor(out=x[:, t], in0=self.y[:, h, k, t], scalar=self.wh[:, h, t, k:k + 1], in1=x[:, t], op0=ALU.mult, op1=ALU.add)
                own.tell(ins, self.taken, b + 3) if (k, t) == (1, NT - 1) else own.done(ins)


R_ = 4
PARTS = 3


def relations(nc, x1_d, adjT_d, y_d, weight, bias, identf, route, x2_d, base, gaps, slots):
    with ExitStack() as c:
        sb = lambda n, s, d: c.enter_context(nc.sbuf_tensor("g_" + n, s, d))
        pb = lambda n, s, d: c.enter_context(nc.psum_tensor("g_" + n, s, d))
        fresh = Semaphores(c, nc)
        sem = lambda n: fresh("g_" + n)
        x1 = sb("x1", [P, 2, NT, D], F32)
        xn = sb("xn", [P, 2, NT, D], F32)
        xo = sb("xo", [P, 2, NT, D], F32)
        aT = sb("aT", [P, 2, NT, N], BF16)
        mask = sb("mask", [P, 2, R_, NT, N], BF16)
        wr = sb("wr", [P, R_ * D], F32)
        bc = sb("bc", [P, 1], F32)
        eps = sb("eps", [P, 1], F32)
        xT = sb("xT", [P, 2, N], F32)
        part = sb("part", [P, 2, PARTS, NT, R_ * D], BF16)
        rest = sb("rest", [P, 2, NT, R_ * D], F32)
        oT = sb("oT", [P, 2, N], F32)
        banks = [[pb(f"b{h}{n}", [P, N], F32) for n in range(4)] for h in range(2)]
        weights_in, consts = sem("weights_in"), sem("consts")
        x_in, a_in, x2_out = ([sem(n + "0"), sem(n + "1")] for n in ("x_in", "a_in", "x2_out"))
        xn_ready, xT_ps, xT_sb, xw_ps, high_sb, rest_sb, mid_sb, parts_sb = (
            sem(n) for n in ("xn_ready", "xT_ps", "xT_sb", "xw_ps", "high_sb", "rest_sb", "mid_sb", "parts_sb"))
        masks, oT_ps, oT_sb, o_ps, x2_ready, xo_ready = (sem(n) for n in ("masks", "oT_ps", "oT_sb", "o_ps", "x2_ready", "xo_ready"))
        dve_own, dve_ticks, sp_ticks = sem("dve_own"), sem("dve_ticks"), sem("sp_ticks")
        n1, n2 = (Norm(c, nc, fresh, f"g_n{k}") for k in range(2))
        new_gaps, new_slots = gaps[1], slots[1]
        r = Router(c, nc, fresh, "g_r", *route, identf)
        q = Gather(c, nc, fresh, "g_q", y_d, gaps[0], slots[0], E_)
        r.ticks_dve = q.ticks_dve = dve_ticks
        halves = (0, 1)

        with nc.Block() as block:
            @block.sync
            def _(sp):
                def load(b, h):
                    sp.dma_start(x1[:, h], x1_d[b].rearrange("(t p) d -> p t d", p=P)).then_inc(x_in[h], 16)
                    sp.dma_start(aT[:, h], adjT_d[b]).then_inc(a_in[h], 16)

                def store(b, h):
                    gate(sp, x2_ready, b + 1, sp_ticks)
                    sp.dma_start(x2_d[b].rearrange("(t p) d -> p t d", p=P), x1[:, h]).then_inc(x2_out[h], 16)

                sp.dma_start(wr[:].rearrange("p (r o) -> p r o", r=R_), weight.rearrange("r d o -> d r o")).then_inc(weights_in, 16)
                sp.dma_start(bc[:], bias.rearrange("(p a) -> p a", a=1), allow_slow_non_contiguous=True).then_inc(weights_in, 16)
                r.load(sp, weights_in)
                for h in halves:
                    load(h, h)
                with sp.Fori(0, PAIRS - 1) as i:
                    for h in halves:
                        store(2 * i + h, h)
                        gate(sp, x2_out[h], 16 * i + 16, sp_ticks)
                        gate(sp, xo_ready, 2 * i + (h + 1), sp_ticks)
                        load(2 * i + (h + 2), h)
                for h in halves:
                    store(B - 2 + h, h)
                for h in halves:
                    sp.wait_ge(x2_out[h], 16 * PAIRS)

            @block.gpsimd
            def _(pool):
                nc.gpsimd.memset(eps[:], EPS).then_inc(consts, 1)
                r.pool_start(pool, base)
                for h in halves:
                    q.pool_bring(pool, h, h)
                with pool.Fori(0, PAIRS - 1) as i:
                    for h in halves:
                        q.pool_bring(pool, h, 2 * i + (h + 2))
                    for h in halves:
                        r.pool_send(pool, h, i, 2 * i + h, xo[:, h])
                for h in halves:
                    r.pool_send(pool, h, PAIRS - 1, B - 2 + h, xo[:, h])

            @block.scalar
            def _(act):
                q.act_start(act)
                act.wait_ge(consts, 1)
                act.wait_ge(weights_in, 16 * 4)
                with act.Fori(0, PAIRS) as i:
                    n1.root(act, i, eps)
                    for h in halves:
                        act.wait_ge(xT_ps, 2 * i + (h + 1))
                        nc.scalar.copy(xT[:, h], banks[h][0][:]).then_inc(xT_sb, 1)
                    for h in halves:
                        for t in range(NT):
                            act.wait_ge(xw_ps, NT * (2 * i + h) + (t + 1))
                            nc.scalar.copy(part[:, h, 0, t], banks[h][2 + t % 2][:]).then_inc(high_sb, 1)
                            act.wait_ge(rest_sb, NT * (2 * i + h) + (t + 3))
                            nc.scalar.copy(part[:, h, 1, t], rest[:, h, t]).then_inc(mid_sb, 1)
                    for h in halves:
                        act.wait_ge(oT_ps, 2 * i + (h + 1))
                        nc.scalar.activation(oT[:, h], banks[h][1][:], ACT.Identity, bias=bc[:], scale=1.0).then_inc(oT_sb, 1)
                    n2.root(act, i, eps)
                    for h in halves:
                        r.act_turn(act, h, 2 * i + h, banks[h][0])

            @block.vector
            def _(dve):
                PER = 112
                v = nc.vector
                dve.wait_ge(r.consts, 6)
                dve.wait_ge(weights_in, 16 * 4)
                dve.sem_inc(dve_own, 1)
                dve.sem_inc(r.slots, 2)
                dve.sem_inc(rest_sb, 2)
                first = Own(dve, q.ix_own, 0, 3)
                dve.sem_inc(q.ix_own, 1)
                q.dve_start(dve, first)
                with dve.Fori(0, PAIRS) as i:
                    own = Own(dve, dve_own, i, PER)
                    for h in halves:
                        b = 2 * i + h
                        gate(dve, x_in[h], 16 * i + 16, dve_ticks)
                        q.dve_add(dve, own, h, i, b, x1[:, h])
                        n1.stats_of(own, x1[:, h], h)
                    n1.variance(dve, own, i, dve_ticks)
                    n1.inverse(dve, own, i)
                    for h in halves:
                        n1.apply(own, x1[:, h], xn[:, h], h, (xn_ready, 2 * i + (h + 1)))
                    for h in halves:
                        gate(dve, a_in[h], 16 * i + 16, dve_ticks)
                        for k in range(R_):
                            ins = v.tensor_scalar(mask[:, h, k], aT[:, h], float(k + 1), None, ALU.is_equal)
                            own.tell(ins, masks, 2 * i + (h + 1)) if k == R_ - 1 else own.done(ins)
                    for h in halves:
                        for t in range(NT):
                            n = NT * (2 * i + h) + t
                            dve.wait_ge(high_sb, n + 1)
                            own.tell(v.tensor_tensor(rest[:, h, t], banks[h][2 + t % 2][:], part[:, h, 0, t], ALU.subtract), rest_sb, n + 3)
                            dve.wait_ge(mid_sb, n + 1)
                            own.tell(v.tensor_tensor(part[:, h, 2, t], rest[:, h, t], part[:, h, 1, t], ALU.subtract), parts_sb, n + 1)
                    for h in halves:
                        b = 2 * i + h
                        dve.wait_ge(o_ps, b + 1)
                        own.tell(v.tensor_tensor(x1[:, h], x1[:, h], banks[h][0][:].rearrange("p (t d) -> p t d", t=NT), ALU.add), x2_ready, b + 1)
                        n2.stats_of(own, x1[:, h], h)
                    n2.variance(dve, own, i, dve_ticks)
                    n2.inverse(dve, own, i)
                    for h in halves:
                        b = 2 * i + h
                        dve.wait_ge(r.gone, b + 1)
                        n2.apply(own, x1[:, h], xo[:, h], h, (xo_ready, b + 1))
                    for h in halves:
                        b = 2 * i + h
                        r.dve_choose(dve, own, h, b, banks[h][1], new_gaps[:, bass.ds(b * NT, NT), :])
                    for h in halves:
                        b = 2 * i + h
                        r.dve_slots(dve, own, h, i, b, banks[h][1], base, new_slots[:, bass.ds(b * (2 * NT), 2 * NT)])
                    own.end()

            @block.tensor
            def _(pe):
                pe.wait_ge(weights_in, 16 * 4)
                pe.wait_ge(r.consts, 6)
                with pe.Fori(0, PAIRS) as i:
                    for h in halves:
                        b = 2 * i + h
                        pe.wait_ge(xn_ready, b + 1)
                        for t in range(NT):
                            mm = nc.tensor.transpose(banks[h][0][:, t * P:(t + 1) * P], xn[:, h, t], identf[:])
                        mm.then_inc(xT_ps, 1)
                    for h in halves:
                        b = 2 * i + h
                        pe.wait_ge(xT_sb, b + 1)
                        for t in range(NT):
                            pe.wait_ge(rest_sb, NT * b + (t + 1))
                            nc.tensor.matmul(banks[h][2 + t % 2][:], xT[:, h, t * P:(t + 1) * P], wr[:], start=True, stop=True).then_inc(xw_ps, 1)
                    for h in halves:
                        b = 2 * i + h
                        pe.wait_ge(masks, b + 1)
                        pe.wait_ge(r.slots, b + 1)
                        for t in range(NT):
                            pe.wait_ge(parts_sb, NT * b + (t + 1))
                            for k in range(R_):
                                for s in range(PARTS):
                                    mm = nc.tensor.matmul(banks[h][1][:], part[:, h, s, t, k * D:(k + 1) * D], mask[:, h, k, t],
                                                          start=(t, k, s) == (0, 0, 0), stop=(t, k, s) == (NT - 1, R_ - 1, PARTS - 1))
                        mm.then_inc(oT_ps, 1)
                    for h in halves:
                        b = 2 * i + h
                        pe.wait_ge(oT_sb, b + 1)
                        for t in range(NT):
                            mm = nc.tensor.transpose(banks[h][0][:, t * P:(t + 1) * P], oT[:, h, t * P:(t + 1) * P], identf[:])
                        mm.then_inc(o_ps, 1)
                    for h in halves:
                        r.pe_turn(pe, h, 2 * i + h, xo[:, h], xo_ready, 2 * i + (h + 1), banks[h][0])
                    for h in halves:
                        r.pe_logits(pe, h, 2 * i + h, banks[h][1])
                    for h in halves:
                        r.pe_rank(pe, h, 2 * i + h, banks[h][1])


def finish(nc, x2_d, y_d, gaps, slots, out):
    with ExitStack() as c:
        fresh = Semaphores(c, nc)
        sem = lambda n: fresh("z_" + n)
        x2 = c.enter_context(nc.sbuf_tensor("z_x2", [P, 2, NT, D], F32))
        x_in, out_done = ([sem(n + "0"), sem(n + "1")] for n in ("x_in", "out_done"))
        dve_own, dve_ticks, sp_ticks = sem("dve_own"), sem("dve_ticks"), sem("sp_ticks")
        q = Gather(c, nc, fresh, "z_q", y_d, gaps, slots, 2)
        q.ticks_dve = dve_ticks
        halves = (0, 1)

        with nc.Block() as block:
            @block.sync
            def _(sp):
                def load(b, h):
                    sp.dma_start(x2[:, h], x2_d[b].rearrange("(t p) d -> p t d", p=P)).then_inc(x_in[h], 16)

                def store(b, h, nth):
                    gate(sp, q.taken, b + 3, sp_ticks)
                    sp.dma_start(out[b].rearrange("(t p) d -> p t d", p=P), x2[:, h]).then_inc(out_done[h], 16)
                    gate(sp, out_done[h], nth, sp_ticks)

                for h in halves:
                    load(h, h)
                with sp.Fori(0, PAIRS - 1) as i:
                    for h in halves:
                        store(2 * i + h, h, 16 * i + 16)
                        load(2 * i + (h + 2), h)
                for h in halves:
                    store(B - 2 + h, h, 16 * PAIRS)

            @block.gpsimd
            def _(pool):
                with pool.Fori(0, PAIRS) as i:
                    for h in halves:
                        q.pool_bring(pool, h, 2 * i + h)

            @block.scalar
            def _(act):
                q.act_start(act)

            @block.vector
            def _(dve):
                dve.sem_inc(q.ix_own, 1)
                q.dve_start(dve, Own(dve, q.ix_own, 0, 3))
                dve.sem_inc(dve_own, 1)
                with dve.Fori(0, PAIRS) as i:
                    own = Own(dve, dve_own, i, 2 * 2 * NT)
                    for h in halves:
                        gate(dve, x_in[h], 16 * i + 16, dve_ticks)
                        q.dve_add(dve, own, h, i, 2 * i + h, x2[:, h])
                    own.end()


def build(nc, x, adj, wqkv, bqkv, wo, bo, g1, c1, w1, b1, w2, b2, g2, c2, gate0_w, gate0_b, pack0,
          rel_w, rel_b, gate1_w, gate1_b, pack1, out):
    dram = lambda n, s, d=F32: nc.dram_tensor(n, s, d, kind="Internal").ap()
    xn_d, x1_d, x2_d = (dram(n, (B, N, D)) for n in ("xn_d", "x1_d", "x2_d"))
    qk_d = dram("qk_d", (B, P, 2, 2, N))
    v_d = dram("v_d", (B, P, NT, HEADS, 32))
    adjT_d, neg_d = dram("adjT_d", (B, P, NT, N), BF16), dram("neg_d", (B, P, NT, N), BF16)
    ctx_d = dram("ctx_d", (UNITS, P, N))
    xs_d = [dram(f"xs{k}_d", (ROWS, D)) for k in range(2)]
    y_d = [dram(f"y{k}_d", (MOE_TILES * TILE, D)) for k in range(2)]
    split_d = [dram(f"split{k}_d", (E_, P, 4 * hc * P + hc + 1)) for k, hc in enumerate((2, 4))]
    with ExitStack() as c:
        sb = lambda n, s, d: c.enter_context(nc.sbuf_tensor(n, s, d))
        identf, identb = sb("identf", [P, P], F32), sb("identb", [P, P], BF16)
        base = [sb(f"base{k}", [P, E_], F32) for k in range(2)]
        gaps = [sb(f"gaps{k}", [P, B * NT, E_], F32) for k in range(2)]
        slots = [sb(f"slots{k}", [P, B * 2 * NT], I32) for k in range(2)]
        made = c.enter_context(nc.semaphore("made"))
        with nc.Block() as block:
            @block.gpsimd
            def _(pool):
                nc.gpsimd.memset(identf[:], 0.0).then_inc(made, 1)
                nc.gpsimd.memset(identb[:], 0.0).then_inc(made, 1)
                pool.wait_ge(made, 2)
                for m in (identf, identb):
                    nc.gpsimd.affine_select(out=m[:], in_=m[:], compare_op=ALU.not_equal, fill=1.0,
                                            base=0, pattern=[[-1, P]], channel_multiplier=1).then_inc(made, 1)
                pool.wait_ge(made, 4)
        prepare(nc, x, adj, wqkv, bqkv, identf, identb, xn_d, qk_d, v_d, adjT_d, neg_d)
        attend(nc, identf, identb, qk_d, v_d, neg_d, ctx_d, ((pack0, split_d[0], 2), (pack1, split_d[1], 4)))
        after_attention(nc, x, xn_d, ctx_d, wo, bo, g1, c1, w1, b1, w2, b2, g2, c2, identf,
                        (gate0_w, gate0_b, xs_d[0]), x1_d, base[0], gaps[0], slots[0])
        experts(nc, "e0_", 2, ACT.Gelu, base[0], xs_d[0], split_d[0], y_d[0], slots[0], identf)
        relations(nc, x1_d, adjT_d, y_d[0], rel_w, rel_b, identf, (gate1_w, gate1_b, xs_d[1]), x2_d, base[1], gaps, slots)
        experts(nc, "e1_", 4, ACT.Relu, base[1], xs_d[1], split_d[1], y_d[1], slots[1], identf)
        finish(nc, x2_d, y_d[1], gaps[1], slots[1], out)


def kernel(**inputs):
    import numpy as np
    import concourse.bacc as bacc
    from concourse.bass_utils import run_bass_kernel_spmd

    a = {k: np.asarray(v) for k, v in inputs.items()}

    def pack(w1, b1, w2, b2):
        e, d, h = w1.shape
        c = h // P
        return np.concatenate([w1, w2.reshape(e, c, P, d).transpose(0, 2, 1, 3).reshape(e, P, h),
                               b1.reshape(e, c, P).transpose(0, 2, 1), b2[:, :, None]], axis=-1)

    arrays = {
        "x": a["x"], "adj": a["adj"],
        "wqkv": a["L0_gnn_Wqkv"].T, "bqkv": a["L0_gnn_bqkv"], "wo": a["L0_gnn_Wo"].T, "bo": a["L0_gnn_bo"],
        "g1": a["L0_gnn_ln1_g"], "c1": a["L0_gnn_ln1_b"], "w1": a["L0_gnn_W1"].T, "b1": a["L0_gnn_b1"],
        "w2": a["L0_gnn_W2"].T.reshape(4, P, D).transpose(1, 0, 2), "b2": a["L0_gnn_b2"],
        "g2": a["L0_gnn_ln2_g"], "c2": a["L0_gnn_ln2_b"],
        "gate0_w": a["L0_ffn_gate_w"], "gate0_b": a["L0_ffn_gate_b"],
        "pack0": pack(a["L0_ffn_W1"], a["L0_ffn_b1"], a["L0_ffn_W2"], a["L0_ffn_b2"]),
        "rel_w": a["L1_gnn_weight"], "rel_b": a["L1_gnn_bias"],
        "gate1_w": a["L1_ffn_Wg"].T, "gate1_b": a["L1_ffn_bg"],
        "pack1": pack(a["L1_ffn_W1"].transpose(0, 2, 1), a["L1_ffn_b1"], a["L1_ffn_W2"].transpose(0, 2, 1), a["L1_ffn_b2"]),
    }
    nc = bacc.Bacc("TRN2", target_bir_lowering=False, num_devices=1)
    given, args = {}, []
    for name, v in arrays.items():
        given[name] = np.ascontiguousarray(v)
        args.append(nc.dram_tensor(name, v.shape, mybir.dt.from_np(v.dtype), kind="ExternalInput").ap())
    out = nc.dram_tensor("out", (B, N, D), F32, kind="ExternalOutput").ap()
    build(nc, *args, out)
    result = run_bass_kernel_spmd(nc, [given], core_ids=[0])
    return result.results[0]["out"]
```

```python
from contextlib import ExitStack

import concourse.bass as bass
from concourse import mybir

F32 = mybir.dt.float32
F32R = mybir.dt.float32r
BF16 = mybir.dt.bfloat16
I32 = mybir.dt.int32
U32 = mybir.dt.uint32
ALU = mybir.AluOpType
ACT = mybir.ActivationFunctionType
AX = mybir.AxisListType

P = 128
B, N, D = 16, 512, 128
NT = N // P
HEADS, HD = 8, 16
GROUPS, GH = 2, 4
NEG = -1.0e30
EPS = 1e-5
PAIRS = B // 2
AHEAD = 4


class Semaphores:

    def __init__(self, c, nc):
        self.nc, self.all = nc, []
        c.callback(self.clear)

    def clear(self):
        self.nc.clear_and_free_semaphores(self.all)
        self.nc.all_engine_barrier()

    def __call__(self, name):
        self.all.append(self.nc.alloc_semaphore(name))
        return self.all[-1]


class Own:

    def __init__(self, eng, sem, turn, per, before=0, here=None):
        self.eng, self.sem, self.k = eng, sem, 0
        self.turn, self.per, self.before = turn, per, before
        self.here = per if here is None else here
        self.last = (sem, turn * per + (before + 1))

    def wait(self):
        self.eng.wait_ge(*self.last)

    def done(self, ins):
        self.k += 1
        self.last = (self.sem, self.turn * self.per + (self.before + self.k + 1))
        ins.then_inc(self.sem, 1)

    def tell(self, ins, sem, value):
        self.last = (sem, value)
        ins.then_inc(sem, 1)

    def end(self):
        assert self.k == self.here, (self.k, self.here)


def bcast_rows(ap, n):
    return ap.partition_broadcast(n)


def gate(eng, sem, value, ticks):
    eng.wait_ge(sem, value)
    eng.sem_inc(ticks, 1)


class Norm:

    def __init__(self, c, nc, fresh, name, ways):
        sb = lambda n, s, d: c.enter_context(nc.sbuf_tensor(name + n, s, d))
        sem = lambda n: fresh(name + n)
        self.nc, self.ways = nc, ways
        self.stats = sb("stats", [P, ways, NT, 6], F32)
        self.mv = sb("mv", [P, ways, NT, 2], F32)
        self.std = sb("std", [P, ways, NT], F32)
        self.r = sb("r", [P, ways, NT], F32)
        self.s = sb("s", [P, ways, NT], F32)
        self.minus = sb("minus", [P, ways, NT], F32)
        self.var_ready, self.std_ready, self.ready = sem("var_ready"), sem("std_ready"), sem("ready")

    def stats_of(self, own, src, h):
        own.wait()
        for t in range(NT):
            own.done(self.nc.vector.bn_stats(self.stats[:, h, t], src[:, t]))

    def variance(self, dve, own, nth, ticks, hs):
        gate(dve, *own.last, ticks)
        for h in hs:
            for t in range(NT):
                ins = self.nc.vector.bn_aggr(self.mv[:, h, t], self.stats[:, h, t])
                own.done(ins) if (h, t) != (hs[-1], NT - 1) else own.tell(ins, self.var_ready, nth + 1)

    def root(self, act, nth, eps, hs):
        act.wait_ge(self.var_ready, nth + 1)
        at = slice(hs[0], hs[-1] + 1)
        self.nc.scalar.activation(self.std[:, at], self.mv[:, at, :, 1], ACT.Sqrt, bias=eps[:], scale=1.0).then_inc(self.std_ready, 1)

    def inverse(self, dve, own, nth, hs, shift=False):
        at = slice(hs[0], hs[-1] + 1)
        v, r, s = self.nc.vector, self.r[:, at], self.s[:, at]
        dve.wait_ge(self.std_ready, nth + 1)
        own.done(v.reciprocal(r, self.std[:, at]))
        own.wait()
        own.done(v.tensor_tensor(s, r, r, ALU.mult))
        own.wait()
        own.done(v.scalar_tensor_tensor(out=s, in0=self.mv[:, at, :, 1], scalar=EPS, in1=s, op0=ALU.add, op1=ALU.mult))
        own.wait()
        own.done(v.tensor_scalar(s, s, -0.5, 1.5, ALU.mult, ALU.add))
        own.wait()
        own.done(v.tensor_tensor(r, r, s, ALU.mult))
        if shift:
            own.wait()
            own.tell(v.scalar_tensor_tensor(out=self.minus[:, at], in0=self.mv[:, at, :, 0], scalar=-1.0, in1=r, op0=ALU.mult, op1=ALU.mult), self.ready, nth + 1)

    def apply(self, own, src, dst, h, last=None):
        own.wait()
        for t in range(NT):
            ins = self.nc.vector.tensor_scalar(dst[:, t], src[:, t], self.mv[:, h, t, 0:1], self.r[:, h, t:t + 1], ALU.subtract, ALU.mult)
            own.tell(ins, *last) if last and t == NT - 1 else own.done(ins)

    def scaled(self, own, src, dst, h, gain, plus, last):
        own.wait()
        for t in range(NT):
            own.done(self.nc.vector.scalar_tensor_tensor(out=dst[:, t], in0=src[:, t], scalar=self.mv[:, h, t, 0:1], in1=gain, op0=ALU.subtract, op1=ALU.mult))
        own.wait()
        for t in range(NT):
            ins = self.nc.vector.scalar_tensor_tensor(out=dst[:, t], in0=dst[:, t], scalar=self.r[:, h, t:t + 1], in1=plus(t), op0=ALU.mult, op1=ALU.add)
            own.tell(ins, *last) if t == NT - 1 else own.done(ins)

    def act_apply(self, act, nth, src, dst, h, done):
        act.wait_ge(self.ready, nth + 1)
        for t in range(NT):
            ins = self.nc.scalar.activation(dst[:, t], src[:, t], ACT.Identity, bias=self.minus[:, h, t:t + 1], scale=self.r[:, h, t:t + 1])
        ins.then_inc(done, 1)


def prepare(nc, x, adj, wqkv, bqkv, ident, identb, xn_d, qk_d, v_d, adjT_d, neg_d, many):
    with ExitStack() as c:
        sb = lambda n, s, d: c.enter_context(nc.sbuf_tensor("p_" + n, s, d))
        pb = lambda n, s, d: c.enter_context(nc.psum_tensor("p_" + n, s, d))
        fresh = Semaphores(c, nc)
        sem = lambda n: fresh("p_" + n)
        two = lambda n: [sem(n + "0"), sem(n + "1")]
        adj_i = sb("adj_i", [P, AHEAD, NT, N], I32)
        adj_b = sb("adj_b", [P, 2, NT, N], BF16)
        adjT = sb("adjT", [P, 2, NT, N], BF16)
        neg = sb("neg", [P, 2, NT, N], BF16)
        wT = sb("wT", [P, 3 * D], F32)
        bqk = sb("bqk", [P, 2], F32)
        bqk_s = sb("bqk_s", [P, 2], F32)
        bv = sb("bv", [P, D], F32)
        eps = sb("eps", [P, 1], F32)
        closed = sb("closed", [P, NT, N], BF16)
        x_raw = sb("x_raw", [P, AHEAD, NT, D], F32)
        xn = sb("xn", [P, 2, NT, D], F32)
        xT = sb("xT", [P, 2, N], F32)
        qk = sb("qk", [P, 2, 2, N], F32)
        parts = sb("parts", [P, 2, 2, 2, N], F32R)
        va = sb("va", [P, 2, NT, HEADS, 32], F32)
        kinds, kind, kind_row = sb("kinds", [P, B], F32), sb("kind", [P, 1], F32), sb("kind_row", [1, 1], F32)
        ps_x = pb("ps_x", [P, N], F32)
        ps_q = pb("ps_q", [P, N], F32)
        ps_k = pb("ps_k", [P, N], F32)
        ps_v = pb("ps_v", [P, N], F32)
        ps_a = [pb(f"ps_a{j}", [P, 1024], BF16) for j in range(NT)]

        weights_in = sem("weights_in")
        adj_in, x_in = ([sem(f"{n}{k}") for k in range(AHEAD)] for n in ("adj_in", "x_in"))
        adj_cast, adjT_ps, adjT_sb = sem("adj_cast"), sem("adjT_ps"), sem("adjT_sb")
        xn_ready = sem("xn")
        norm = Norm(c, nc, fresh, "p_n", 2)
        sp_ticks, pool_ticks, dve_ticks = sem("sp_ticks"), sem("pool_ticks"), sem("dve_ticks")
        xT_ps, xT_sb, qk_ps, qk_sb, v_ps, v_sb = (sem(n) for n in ("xT_ps", "xT_sb", "qk_ps", "qk_sb", "v_ps", "v_sb"))
        kind_ready, kind_ps, flag_own = sem("kind_ready"), sem("kind_ps"), sem("flag_own")
        parts_ready, neg_ready, consts = sem("parts"), sem("neg_ready"), sem("consts")
        parts_out, v_out, adjT_out, neg_out = two("parts_out"), two("v_out"), two("adjT_out"), two("neg_out")
        xn_out = two("xn_out")
        dve_own = sem("dve_own")

        with nc.Block() as block:
            @block.sync
            def _(sp):
                def load(b, k):
                    sp.dma_start(adj_i[:, k], adj[b].rearrange("(t p) m -> p t m", p=P)).then_inc(adj_in[k], 16)
                    sp.dma_start(x_raw[:, k], x[b].rearrange("(t p) d -> p t d", p=P)).then_inc(x_in[k], 16)

                def store(b, h):
                    gate(sp, xn_ready, b + 1, sp_ticks)
                    sp.dma_start(xn_d[b].rearrange("(t p) d -> p t d", p=P), xn[:, h]).then_inc(xn_out[h], 16)
                    gate(sp, v_sb, b + 2, sp_ticks)
                    sp.dma_start(v_d[b], va[:, h]).then_inc(v_out[h], 16)
                    gate(sp, parts_ready, b + 1, sp_ticks)
                    sp.dma_start(qk_d[b], parts[:, h].bitcast(F32)).then_inc(parts_out[h], 16)
                    gate(sp, adjT_sb, NT * (b + 2), sp_ticks)
                    sp.dma_start(adjT_d[b], adjT[:, h]).then_inc(adjT_out[h], 16)
                    gate(sp, neg_ready, b + 3, sp_ticks)
                    sp.dma_start(neg_d[b], neg[:, h]).then_inc(neg_out[h], 16)

                sp.dma_start(wT[:], wqkv).then_inc(weights_in, 16)
                sp.dma_start(bqk[:], bqkv[0:2 * D].rearrange("(a p) -> p a", p=P), allow_slow_non_contiguous=True).then_inc(weights_in, 16)
                sp.dma_start(bv[:], bcast_rows(bqkv[2 * D:3 * D], P)).then_inc(weights_in, 16)
                for k in range(AHEAD):
                    load(k, k)
                with sp.Fori(0, B // AHEAD - 1) as i:
                    for k in range(AHEAD):
                        b = AHEAD * i + k
                        gate(sp, adj_cast, b + 1, sp_ticks)
                        gate(sp, xn_ready, b + 1, sp_ticks)
                        load(AHEAD * i + (k + AHEAD), k)
                        store(b, k % 2)
                for k in range(AHEAD):
                    store(B - AHEAD + k, k % 2)
                for h in range(2):
                    for s in (xn_out, parts_out, v_out, adjT_out, neg_out):
                        sp.wait_ge(s[h], 16 * (PAIRS + 1))

            @block.gpsimd
            def _(pool):
                nc.gpsimd.memset(eps[:], EPS).then_inc(consts, 1)
                nc.gpsimd.memset(va[:], 0.0).then_inc(consts, 1)
                pool.wait_ge(consts, 2)
                nc.gpsimd.memset(va[:, :, :, :, HD:HD + 1], 1.0).then_inc(consts, 1)
                for h in range(2):
                    for s in (xn_out, parts_out, v_out, adjT_out, neg_out):
                        pool.sem_inc(s[h], 16)
                nc.gpsimd.memset(closed[:], NEG).then_inc(consts, 1)
                pool.wait_ge(consts, 4)
                nc.gpsimd.affine_select(out=closed[:], in_=closed[:], compare_op=ALU.not_equal, fill=0.0,
                                        base=0, pattern=[[P, NT], [-1, N]], channel_multiplier=1).then_inc(consts, 1)
                pool.sem_inc(neg_ready, 2)
                with pool.Fori(0, B // AHEAD) as q:
                    for s in range(AHEAD // 2):
                        i = (AHEAD // 2) * q + s
                        for h in range(2):
                            b = 2 * i + h
                            gate(pool, adj_in[2 * s + h], 16 * q + 16, pool_ticks)
                            gate(pool, neg_ready, b + 1, pool_ticks)
                            nc.gpsimd.tensor_scalar(adj_b[:, h], adj_i[:, 2 * s + h], 0.0, 5.0, ALU.max, ALU.min).then_inc(adj_cast, 1)

            @block.scalar
            def _(act):
                act.wait_ge(consts, 5)
                act.wait_ge(weights_in, 48)
                nc.scalar.mul(bqk_s[:, 0:1], bqk[:, 0:1], 0.25).then_inc(consts, 1)
                act.wait_ge(consts, 6)
                act.sem_inc(adjT_sb, NT)
                act.sem_inc(xT_sb, 1)
                act.sem_inc(qk_sb, 2)
                with act.Fori(0, B // AHEAD) as q:
                    for s in range(AHEAD // 2):
                        i = (AHEAD // 2) * q + s
                        norm.root(act, i, eps, (0, 1))
                        for h in range(2):
                            b = 2 * i + h
                            act.wait_ge(adjT_out[h], 16 * i + 16)
                            for j in range(NT):
                                act.wait_ge(adjT_ps, NT * (b + 1) + (j + 1))
                                nc.scalar.copy(adjT[:, h, j], ps_a[j][:, 0:N]).then_inc(adjT_sb, 1)
                            act.wait_ge(xT_ps, b + 1)
                            nc.scalar.copy(xT[:, h], ps_x[:]).then_inc(xT_sb, 1)
                            act.wait_ge(qk_ps, 2 * b + 1)
                            nc.scalar.activation(qk[:, h, 0], ps_q[:], ACT.Identity, bias=bqk_s[:, 0:1], scale=0.25).then_inc(qk_sb, 1)
                            act.wait_ge(qk_ps, 2 * b + 2)
                            nc.scalar.activation(qk[:, h, 1], ps_k[:], ACT.Identity, bias=bqk[:, 1:2], scale=1.0).then_inc(qk_sb, 1)

            @block.vector
            def _(dve):
                PER = 32
                dve.wait_ge(consts, 5)
                dve.wait_ge(weights_in, 48)
                dve.sem_inc(dve_own, 1)
                dve.sem_inc(v_sb, 1)
                with dve.Fori(0, B // AHEAD) as q:
                    for s in range(AHEAD // 2):
                        i = (AHEAD // 2) * q + s
                        own = Own(dve, dve_own, i, PER)
                        for h in range(2):
                            dve.wait_ge(x_in[2 * s + h], 16 * q + 16)
                            norm.stats_of(own, x_raw[:, 2 * s + h], h)
                        norm.variance(dve, own, i, dve_ticks, (0, 1))
                        norm.inverse(dve, own, i, (0, 1))
                        for h in range(2):
                            dve.wait_ge(xn_out[h], 16 * i + 16)
                            norm.apply(own, x_raw[:, 2 * s + h], xn[:, h], h, (xn_ready, 2 * i + (h + 1)))
                        for h in range(2):
                            b = 2 * i + h
                            dve.wait_ge(adjT_sb, NT * (b + 2))
                            dve.wait_ge(neg_out[h], 16 * i + 16)
                            own.wait()
                            own.done(nc.vector.tensor_reduce(kinds[:, bass.ds(AHEAD * q + (2 * s + h), 1)], adj_b[:, h].rearrange("p t m -> p (t m)"), AX.X, ALU.max))
                            own.done(nc.vector.tensor_tensor(neg[:, h], adj_b[:, h], adjT[:, h], ALU.max))
                            own.wait()
                            own.tell(nc.vector.scalar_tensor_tensor(
                                out=neg[:, h].rearrange("p t m -> p (t m)"), in0=neg[:, h].rearrange("p t m -> p (t m)"), scalar=0.0,
                                in1=closed[:].rearrange("p t m -> p (t m)"), op0=ALU.is_le, op1=ALU.mult), neg_ready, b + 3)
                            dve.wait_ge(v_ps, b + 1)
                            dve.wait_ge(v_out[h], 16 * i + 16)
                            own.wait()
                            own.tell(nc.vector.tensor_tensor(
                                va[:, h, :, :, 0:HD], ps_v[:].rearrange("p (t h d) -> p t h d", t=NT, h=HEADS),
                                bv[:].rearrange("p (o h d) -> p o h d", o=1, h=HEADS).broadcast_to([P, NT, HEADS, HD]), ALU.add), v_sb, b + 2)
                            dve.wait_ge(qk_sb, 2 * b + 4)
                            dve.wait_ge(parts_out[h], 16 * i + 16)
                            own.wait()
                            own.done(nc.vector.tensor_copy(parts[:, h, 0], qk[:, h]))
                            own.wait()
                            own.tell(nc.vector.tensor_tensor(parts[:, h, 1], qk[:, h], parts[:, h, 0].bitcast(F32), ALU.subtract), parts_ready, b + 1)
                        own.end()
                flag = Own(dve, flag_own, 0, 2)
                dve.sem_inc(flag_own, 1)
                flag.tell(nc.vector.tensor_reduce(kind[:], kinds[:], AX.X, ALU.max), kind_ready, 1)
                dve.wait_ge(kind_ps, 1)
                flag.done(nc.vector.tensor_reduce(kind_row[:], ps_x[0:1, 0:P], AX.X, ALU.max))
                flag.wait()
                flag.done(nc.vector.tensor_scalar(many[0:1, 0:1], kind_row[:], 1.0, None, ALU.is_gt))
                flag.end()

            @block.tensor
            def _(pe):
                pe.wait_ge(weights_in, 48)
                pe.sem_inc(adjT_ps, NT)
                with pe.Fori(0, B // AHEAD) as q:
                    for s in range(AHEAD // 2):
                        i = (AHEAD // 2) * q + s
                        for h in range(2):
                            b = 2 * i + h
                            pe.wait_ge(adj_cast, b + 1)
                            for j in range(NT):
                                pe.wait_ge(adjT_sb, NT * b + (j + 1))
                                for t in range(NT):
                                    mm = nc.tensor.transpose(ps_a[j][:, t * P:(t + 1) * P], adj_b[:, h, t, j * P:(j + 1) * P], identb[:])
                                mm.then_inc(adjT_ps, 1)
                            pe.wait_ge(xn_ready, b + 1)
                            pe.wait_ge(xT_sb, b + 1)
                            for t in range(NT):
                                mm = nc.tensor.transpose(ps_x[:, t * P:(t + 1) * P], xn[:, h, t], ident[:])
                            mm.then_inc(xT_ps, 1)
                            pe.wait_ge(xT_sb, b + 2)
                            pe.wait_ge(qk_sb, 2 * b + 1)
                            nc.tensor.matmul(ps_q[:], wT[:, 0:D], xT[:, h], start=True, stop=True).then_inc(qk_ps, 1)
                            pe.wait_ge(qk_sb, 2 * b + 2)
                            nc.tensor.matmul(ps_k[:], wT[:, D:2 * D], xT[:, h], start=True, stop=True).then_inc(qk_ps, 1)
                            pe.wait_ge(v_sb, b + 1)
                            for t in range(NT):
                                mm = nc.tensor.matmul(ps_v[:, t * P:(t + 1) * P], xT[:, h, t * P:(t + 1) * P], wT[:, 2 * D:3 * D], start=True, stop=True)
                            mm.then_inc(v_ps, 1)
                pe.wait_ge(kind_ready, 1)
                pe.wait_ge(xT_sb, B + 1)
                nc.tensor.transpose(ps_x[0:1, 0:P], kind[:], ident[:]).then_inc(kind_ps, 1)


UNITS = B * GROUPS
LOADS = 9
TILES = NT * GH


def attend(nc, identf, identb, qk_d, v_d, neg_d, ctx_d, packs):
    with ExitStack() as c:
        sb = lambda n, s, d: c.enter_context(nc.sbuf_tensor("a_" + n, s, d))
        pb = lambda n, s, d: c.enter_context(nc.psum_tensor("a_" + n, s, d))
        fresh = Semaphores(c, nc)
        sem = lambda n: fresh("a_" + n)
        many = lambda n: [sem(f"{n}{k}") for k in range(AHEAD)]
        SHIFT = 3 * HD
        qs = [sb(f"qs{k}", [P, GH, N], F32R) for k in range(AHEAD)]
        ks = [sb(f"ks{k}", [P, GH, N], F32R) for k in range(AHEAD)]
        nm = sb("nm", [P, AHEAD, NT, N], BF16)
        va = sb("va", [P, AHEAD, NT, GH, 32], F32)
        rows = sb("rows", [1, 2, GH * N], F32)
        junk = sb("junk", [P, 4, N], BF16)
        mx = sb("mx", [P, 2, TILES], F32)
        nmx = sb("nmx", [TILES, 2, P], F32R)
        pt = sb("pt", [P, 8, N], F32)
        ctx = sb("ctx", [P, 2, N], F32)
        WIDE = 2 * P * max(hc for _, _, hc in packs)
        w_raw, w_high, w_low = sb("w_raw", [P, WIDE + 8], F32), sb("w_high", [P, WIDE], F32R), sb("w_low", [P, WIDE], F32R)
        nothing = sb("nothing", [P, WIDE], F32)
        w_zeros, w_came, w_split, w_gone, w_ticks = (sem(n) for n in ("w_zeros", "w_came", "w_split", "w_gone", "w_ticks"))
        s1 = [pb(f"s1_{k}", [P, N], F32) for k in range(2)]
        s2 = [pb(f"s2_{k}", [P, N], F32) for k in range(GH)]
        ps_c = pb("ps_c", [P, N], F32)
        ps_m = pb("ps_m", [P, N], F32)
        unit_in, shift_in = many("unit_in"), many("shift_in")
        ctx_out = [sem("ctx_out0"), sem("ctx_out1")]
        consts, s1_ps, max_done, mxT_ps, nmx_ready = (sem(n) for n in ("consts", "s1_ps", "max_done", "mxT_ps", "nmx_ready"))
        s2_ps, exp_done, pv_done, ctx_sb = (sem(n) for n in ("s2_ps", "exp_done", "pv_done", "ctx_sb"))
        sp_ticks, dve_ticks, q_zeros, k_zeros = (sem(n) for n in ("sp_ticks", "dve_ticks", "q_zeros", "k_zeros"))

        with nc.Block() as block:
            @block.sync
            def _(sp):
                def load(b, g, k, turn):
                    heads = slice(g * GH, (g + 1) * GH)
                    if turn is not None:
                        gate(sp, ctx_sb, turn, sp_ticks)
                    src = qk_d[b].rearrange("(h d) a q n -> d h a q n", d=HD)
                    for s, (qpart, kpart) in enumerate(((0, 0), (0, 1), (1, 0))):
                        at = slice(s * HD, (s + 1) * HD)
                        sp.dma_start(qs[k][at].bitcast(F32), src[:, heads, qpart, 0]).then_inc(unit_in[k], 16)
                        sp.dma_start(ks[k][at].bitcast(F32), src[:, heads, kpart, 1]).then_inc(unit_in[k], 16)
                    sp.dma_start(qs[k][SHIFT:SHIFT + 1].bitcast(F32).rearrange("p h n -> p (h n)"), rows[:, 0]).then_inc(unit_in[k], 16)
                    sp.dma_start(nm[:, k], neg_d[b]).then_inc(unit_in[k], 16)
                    sp.dma_start(va[:, k], v_d[b][:, :, heads]).then_inc(unit_in[k], 16)

                def shift(u, k):
                    gate(sp, nmx_ready, u + 1, sp_ticks)
                    sp.dma_start(qs[k][SHIFT:SHIFT + 1].bitcast(F32).rearrange("o h n -> o (h n)"), nmx[:, k % 2].bitcast(F32)).then_inc(shift_in[k], 16)

                def store(u, k):
                    gate(sp, ctx_sb, u + 2, sp_ticks)
                    sp.dma_start(ctx_d[u], ctx[:, k % 2]).then_inc(ctx_out[k % 2], 16)

                sp.wait_ge(consts, 2)
                for k in range(AHEAD):
                    sp.wait_ge(q_zeros, k + 1)
                    sp.wait_ge(k_zeros, k + 1)
                    sp.dma_start(ks[k][SHIFT:SHIFT + 1].bitcast(F32).rearrange("p h n -> p (h n)"), rows[:, 1]).then_inc(unit_in[k], 16)
                    if k < 3:
                        load(k // 2, k % 2, k, None)
                shift(0, 0)
                shift(1, 1)
                with sp.Fori(0, PAIRS - 1) as i:
                    for w in range(4):
                        load(2 * i + (w + 3) // 2, (w + 3) % 2, (w + 3) % 4, 4 * i + w + 1)
                        shift(4 * i + (w + 2), (w + 2) % 4)
                        store(4 * i + w, w)
                u = UNITS - 4
                for w in range(4):
                    if w == 0:
                        load(B - 1, 1, 3, u + 1)
                    if w < 2:
                        shift(u + w + 2, w + 2)
                    store(u + w, w)
                for k in range(2):
                    sp.wait_ge(ctx_out[k], 16 * (UNITS // 2 + 1))

            @block.gpsimd
            def _(pool):
                nc.gpsimd.memset(rows[:, 0], 0.0).then_inc(consts, 1)
                nc.gpsimd.memset(rows[:, 1], 1.0).then_inc(consts, 1)
                for k in range(AHEAD):
                    nc.gpsimd.memset(qs[k][:].bitcast(F32), 0.0).then_inc(q_zeros, 1)
                nc.gpsimd.memset(nothing[:], 0.0).then_inc(w_zeros, 1)
                pool.wait_ge(w_zeros, 1)
                for n, (given, parts, hc) in enumerate(packs):
                    split_weights(pool, nc, w_raw, w_high, w_low, nothing, given, parts, w_came, w_split, (w_gone, w_ticks), hc, E_ * n)

            @block.scalar
            def _(act):
                def unit(i, w, last):
                    u = 4 * i + w
                    for kt in range(NT):
                        act.wait_ge(pv_done, 4 * u + (kt + 1))
                        for hh in range(GH):
                            m = 16 * u + (kt * GH + hh)
                            act.wait_ge(s2_ps, m + 1)
                            nc.scalar.activation(pt[:, (kt * GH + hh) % 8], s2[hh][:], ACT.Exp).then_inc(exp_done, 1)
                    if not last:
                        negated(u + 2, w % 2, i, w)

                def negated(u, k, i, w):
                    act.wait_ge(mxT_ps, u + 1)
                    act.wait_ge(shift_in[w], 16 * i + 32)
                    nc.scalar.activation(nmx[:, k], ps_m[0:TILES, 0:P], ACT.Copy, scale=-1.0).then_inc(nmx_ready, 1)

                act.sem_inc(exp_done, 4)
                for k in range(AHEAD):
                    act.sem_inc(shift_in[k], 16)
                for k in range(2):
                    act.wait_ge(mxT_ps, k + 1)
                    nc.scalar.activation(nmx[:, k], ps_m[0:TILES, 0:P], ACT.Copy, scale=-1.0).then_inc(nmx_ready, 1)
                with act.Fori(0, PAIRS - 1) as i:
                    for w in range(4):
                        unit(i, w, False)
                for w in range(4):
                    unit(PAIRS - 1, w, w >= 2)

            @block.vector
            def _(dve):
                def maxima(u, k, nth):
                    gate(dve, unit_in[k], nth, dve_ticks)
                    for j in range(TILES):
                        qt, hh = divmod(j, GH)
                        n = 16 * u + j
                        gate(dve, max_done, n + 1, dve_ticks)
                        gate(dve, s1_ps, n + 1, dve_ticks)
                        nc.vector.tensor_tensor_reduce(
                            out=junk[:, j % 4], in0=s1[j % 2][:], in1=nm[:, k, qt], scale=1.0, scalar=-3.0e38,
                            op0=ALU.add, op1=ALU.max, accum_out=mx[:, k % 2, hh * NT + qt:hh * NT + qt + 1]).then_inc(max_done, 1)

                def result(u, w, turn):
                    gate(dve, pv_done, 4 * u + 6, dve_ticks)
                    gate(dve, ctx_out[w % 2], turn, dve_ticks)
                    nc.vector.tensor_copy(ctx[:, w % 2], ps_c[:]).then_inc(ctx_sb, 1)

                for k in range(AHEAD):
                    nc.vector.memset(ks[k][:].bitcast(F32), 0.0).then_inc(k_zeros, 1)
                dve.sem_inc(max_done, 4)
                dve.sem_inc(ctx_sb, 1)
                for k in range(2):
                    dve.sem_inc(ctx_out[k], 16)
                for k in range(2):
                    maxima(k, k, 16 * (LOADS + 1))
                with dve.Fori(0, PAIRS - 1) as i:
                    for w in range(4):
                        maxima(4 * i + (w + 2), (w + 2) % 4, 16 * LOADS * i + 16 * (LOADS * (2 if w >= 2 else 1) + 1))
                        result(4 * i + w, w, 32 * i + 16 * (w // 2 + 1))
                i = PAIRS - 1
                for w in range(4):
                    if w < 2:
                        maxima(4 * i + w + 2, w + 2, 16 * (LOADS * (i + 1) + 1))
                    result(4 * i + w, w, 32 * i + 16 * (w // 2 + 1))

            @block.tensor
            def _(pe):
                def by_query(u, k, j):
                    qt, hh = divmod(j, GH)
                    pe.wait_ge(max_done, 16 * u + (j + 3))
                    nc.tensor.matmul(s1[j % 2][:], qs[k][:, hh, qt * P:(qt + 1) * P], ks[k][:, hh], start=True, stop=True).then_inc(s1_ps, 1)

                def maxima_turned(u, k):
                    pe.wait_ge(max_done, 16 * u + 20)
                    pe.wait_ge(nmx_ready, u)
                    nc.tensor.transpose(ps_m[0:TILES, 0:P], mx[:, k % 2], identf[:]).then_inc(mxT_ps, 1)

                def by_key(u, k, kt, hh):
                    pe.wait_ge(exp_done, 16 * u + (kt * GH + hh + 1))
                    nc.tensor.matmul(s2[hh][:], ks[k][:, hh, kt * P:(kt + 1) * P], qs[k][:, hh], start=True, stop=False)
                    nc.tensor.matmul(s2[hh][:], identb[:], nm[:, k, kt], start=False, stop=True).then_inc(s2_ps, 1)

                def values(u, k, kt, hh):
                    if (kt, hh) == (0, 0):
                        pe.wait_ge(ctx_sb, u + 1)
                    pe.wait_ge(exp_done, 16 * u + (kt * GH + hh + 5))
                    mm = nc.tensor.matmul(ps_c[32 * hh:32 * hh + 32, :], va[:, k, kt, hh], pt[:, (kt * GH + hh) % 8],
                                          start=(kt == 0), stop=(kt == NT - 1))
                    if hh == GH - 1:
                        mm.then_inc(pv_done, 1)

                def unit(i, w, last, nth):
                    u, k = 4 * i + w, (w + 2) % 4
                    pe.wait_ge(shift_in[w], 16 * i + 32)
                    if not last:
                        pe.wait_ge(unit_in[k], nth)
                    for kt in range(NT):
                        for hh in range(GH):
                            by_key(u, w, kt, hh)
                            if not last:
                                by_query(u + 2, k, kt * GH + hh)
                        if kt >= 1:
                            for hh in range(GH):
                                values(u, w, kt - 1, hh)
                    if not last:
                        maxima_turned(u + 2, k)
                    for hh in range(GH):
                        values(u, w, NT - 1, hh)

                pe.sem_inc(pv_done, 2)
                for u in range(2):
                    pe.wait_ge(unit_in[u], 16 * (LOADS + 1))
                    for j in range(TILES):
                        by_query(u, u, j)
                    pe.wait_ge(max_done, 16 * u + 20)
                    if u > 0:
                        pe.wait_ge(nmx_ready, u)
                    nc.tensor.transpose(ps_m[0:TILES, 0:P], mx[:, u], identf[:]).then_inc(mxT_ps, 1)
                with pe.Fori(0, PAIRS - 1) as i:
                    for w in range(4):
                        unit(i, w, False, 16 * LOADS * i + 16 * (LOADS * (2 if w >= 2 else 1) + 1))
                for w in range(4):
                    unit(PAIRS - 1, w, w >= 2, 16 * (LOADS * PAIRS + 1))


E_ = 8
TILE = 512
CAP = B * N + TILE
ROWS = E_ * CAP + 2 * TILE
LAST = ROWS - TILE
MOE_TILES = 2 * B * N // TILE + E_
TAGGED = D + 2
RESULTS = 2 * B * N


def wide(ap, shape):
    return ap.rearrange("p (o d) -> p o d", o=1).broadcast_to(shape)


class Router:

    def __init__(self, c, nc, fresh, name, ways, gate_w, gate_b, xs_d, identf):
        sb = lambda n, s, d: c.enter_context(nc.sbuf_tensor(name + n, s, d))
        sem = lambda n: fresh(name + n)
        self.nc, self.ways, self.gate_w, self.gate_b, self.xs_d, self.identf = nc, ways, gate_w, gate_b, xs_d, identf
        self.gw = sb("gw", [P, E_], F32)
        self.gb = sb("gb", [P, E_], F32)
        self.xT = sb("xT", [P, ways, N], F32)
        self.lg = sb("lg", [P, ways, NT, E_], F32)
        self.top = sb("top", [P, ways, NT, E_], F32)
        self.ix = sb("ix", [P, ways, NT, E_], U32)
        self.ixf = sb("ixf", [P, ways, 2, NT], F32)
        self.iota = sb("iota", [P, E_], F32)
        self.iota_i = sb("iota_i", [P, E_], I32)
        self.hot = sb("hot", [P, ways, 2, NT, E_], F32)
        self.both = sb("both", [P, ways, NT, E_], BF16)
        self.pos = sb("pos", [P, ways, NT, E_], F32)
        self.pick = sb("pick", [P, ways, 2, NT, E_], F32)
        self.slot = sb("slot", [P, ways, 2, NT], F32)
        self.slot_i = sb("slot_i", [P, ways, 2, NT], I32)
        self.token_i = sb("token_i", [P, ways, NT], I32)
        self.token = sb("token", [P, ways, NT], F32)
        self.before = sb("before", [P, P], BF16)
        self.ones = sb("ones", [P, P], BF16)
        self.consts, self.gxT_ps, self.gxT_sb = sem("consts"), sem("gxT_ps"), sem("gxT_sb")
        self.lg_ps, self.chosen, self.rank_ps, self.slots = sem("lg_ps"), sem("chosen"), sem("rank_ps"), sem("slots")
        self.sent, self.gone, self.ticks = sem("sent"), sem("gone"), sem("ticks")

    def load(self, sp, done):
        sp.dma_start(self.gw[:], self.gate_w).then_inc(done, 16)
        sp.dma_start(self.gb[:], bcast_rows(self.gate_b, P)).then_inc(done, 16)

    def pool_start(self, pool, base):
        nc = self.nc
        nc.gpsimd.memset(self.ones[:], 1.0).then_inc(self.consts, 1)
        nc.gpsimd.memset(self.before[:], 1.0).then_inc(self.consts, 1)
        nc.gpsimd.iota(self.iota_i[:], pattern=[[1, E_]], base=0, channel_multiplier=0).then_inc(self.consts, 1)
        nc.gpsimd.iota(self.token_i[:], pattern=[[N, self.ways], [P, NT]], base=1, channel_multiplier=1).then_inc(self.consts, 1)
        pool.wait_ge(self.consts, 4)
        nc.gpsimd.affine_select(out=self.before[:], in_=self.before[:], compare_op=ALU.is_gt, fill=0.0,
                                base=0, pattern=[[1, P]], channel_multiplier=-1).then_inc(self.consts, 1)
        nc.gpsimd.tensor_copy(self.iota[:], self.iota_i[:]).then_inc(self.consts, 1)
        nc.gpsimd.tensor_copy(self.token[:], self.token_i[:]).then_inc(self.consts, 1)
        pool.wait_ge(self.consts, 7)
        nc.gpsimd.tensor_scalar(base[:], self.iota[:], float(CAP), None, ALU.mult).then_inc(self.consts, 1)
        pool.sem_inc(self.gone, self.ways)

    def pool_send(self, pool, h, b, rows):
        gate(pool, self.slots, b + (self.ways + 1), self.ticks)
        for k in range(2):
            for t in range(NT):
                self.nc.gpsimd.indirect_dma_start(
                    self.xs_d, bass.IndirectOffsetOnAxis(self.slot_i[:, h, k, t:t + 1], 0), rows[:, t], None).then_inc(self.sent, 16)

    def pool_sent(self, pool, b):
        gate(pool, self.sent, 16 * 2 * NT * (b + 1), self.ticks)
        pool.sem_inc(self.gone, 2)

    def pe_turn(self, pe, h, b, rows, ready, value, ps):
        pe.wait_ge(ready, value)
        for t in range(NT):
            mm = self.nc.tensor.transpose(ps[:, t * P:(t + 1) * P], rows[:, t], self.identf[:])
        mm.then_inc(self.gxT_ps, 1)

    def act_turn(self, act, h, b, ps):
        act.wait_ge(self.gxT_ps, b + 1)
        self.nc.scalar.copy(self.xT[:, h], ps[:]).then_inc(self.gxT_sb, 1)

    def pe_logits(self, pe, h, b, ps):
        pe.wait_ge(self.gxT_sb, b + 1)
        for t in range(NT):
            mm = self.nc.tensor.matmul(ps[:, t * E_:(t + 1) * E_], self.xT[:, h, t * P:(t + 1) * P], self.gw[:], start=True, stop=True)
        mm.then_inc(self.lg_ps, 1)

    def dve_choose(self, dve, own, pair, ps, gaps_out):
        nc, hs = self.nc, pair.hs
        gate(dve, self.lg_ps, pair.graph(hs[1], 1), self.ticks_dve)
        own.wait()
        for h in hs:
            own.done(nc.vector.tensor_tensor(self.lg[:, h], ps(h)[:, 0:NT * E_].rearrange("p (t e) -> p t e", t=NT), wide(self.gb[:], [P, NT, E_]), ALU.add))
        gate(dve, *own.last, self.ticks_dve)
        for h in hs:
            for t in range(NT):
                own.done(nc.vector.max(self.top[:, h, t], self.lg[:, h, t]))
        gate(dve, *own.last, self.ticks_dve)
        for h in hs:
            for t in range(NT):
                own.done(nc.vector.max_index(self.ix[:, h, t], self.top[:, h, t], self.lg[:, h, t]))
        own.wait()
        for h in hs:
            own.done(nc.vector.tensor_copy(self.ixf[:, h], self.ix[:, h, :, 0:2].rearrange("p t k -> p k t")))
        own.wait()
        for h in hs:
            for k in range(2):
                own.done(nc.vector.tensor_tensor(self.hot[:, h, k], wide(self.iota[:], [P, NT, E_]),
                                                 self.ixf[:, h, k].rearrange("p (t o) -> p t o", o=1).broadcast_to([P, NT, E_]), ALU.is_equal))
        own.wait()
        for h in hs:
            own.tell(nc.vector.tensor_tensor(self.both[:, h], self.hot[:, h, 0], self.hot[:, h, 1], ALU.add), self.chosen, pair.graph(h, 1))
        for h in hs:
            own.done(nc.vector.tensor_tensor(gaps_out(h), self.top[:, h], self.top[:, h, :, 0:1].broadcast_to([P, NT, E_]), ALU.subtract))

    def pe_rank(self, pe, h, b, ps, after=0):
        pe.wait_ge(self.chosen, b + (after + 1))
        at = NT * E_
        for t in range(NT):
            for s in range(t + 1):
                self.nc.tensor.matmul(ps[:, at + t * E_:at + (t + 1) * E_], (self.before if s == t else self.ones)[:], self.both[:, h, s],
                                      start=(s == 0), stop=(s == t))
        for s in range(NT):
            mm = self.nc.tensor.matmul(ps[:, 2 * at:2 * at + E_], self.ones[:], self.both[:, h, s], start=(s == 0), stop=(s == NT - 1))
        mm.then_inc(self.rank_ps, 1)

    def dve_slots(self, dve, own, pair, ps, base, rows):
        nc, at, hs, v = self.nc, NT * E_, pair.hs, self.nc.vector

        def places(h):
            own.done(v.tensor_tensor(self.pos[:, h], ps(h)[:, at:2 * at].rearrange("p (t e) -> p t e", t=NT), wide(base[:], [P, NT, E_]), ALU.add))

        def counted(h):
            own.done(v.tensor_tensor(base[:], base[:], ps(h)[:, 2 * at:2 * at + E_], ALU.add))

        def picked(h):
            for k in range(2):
                own.done(v.tensor_tensor(self.pick[:, h, k], self.hot[:, h, k], self.pos[:, h], ALU.mult))

        gate(dve, self.rank_ps, pair.graph(hs[1], 1), self.ticks_dve)
        own.wait()
        places(hs[0])
        own.wait()
        counted(hs[0])
        picked(hs[0])
        own.wait()
        places(hs[1])
        own.wait()
        counted(hs[1])
        picked(hs[1])
        own.wait()
        for h in hs:
            own.done(v.tensor_reduce(self.slot[:, h], self.pick[:, h], AX.X, ALU.add))
        gate(dve, self.gone, pair.graph(hs[1], 1), self.ticks_dve)
        own.wait()
        for h in hs:
            own.done(v.tensor_copy(rows[:, h, :, D], self.token[:, h]))
            own.done(v.tensor_copy(rows[:, h, :, D + 1], self.ixf[:, h, 0]))
        own.wait()
        for h in hs:
            own.done(v.tensor_scalar(self.token[:, h], self.token[:, h], float(N * self.ways), None, ALU.add))
        for h in hs:
            own.tell(v.tensor_copy(self.slot_i[:, h], self.slot[:, h]), self.slots, pair.graph(h, self.ways + 1))


WAYS = 4
QUADS = B // WAYS


class Stage:

    def __init__(self, i, s, off):
        self.i, self.s, self.off = i, s, off
        self.hs = (2 * s, 2 * s + 1)
        self.pair = 2 * i + (2 * off + s)

    def graph(self, h, plus=0):
        return WAYS * self.i + (WAYS * self.off + h + plus)

    def loads(self, each=16):
        return each * self.i + each * (self.off + 1)


def pipeline(eng, step):
    step(0, Stage(0, 0, 0), None, None)
    step(0, Stage(0, 1, 0), Stage(0, 0, 0), None)
    with eng.Fori(0, QUADS - 1) as i:
        step(i, Stage(i, 0, 1), Stage(i, 1, 0), Stage(i, 0, 0))
        step(i, Stage(i, 1, 1), Stage(i, 0, 1), Stage(i, 1, 0))
    last = QUADS - 1
    step(last, None, Stage(last, 1, 0), Stage(last, 0, 0))
    step(last, None, None, Stage(last, 1, 0))


def own_of(dve, sem, i, stages, counts):
    before = 0
    for stage, n in zip(stages, counts):
        before += n * (2 * stage.off + stage.s) if stage else 0
    if stages[0] is None:
        before += 2 * counts[0]
    if stages[1] is None and stages[0] is None:
        before += 2 * counts[1]
    return Own(dve, sem, i, 2 * sum(counts), before, sum(n for stage, n in zip(stages, counts) if stage))


def after_attention(nc, x, xn_d, ctx_d, wo, bo, g1, c1, w1, b1, w2, b2, g2, c2, identf, route, x1_d, base, gaps):
    with ExitStack() as c:
        sb = lambda n, s, d: c.enter_context(nc.sbuf_tensor("f_" + n, s, d))
        pb = lambda n, s, d: c.enter_context(nc.psum_tensor("f_" + n, s, d))
        fresh = Semaphores(c, nc)
        sem = lambda n: fresh("f_" + n)
        FC = 4
        ctx = sb("ctx", [P, WAYS, GROUPS, N], F32)
        xn = sb("xn", [P, WAYS, NT, D], F32)
        x0 = sb("x0", [P, WAYS, NT, D], F32)
        woT, w1T, w2T = sb("woT", [P, D], F32), sb("w1T", [P, FC * P], F32), sb("w2T", [P, FC, D], F32)
        b1c, b2c = sb("b1c", [P, FC], F32), sb("b2c", [P, 1], F32)
        rows = {n: sb(n, [P, D], F32) for n in ("bo", "g1", "c1", "g2", "c2")}
        eps = sb("eps", [P, 1], F32)
        rd = sb("rd", [P, WAYS, GROUPS, NT, GH], F32)
        cn = sb("cn", [P, WAYS, NT, D], F32)
        cT = sb("cT", [P, WAYS, N], F32)
        y = sb("y", [P, WAYS, NT, D], F32)
        yh = sb("yh", [P, WAYS, NT, D], F32)
        yT = sb("yT", [P, WAYS, N], F32)
        hT = sb("hT", [P, WAYS, FC, N], F32)
        zT = sb("zT", [P, WAYS, N], F32)
        z = sb("z", [P, WAYS, NT, D], F32)
        x1 = sb("x1", [P, WAYS, NT, D], F32)
        xo = sb("xo", [P, WAYS, NT, TAGGED], F32)
        into = [pb(f"into{n}", [P, N], F32) for n in range(2)]
        up = [pb(f"up{n}", [P, N], F32) for n in range(2)]
        down = pb("down", [P, N], F32)
        back = [pb(f"back{n}", [P, N], F32) for n in range(2)]
        small = pb("small", [P, 2, P], F32)
        weights_in, consts = sem("weights_in"), sem("consts")
        ctx_in, xn_in, x_in, x1_out = ([sem(f"{n}{h}") for h in range(WAYS)] for n in ("ctx_in", "xn_in", "x_in", "x1_out"))
        ctxT_ps, cn_ready, cnT_ps, cT_sb, o_ps, y_ready = (sem(n) for n in ("ctxT_ps", "cn_ready", "cnT_ps", "cT_sb", "o_ps", "y_ready"))
        yT_ps, yT_sb, ff1_ps, hT_sb, ff2_ps, zT_sb, z_ps = (sem(n) for n in ("yT_ps", "yT_sb", "ff1_ps", "hT_sb", "ff2_ps", "zT_sb", "z_ps"))
        x1_ready, xo_ready, xn_plus, x0_plus, summed, yh_ready, y_gained = (
            sem(n) for n in ("x1_ready", "xo_ready", "xn_plus", "x0_plus", "summed", "yh_ready", "y_gained"))
        dve_own, dve_ticks, sp_ticks, pool_ticks = sem("dve_own"), sem("dve_ticks"), sem("sp_ticks"), sem("pool_ticks")
        n1, n2, n3 = (Norm(c, nc, fresh, f"f_n{k}", WAYS) for k in range(3))
        r = Router(c, nc, fresh, "f_r", WAYS, *route, identf)
        r.ticks_dve = dve_ticks
        IN = 16 * 12

        with nc.Block() as block:
            @block.sync
            def _(sp):
                tiled = lambda src, b: src[b].rearrange("(t p) d -> p t d", p=P)

                def load_ctx(h, b, pair):
                    sp.dma_start(ctx[:, h], ctx_d[pair].rearrange("g p n -> p g n")).then_inc(ctx_in[h], 16)
                    sp.dma_start(xn[:, h], tiled(xn_d, b)).then_inc(xn_in[h], 16)

                def load_x(h, b):
                    sp.dma_start(x0[:, h], tiled(x, b)).then_inc(x_in[h], 16)

                def ctx_after(now):
                    for h in now.hs:
                        gate(sp, y_ready, now.graph(h, 1), sp_ticks)
                        at = GROUPS * WAYS * now.i + GROUPS * (WAYS * now.off + h + WAYS)
                        load_ctx(h, now.graph(h, WAYS), bass.ds(at, GROUPS))

                def store(now, more=True):
                    for h in now.hs:
                        gate(sp, x1_ready, now.graph(h, 1), sp_ticks)
                        sp.dma_start(tiled(x1_d, now.graph(h)), x1[:, h]).then_inc(x1_out[h], 16)
                        if more:
                            load_x(h, now.graph(h, WAYS))

                for t_, src in ((woT[:], wo), (w1T[:], w1), (w2T[:], w2)):
                    sp.dma_start(t_, src).then_inc(weights_in, 16)
                sp.dma_start(b1c[:], b1.rearrange("(a p) -> p a", p=P), allow_slow_non_contiguous=True).then_inc(weights_in, 16)
                sp.dma_start(b2c[:], b2.rearrange("(p a) -> p a", a=1), allow_slow_non_contiguous=True).then_inc(weights_in, 16)
                for n, src in (("bo", bo), ("g1", g1), ("c1", c1), ("g2", g2), ("c2", c2)):
                    sp.dma_start(rows[n][:], bcast_rows(src, P)).then_inc(weights_in, 16)
                r.load(sp, weights_in)
                for h in range(WAYS):
                    load_ctx(h, h, slice(GROUPS * h, GROUPS * h + GROUPS))
                    load_x(h, h)
                for s in range(2):
                    ctx_after(Stage(0, s, 0))
                with sp.Fori(0, QUADS - 2) as i:
                    for s in range(2):
                        store(Stage(i, s, 0))
                        ctx_after(Stage(i, s, 1))
                for s in range(2):
                    store(Stage(QUADS - 2, s, 0))
                for s in range(2):
                    store(Stage(QUADS - 1, s, 0), False)
                for h in range(WAYS):
                    sp.wait_ge(x1_out[h], 16 * (QUADS + 1))

            @block.gpsimd
            def _(pool):
                def plus_bo(now):
                    for h in now.hs:
                        gate(pool, xn_in[h], now.loads(), pool_ticks)
                        nc.gpsimd.tensor_tensor(xn[:, h], xn[:, h], wide(rows["bo"][:], [P, NT, D]), ALU.add).then_inc(xn_plus, 1)

                def plus_c2(now):
                    for h in now.hs:
                        gate(pool, x_in[h], now.loads(), pool_ticks)
                        nc.gpsimd.tensor_tensor(x0[:, h], x0[:, h], wide(rows["c2"][:], [P, NT, D]), ALU.add).then_inc(x0_plus, 1)

                def gained(now):
                    for h in now.hs:
                        gate(pool, yh_ready, now.graph(h, 1), pool_ticks)
                        nc.gpsimd.tensor_tensor(y[:, h], yh[:, h], wide(rows["g1"][:], [P, NT, D]), ALU.mult).then_inc(y_gained, 1)
                        gate(pool, y_gained, now.graph(h, 1), pool_ticks)
                        nc.gpsimd.tensor_tensor(y[:, h], y[:, h], wide(rows["c1"][:], [P, NT, D]), ALU.add).then_inc(y_ready, 1)

                def send(third):
                    for h in third.hs:
                        r.pool_send(pool, h, third.graph(h), xo[:, h])
                    r.pool_sent(pool, third.graph(third.hs[-1]))

                nc.gpsimd.memset(eps[:], EPS).then_inc(consts, 1)
                r.pool_start(pool, base)
                pool.wait_ge(weights_in, IN)
                for s in range(2):
                    plus_bo(Stage(0, s, 0))
                    plus_c2(Stage(0, s, 0))
                for s in range(2):
                    gained(Stage(0, s, 0))
                    plus_bo(Stage(0, s, 1))
                with pool.Fori(0, QUADS - 2) as i:
                    for s in range(2):
                        gained(Stage(i, s, 1))
                        send(Stage(i, s, 0))
                        plus_c2(Stage(i, s, 1))
                        plus_bo(Stage(i, s, 2))
                for s in range(2):
                    gained(Stage(QUADS - 2, s, 1))
                    send(Stage(QUADS - 2, s, 0))
                    plus_c2(Stage(QUADS - 2, s, 1))
                for s in range(2):
                    send(Stage(QUADS - 1, s, 0))

            @block.scalar
            def _(act):
                act.wait_ge(consts, 1)
                act.wait_ge(weights_in, IN)
                for h in range(WAYS):
                    act.sem_inc(x1_out[h], 16)
                act.sem_inc(hT_sb, 2)
                act.sem_inc(zT_sb, 1)

                def step(i, first, second, third):
                    def hidden(h):
                        for f in range(FC):
                            act.wait_ge(ff1_ps, FC * WAYS * i + (FC * (WAYS * second.off + h) + f + 1))
                            nc.scalar.activation(hT[:, h, f], up[f % 2][:], ACT.Relu, bias=b1c[:, f:f + 1]).then_inc(hT_sb, 1)

                    def heads(h):
                        act.wait_ge(cnT_ps, first.graph(h, 1))
                        nc.scalar.copy(cT[:, h], into[0][:]).then_inc(cT_sb, 1)

                    def fed(h):
                        act.wait_ge(ff2_ps, second.graph(h, 1))
                        nc.scalar.activation(zT[:, h], down[:], ACT.Identity, bias=b2c[:]).then_inc(zT_sb, 1)

                    if second:
                        for h in second.hs:
                            act.wait_ge(yT_ps, second.graph(h, 1))
                            nc.scalar.copy(yT[:, h], up[h % 2][:]).then_inc(yT_sb, 1)
                    if third:
                        n2.root(act, third.pair, eps, third.hs)
                    if second:
                        hidden(second.hs[0])
                    if first:
                        heads(first.hs[0])
                    if second:
                        hidden(second.hs[1])
                    if second:
                        fed(second.hs[0])
                    if first:
                        heads(first.hs[1])
                    if third:
                        n3.root(act, third.pair, eps, third.hs)
                        for h in third.hs:
                            act.wait_ge(r.gone, third.graph(h, 1))
                            n3.act_apply(act, third.pair, x1[:, h], xo[:, h, :, 0:D], h, xo_ready)
                    if second:
                        fed(second.hs[1])
                    if first:
                        n1.root(act, first.pair, eps, first.hs)
                    if third:
                        for h in third.hs:
                            r.act_turn(act, h, third.graph(h), back[h % 2])
                    if first:
                        for h in first.hs:
                            n1.act_apply(act, first.pair, y[:, h], yh[:, h], h, yh_ready)

                pipeline(act, step)

            @block.vector
            def _(dve):
                COUNTS = (26, 0, 98)
                v = nc.vector
                tiles = lambda ps: ps[:].rearrange("p (t d) -> p t d", t=NT)
                dve.wait_ge(r.consts, 8)
                dve.wait_ge(weights_in, IN)
                dve.sem_inc(dve_own, 1)
                dve.sem_inc(r.slots, WAYS)
                dve.sem_inc(summed, 1)

                def step(i, first, second, third):
                    own = own_of(dve, dve_own, i, (first, second, third), COUNTS)

                    def heads(h):
                        for g in range(GROUPS):
                            src = into[g][:].rearrange("p (t h d) -> p t h d", t=NT, h=GH)
                            dve.wait_ge(ctxT_ps, GROUPS * WAYS * i + (GROUPS * (WAYS * first.off + h) + g + 1))
                            own.done(v.reciprocal(rd[:, h, g], src[:, :, :, HD]))
                            own.wait()
                            ins = v.tensor_tensor(cn[:, h, :, g * GH * HD:(g + 1) * GH * HD].rearrange("p t (h d) -> p t h d", h=GH), src[:, :, :, 0:HD],
                                                  rd[:, h, g].rearrange("p t (h o) -> p t h o", o=1).broadcast_to([P, NT, GH, HD]), ALU.mult)
                            own.done(ins) if g == 0 else own.tell(ins, cn_ready, first.graph(h, 1))

                    def projected(h):
                        dve.wait_ge(xn_plus, first.graph(h, 1))
                        dve.wait_ge(o_ps, first.graph(h, 1))
                        own.wait()
                        own.tell(v.tensor_tensor(y[:, h], tiles(into[1]), xn[:, h], ALU.add), summed, first.graph(h, 2))
                        n1.stats_of(own, y[:, h], h)

                    if third:
                        for h in third.hs:
                            dve.wait_ge(z_ps, third.graph(h, 1))
                            own.done(v.tensor_tensor(z[:, h], tiles(back[h % 2]), y[:, h], ALU.add))
                            n2.stats_of(own, z[:, h], h)
                        n2.variance(dve, own, third.pair, dve_ticks, third.hs)
                        n2.inverse(dve, own, third.pair, third.hs)
                    if first:
                        heads(first.hs[0])
                    if third:
                        for h in third.hs:
                            if first and h == third.hs[1]:
                                projected(first.hs[0])
                                heads(first.hs[1])
                            dve.wait_ge(x0_plus, third.graph(h, 1))
                            dve.wait_ge(x1_out[h], third.loads())
                            n2.scaled(own, z[:, h], x1[:, h], h, rows["g2"][:], lambda t: x0[:, h, t], (x1_ready, third.graph(h, 1)))
                            n3.stats_of(own, x1[:, h], h)
                        n3.variance(dve, own, third.pair, dve_ticks, third.hs)
                        n3.inverse(dve, own, third.pair, third.hs, True)
                    if first:
                        if not third:
                            projected(first.hs[0])
                            heads(first.hs[1])
                        projected(first.hs[1])
                        n1.variance(dve, own, first.pair, dve_ticks, first.hs)
                        n1.inverse(dve, own, first.pair, first.hs, True)
                    if third:
                        r.dve_choose(dve, own, third, lambda h: small[:, h % 2],
                                     lambda h: gaps[:, bass.ds(NT * WAYS * i + NT * (WAYS * third.off + h), NT), :])
                        r.dve_slots(dve, own, third, lambda h: small[:, h % 2], base, xo)
                    own.end()

                pipeline(dve, step)

            @block.tensor
            def _(pe):
                pe.wait_ge(weights_in, IN)
                pe.wait_ge(r.consts, 8)

                def turned(ps, tile):
                    for t in range(NT):
                        mm = nc.tensor.transpose(ps[:, t * P:(t + 1) * P], tile(t), identf[:])
                    return mm

                def step(i, first, second, third):
                    def ctx_turned(h):
                        pe.wait_ge(ctx_in[h], first.loads())
                        pe.wait_ge(summed, first.graph(h, 1))
                        for g in range(GROUPS):
                            turned(into[g], lambda t: ctx[:, h, g, t * P:(t + 1) * P]).then_inc(ctxT_ps, 1)

                    def heads_turned(h):
                        pe.wait_ge(cn_ready, first.graph(h, 1))
                        turned(into[0], lambda t: cn[:, h, t]).then_inc(cnT_ps, 1)

                    def projected(h):
                        pe.wait_ge(cT_sb, first.graph(h, 1))
                        for t in range(NT):
                            mm = nc.tensor.matmul(into[1][:, t * P:(t + 1) * P], cT[:, h, t * P:(t + 1) * P], woT[:], start=True, stop=True)
                        mm.then_inc(o_ps, 1)

                    def fed_up(h):
                        pe.wait_ge(yT_sb, second.graph(second.hs[1], 1))
                        for f in range(FC):
                            pe.wait_ge(hT_sb, FC * WAYS * i + (FC * (WAYS * second.off + h) + f + 1))
                            nc.tensor.matmul(up[f % 2][:], w1T[:, f * P:(f + 1) * P], yT[:, h], start=True, stop=True).then_inc(ff1_ps, 1)

                    def fed_down(h):
                        pe.wait_ge(hT_sb, FC * WAYS * i + (FC * (WAYS * second.off + h) + FC + 2))
                        pe.wait_ge(zT_sb, second.graph(h, 1))
                        for f in range(FC):
                            mm = nc.tensor.matmul(down[:], w2T[:, f], hT[:, h, f], start=(f == 0), stop=(f == FC - 1))
                        mm.then_inc(ff2_ps, 1)

                    if second:
                        for h in second.hs:
                            pe.wait_ge(y_ready, second.graph(h, 1))
                            pe.wait_ge(hT_sb, FC * WAYS * i + (FC * (WAYS * second.off + second.hs[0]) + 2))
                            turned(up[h % 2], lambda t: y[:, h, t]).then_inc(yT_ps, 1)
                    if first:
                        ctx_turned(first.hs[0])
                    if second:
                        fed_up(second.hs[0])
                    if first:
                        heads_turned(first.hs[0])
                        projected(first.hs[0])
                    if second:
                        fed_up(second.hs[1])
                    if first:
                        ctx_turned(first.hs[1])
                    if second:
                        fed_down(second.hs[0])
                    if first:
                        heads_turned(first.hs[1])
                        projected(first.hs[1])
                    if second:
                        fed_down(second.hs[1])
                    if third:
                        for h in third.hs:
                            r.pe_turn(pe, h, third.graph(h), xo[:, h, :, 0:D], xo_ready, third.graph(h, 1), back[h % 2])
                        for h in third.hs:
                            pe.wait_ge(r.slots, third.graph(third.hs[0], WAYS))
                            r.pe_logits(pe, h, third.graph(h), small[:, h % 2])
                    if second:
                        for h in second.hs:
                            if third:
                                pe.wait_ge(r.gxT_sb, third.graph(third.hs[h % 2], 1))
                            pe.wait_ge(zT_sb, second.graph(h, 2))
                            turned(back[h % 2], lambda t: zT[:, h, t * P:(t + 1) * P]).then_inc(z_ps, 1)
                    if third:
                        for h in third.hs:
                            r.pe_rank(pe, h, third.graph(h), small[:, h % 2], 1 - h % 2)

                pipeline(pe, step)


def experts(nc, name, hc, func, base, xs_d, pack_d, y_d, identf):
    H = hc * P
    LOW = 2 * H
    W1, W2, B1, B2 = 0, H, 4 * H, 4 * H + hc
    WIDTH = 4 * H + hc + 1
    DEEP = 4
    TURNS = MOE_TILES // 4 - 1
    with ExitStack() as c:
        sb = lambda n, s, d: c.enter_context(nc.sbuf_tensor(name + n, s, d))
        pb = lambda n, s, d: c.enter_context(nc.psum_tensor(name + n, s, d))
        fresh = Semaphores(c, nc)
        sem = lambda n: fresh(name + n)
        K = B * N // TILE
        iota_e, iota_k, iota_j = sb("iota_e", [P, E_], I32), sb("iota_k", [P, K], I32), sb("iota_j", [P, MOE_TILES], I32)
        iota_l, spare, idle = sb("iota_l", [P, MOE_TILES], I32), sb("spare", [P, MOE_TILES], F32), sb("idle", [P, MOE_TILES], F32)
        caps, steps, js = sb("caps", [P, E_], F32), sb("steps", [P, K], F32), sb("js", [P, MOE_TILES], F32)
        ones = sb("ones", [P, E_], F32)
        count, need, upto = sb("count", [P, E_], F32), sb("need", [P, E_], F32), sb("upto", [P, E_], F32)
        over = sb("over", [P, E_, K], F32)
        past = sb("past", [P, 2, MOE_TILES, E_], F32)
        sums = sb("sums", [P, 2, MOE_TILES], F32)
        row = sb("row", [P, 2, MOE_TILES], F32)
        table = sb("table", [P, 2, MOE_TILES], I32)
        ends = sb("ends", [P, E_], I32)
        zeros = sb("zeros", [P, NT * TAGGED], F32)
        iota_r, nowhere = sb("iota_r", [P, MOE_TILES, NT], I32), sb("nowhere", [P, MOE_TILES * NT], F32)
        expert = sb("expert", [P, MOE_TILES * NT], F32)
        wrong = sb("wrong", [P, MOE_TILES * NT], F32)
        second, none, place = sb("second", [P, NT], F32), sb("none", [P, NT], F32), sb("place", [P, NT], F32)
        tags = sb("tags", [P, DEEP, NT, TAGGED - D], F32)
        goal = sb("goal", [P, 2, NT], I32)
        pack = [sb(f"pack{k}", [P, WIDTH], F32R) for k in range(DEEP)]
        xs = sb("xs", [P, DEEP, NT, TAGGED], F32)
        xT = sb("xT", [P, 2, 2, TILE], F32R)
        h_full = sb("h_full", [P, 2, hc, TILE], F32)
        h_high, h_low = sb("h_high", [P, 2, hc, TILE], F32R), sb("h_low", [P, 2, hc, TILE], F32R)
        yT = sb("yT", [P, 2, TILE], F32)
        ys = sb("ys", [P, 2, NT, D], F32)
        ps_x, ps_b = pb("ps_x", [P, TILE], F32), pb("ps_b", [P, TILE], F32)
        ps_h = [pb(f"ps_h{h}", [P, TILE], F32) for h in range(4)]
        ps_y = [pb(f"ps_y{h}", [P, TILE], F32) for h in range(2)]
        consts, dve_own, tables, zeroed = sem("consts"), sem("dve_own"), sem("tables"), (sem("zeroed0"), sem("zeroed1"))
        ends_ready = sem("ends_ready")
        x_in, w_in = [sem(f"x_in{k}") for k in range(DEEP)], [sem(f"w_in{k}") for k in range(DEEP)]
        y_out, y_free, goal_parts, goal_sum = (sem("y_out0"), sem("y_out1")), sem("y_free"), sem("goal_parts"), sem("goal_sum")
        xT_ps, xT_high, xT_sb, h_ps, h_sb, low_sb = (sem(n) for n in ("xT_ps", "xT_high", "xT_sb", "h_ps", "h_sb", "low_sb"))
        y_ps, yT_sb, back_ps, y_sb = (sem(n) for n in ("y_ps", "yT_sb", "back_ps", "y_sb"))
        ticks, sp_ticks = sem("ticks"), sem("sp_ticks")
        tile_at = lambda d, at: d[bass.ds(at, TILE), :].rearrange("(p t) d -> p (t d)", p=P)
        flat = lambda a: a.rearrange("p t d -> p (t d)")

        def zero_fill(eng, places, done):
            for e in places:
                at = E_ * CAP + (e - E_) * TILE if e >= E_ else eng.value_load(ends[0:1, e:e + 1], min_val=0, max_val=E_ * CAP)
                eng.dma_start(tile_at(xs_d, at), zeros[:]).then_inc(done, 16)

        with nc.Block() as block:
            @block.gpsimd
            def _(pool):
                g = nc.gpsimd
                g.iota(iota_e[:], pattern=[[CAP, E_]], base=0, channel_multiplier=0).then_inc(consts, 1)
                g.iota(iota_k[:], pattern=[[TILE, K]], base=0, channel_multiplier=0).then_inc(consts, 1)
                g.iota(iota_j[:], pattern=[[1, MOE_TILES]], base=0, channel_multiplier=0).then_inc(consts, 1)
                g.iota(iota_l[:], pattern=[[0, MOE_TILES // 2], [TILE, 2]], base=0, channel_multiplier=0).then_inc(consts, 1)
                g.memset(ones[:], 1.0).then_inc(consts, 1)
                g.memset(zeros[:], 0.0).then_inc(consts, 1)
                g.iota(iota_r[:], pattern=[[TILE, MOE_TILES], [1, NT]], base=RESULTS + 1, channel_multiplier=NT).then_inc(consts, 1)
                pool.wait_ge(consts, 7)
                pool.wait_ge(ends_ready, 1)
                zero_fill(g, range(0, E_ // 2 + 1), zeroed[0])

                def send(i, c):
                    h = c % 2
                    gate(pool, y_sb, 4 * i + (c + 2), ticks)
                    for t in range(NT):
                        g.indirect_dma_start(y_d, bass.IndirectOffsetOnAxis(goal[:, h, t:t + 1], 0), ys[:, h, t], None).then_inc(y_out[h], 16)

                def sent(i, c):
                    gate(pool, y_out[c % 2], 16 * NT * 2 * i + 16 * NT * (c // 2 + 1), ticks)
                    pool.sem_inc(y_free, 1)

                send(0, 0)
                with pool.Fori(0, TURNS) as i:
                    for c in range(1, 5):
                        send(i, c)
                        sent(i, c - 1)
                for c in range(1, 4):
                    send(TURNS, c)
                    sent(TURNS, c - 1)
                sent(TURNS, 3)

            @block.sync
            def _(sp):
                def load(i, c):
                    k = c % DEEP
                    e = sp.value_load(table[0:1, 0, bass.ds(4 * i + c, 1)], min_val=0, max_val=E_ - 1)
                    sp.dma_start(pack[k][:].bitcast(F32), pack_d[e]).then_inc(w_in[k], 16)
                    at = sp.value_load(table[0:1, 1, bass.ds(4 * i + c, 1)], min_val=0, max_val=LAST)
                    sp.dma_start(flat(xs[:, k]), tile_at(xs_d, at)).then_inc(x_in[k], 16)

                sp.wait_ge(consts, 7)
                sp.wait_ge(ends_ready, 1)
                zero_fill(sp, range(E_ // 2 + 1, E_ + 2), zeroed[1])
                sp.wait_ge(tables, 1)
                for done in zeroed:
                    sp.wait_ge(done, 16 * (E_ // 2 + 1))
                for c in range(DEEP):
                    load(0, c)
                with sp.Fori(0, MOE_TILES // DEEP - 1) as i:
                    for c in range(DEEP):
                        gate(sp, yT_sb, 4 * i + (c + 1), sp_ticks)
                        load(i, c + DEEP)

            @block.vector
            def _(dve):
                v = nc.vector
                dve.wait_ge(consts, 7)
                dve.sem_inc(dve_own, 1)
                own = Own(dve, dve_own, 0, 0)
                for dst, src in ((caps, iota_e), (steps, iota_k), (js, iota_j), (spare, iota_l)):
                    own.done(v.tensor_copy(dst[:], src[:]))
                own.tell(v.tensor_copy(ends[:], base[:]), ends_ready, 1)
                own.wait()
                own.done(v.tensor_tensor(count[:], base[:], caps[:], ALU.subtract))
                own.wait()
                own.done(v.tensor_tensor(over[:], count[:].rearrange("p (e o) -> p e o", o=1).broadcast_to([P, E_, K]), wide(steps[:], [P, E_, K]), ALU.is_gt))
                own.wait()
                own.done(v.tensor_reduce(need[:], over[:], AX.X, ALU.add))
                own.wait()
                own.done(v.tensor_tensor_scan(upto[:], ones[:], need[:], 0.0, ALU.mult, ALU.add))
                own.wait()
                each = [P, MOE_TILES, E_]
                own.done(v.tensor_tensor(past[:, 0], js[:].rearrange("p (j o) -> p j o", o=1).broadcast_to(each), wide(upto[:], each), ALU.is_ge))
                own.wait()
                own.done(v.tensor_tensor(past[:, 1], past[:, 0], wide(need[:], each), ALU.mult))
                own.wait()
                own.done(v.tensor_reduce(sums[:], past[:], AX.X, ALU.add))
                own.wait()
                own.done(v.tensor_tensor(row[:, 1], js[:], sums[:, 1], ALU.subtract))
                own.wait()
                own.done(v.tensor_scalar(row[:, 1], row[:, 1], float(TILE), None, ALU.mult))
                own.wait()
                own.done(v.scalar_tensor_tensor(out=row[:, 1], in0=sums[:, 0], scalar=float(CAP), in1=row[:, 1], op0=ALU.mult, op1=ALU.add))
                own.wait()
                own.done(v.tensor_scalar(idle[:], sums[:, 0], float(E_), float(ROWS), ALU.is_ge, ALU.mult))
                own.done(v.tensor_scalar(spare[:], spare[:], float(E_ * CAP), None, ALU.add))
                own.wait()
                own.done(v.tensor_tensor(row[:, 1], row[:, 1], idle[:], ALU.add))
                own.wait()
                own.done(v.tensor_tensor(row[:, 1], row[:, 1], spare[:], ALU.min))
                own.done(v.tensor_scalar(row[:, 0], sums[:, 0], float(E_ - 1), None, ALU.min))
                own.wait()
                own.tell(v.tensor_copy(table[:], row[:]), tables, 1)

                by_row = lambda x: x.rearrange("p (j t) -> p j t", t=NT)
                own.done(v.tensor_copy(nowhere[:], iota_r[:].rearrange("p j t -> p (j t)")))
                own.done(v.tensor_copy(by_row(expert[:]), row[:, 0].rearrange("p (j o) -> p j o", o=1).broadcast_to([P, MOE_TILES, NT])))
                own.wait()
                own.done(v.tensor_scalar(wrong[:], expert[:], 0.0, float(-B * N), ALU.is_gt, ALU.mult))
                own.wait()
                own.done(v.tensor_tensor(nowhere[:], nowhere[:], wrong[:], ALU.add))
                own.wait()

                def turned(i, c):
                    j, h = 4 * i + c, c % 2
                    dve.wait_ge(xT_ps, j + 1)
                    if c > 2:
                        dve.wait_ge(goal_sum, 4 * i + (c - 2))
                    v.tensor_copy(tags[:, c % DEEP], xs[:, c % DEEP, :, D:TAGGED])
                    v.tensor_copy(xT[:, h, 0], ps_x[:]).then_inc(xT_high, 1)
                    dve.wait_ge(xT_high, j + 1)
                    v.tensor_tensor(xT[:, h, 1], ps_x[:], xT[:, h, 0].bitcast(F32), ALU.subtract).then_inc(xT_sb, 1)

                def low(i, c, f):
                    h = c % 2
                    dve.wait_ge(h_sb, 4 * hc * i + (hc * c + f + 5))
                    v.tensor_tensor(h_low[:, h, f], h_full[:, h, f], h_high[:, h, f].bitcast(F32), ALU.subtract).then_inc(low_sb, 1)

                def result(i, c):
                    j, h = 4 * i + c, c % 2
                    token, first = tags[:, c % DEEP, :, 0], tags[:, c % DEEP, :, 1]
                    at = bass.ds(4 * NT * i + NT * c, NT)
                    dve.wait_ge(y_free, j + 1)
                    dve.wait_ge(goal_sum, 4 * i + (c + 1))
                    v.tensor_tensor(second[:], first, expert[:, at], ALU.not_equal).then_inc(goal_parts, 1)
                    v.scalar_tensor_tensor(out=none[:], in0=token, scalar=0.0, in1=nowhere[:, at], op0=ALU.is_equal, op1=ALU.mult).then_inc(goal_parts, 1)
                    dve.wait_ge(goal_parts, 8 * i + (2 * c + 2))
                    v.scalar_tensor_tensor(out=place[:], in0=second[:], scalar=float(B * N), in1=token, op0=ALU.mult, op1=ALU.add).then_inc(goal_sum, 1)
                    dve.wait_ge(goal_sum, 4 * i + (c + 2))
                    v.scalar_tensor_tensor(out=goal[:, h], in0=place[:], scalar=-1.0, in1=none[:], op0=ALU.add, op1=ALU.add)
                    dve.wait_ge(back_ps, j + 1)
                    v.tensor_copy(ys[:, h], ps_b[:].rearrange("p (t d) -> p t d", t=NT)).then_inc(y_sb, 1)

                def step(i, c, last=MOE_TILES):
                    if c + 1 < last:
                        for f in range(hc - 1):
                            low(i, c + 1, f)
                    if c + 2 < last:
                        turned(i, c + 2)
                    if c + 1 < last:
                        low(i, c + 1, hc - 1)
                    if not (isinstance(i, int) and i == 0 and c == 0):
                        result(i, c - 1)

                dve.sem_inc(y_sb, 1)
                dve.sem_inc(y_free, 2)
                dve.sem_inc(goal_sum, 1)
                turned(0, 0)
                turned(0, 1)
                for f in range(hc):
                    low(0, 0, f)
                step(0, 0)
                with dve.Fori(0, TURNS) as i:
                    for c in range(1, 5):
                        step(i, c)
                for c in range(1, 4):
                    step(TURNS, c, 4)
                result(TURNS, 3)

            @block.scalar
            def _(act):
                def hidden(i, c):
                    j, h = 4 * i + c, c % 2
                    act.wait_ge(y_ps, j + 1)
                    for f in range(hc):
                        n = hc * c + f
                        act.wait_ge(h_ps, 4 * hc * i + (n + 1))
                        bias = pack[c % DEEP][:, B1 + f:B1 + f + 1].bitcast(F32)
                        nc.scalar.activation(h_high[:, h, f], ps_h[n % 4][:], func, bias=bias)
                        nc.scalar.activation(h_full[:, h, f], ps_h[n % 4][:], func, bias=bias).then_inc(h_sb, 1)

                def biased(i, c):
                    j, h = 4 * i + c, c % 2
                    act.wait_ge(y_ps, j + 3)
                    nc.scalar.activation(yT[:, h], ps_y[h][:], ACT.Identity, bias=pack[c % DEEP][:, B2:B2 + 1].bitcast(F32)).then_inc(yT_sb, 1)

                act.sem_inc(h_sb, 4)
                hidden(0, 0)
                hidden(0, 1)
                biased(0, 0)
                with act.Fori(0, TURNS) as i:
                    for c in range(1, 5):
                        hidden(i, c + 1)
                        biased(i, c)
                for c in range(1, 4):
                    if c < 3:
                        hidden(TURNS, c + 1)
                    biased(TURNS, c)

            @block.tensor
            def _(pe):
                def turn(i, c):
                    k = c % DEEP
                    pe.wait_ge(x_in[k], 16 * (i + (c // DEEP + 1)))
                    if not (isinstance(i, int) and i == 0 and c == 0):
                        pe.wait_ge(xT_sb, 4 * i + c)
                    for t in range(NT):
                        mm = nc.tensor.transpose(ps_x[:, t * P:(t + 1) * P], xs[:, k, t, 0:D], identf[:])
                    mm.then_inc(xT_ps, 1)

                def products(out, weights, at, rows, start, stop):
                    high, low = weights[:, at:at + P], weights[:, LOW + at:LOW + at + P]
                    nc.tensor.matmul(out, high, rows[0], start=start, stop=False)
                    nc.tensor.matmul(out, high, rows[1], start=False, stop=False)
                    return nc.tensor.matmul(out, low, rows[0], start=False, stop=stop)

                def up(i, c):
                    k, h = c % DEEP, c % 2
                    pe.wait_ge(w_in[k], 16 * (i + (c // DEEP + 1)))
                    pe.wait_ge(xT_sb, 4 * i + (c + 1))
                    for f in range(hc):
                        n = hc * c + f
                        pe.wait_ge(h_sb, 4 * hc * i + (n + 1))
                        products(ps_h[n % 4][:], pack[k], W1 + f * P, (xT[:, h, 0], xT[:, h, 1]), True, True).then_inc(h_ps, 1)

                def down(i, c):
                    k, h = c % DEEP, c % 2
                    for f in range(hc):
                        pe.wait_ge(low_sb, 4 * hc * i + (hc * c + f + 1))
                        mm = products(ps_y[h][:], pack[k], W2 + f * P, (h_high[:, h, f], h_low[:, h, f]), f == 0, f == hc - 1)
                    mm.then_inc(y_ps, 1)

                def back(i, c):
                    h = c % 2
                    pe.wait_ge(yT_sb, 4 * i + (c + 1))
                    pe.wait_ge(y_sb, 4 * i + (c + 1))
                    for t in range(NT):
                        mm = nc.tensor.transpose(ps_b[:, t * P:(t + 1) * P], yT[:, h, t * P:(t + 1) * P], identf[:])
                    mm.then_inc(back_ps, 1)

                pe.sem_inc(y_ps, 2)
                turn(0, 0)
                turn(0, 1)
                up(0, 0)
                up(0, 1)
                turn(0, 2)
                down(0, 0)
                with pe.Fori(0, TURNS) as i:
                    for c in range(1, 5):
                        up(i, c + 1)
                        turn(i, c + 2)
                        back(i, c - 1)
                        down(i, c)
                for c in range(1, 4):
                    if c < 3:
                        up(TURNS, c + 1)
                    if c < 2:
                        turn(TURNS, c + 2)
                    back(TURNS, c - 1)
                    down(TURNS, c)
                back(TURNS, 3)


def split_weights(pool, nc, raw, high, low, rest, pack_in, pack_out, came, split, gone, hc, first):
    H2 = 2 * hc * P
    with pool.Fori(0, E_) as e:
        nc.gpsimd.dma_start(raw[:, 0:H2 + hc + 1], pack_in[e]).then_inc(came, 16)
        pool.wait_ge(came, 16 * e + (16 * first + 16))
        nc.gpsimd.tensor_tensor(high[:, 0:H2], raw[:, 0:H2], rest[:, 0:H2], ALU.add).then_inc(split, 1)
        pool.wait_ge(split, 2 * e + (2 * first + 1))
        nc.gpsimd.tensor_tensor(low[:, 0:H2], raw[:, 0:H2], high[:, 0:H2].bitcast(F32), ALU.subtract).then_inc(split, 1)
        gate(pool, split, 2 * e + (2 * first + 2), gone[1])
        nc.gpsimd.dma_start(pack_out[e][:, 0:H2], high[:, 0:H2].bitcast(F32)).then_inc(gone[0], 16)
        nc.gpsimd.dma_start(pack_out[e][:, H2:2 * H2], low[:, 0:H2].bitcast(F32)).then_inc(gone[0], 16)
        nc.gpsimd.dma_start(pack_out[e][:, 2 * H2:2 * H2 + hc + 1], raw[:, H2:H2 + hc + 1]).then_inc(gone[0], 16)
        gate(pool, gone[0], 48 * e + (48 * first + 48), gone[1])


class Results:

    def __init__(self, c, nc, fresh, name, ways, y_d, gaps, among):
        sb = lambda n, s, d: c.enter_context(nc.sbuf_tensor(name + n, s, d))
        sem = lambda n: fresh(name + n)
        self.nc, self.ways, self.gaps, self.among = nc, ways, gaps, among
        self.y_d = y_d[0:RESULTS].rearrange("(k b t p) d -> k b p t d", k=2, b=B, t=NT)
        self.e = sb("e", [P, B * NT, E_], F32)
        self.total = sb("total", [P, B * NT], F32)
        self.inv = sb("inv", [P, B * NT], F32)
        self.w = sb("w", [P, B * NT, 2], F32)
        self.wh = sb("wh", [P, ways, NT, 2], F32)
        self.y = sb("y", [P, ways, 2, NT, D], F32)
        self.exps, self.own = sem("exps"), sem("own")
        self.came = [sem(f"came{h}") for h in range(ways)]
        self.taken = sem("taken")

    def load(self, sp, h, b):
        for k in range(2):
            sp.dma_start(self.y[:, h, k], self.y_d[k, b]).then_inc(self.came[h], 16)

    def act_start(self, act):
        self.nc.scalar.activation(self.e[:], self.gaps[:], ACT.Exp).then_inc(self.exps, 1)

    def dve_start(self, dve, own):
        v, full = self.nc.vector, [P, B * NT, 2]
        dve.sem_inc(self.taken, self.ways)
        dve.wait_ge(self.exps, 1)
        own.done(v.tensor_reduce(self.total[:], self.e[:, :, 0:self.among], AX.X, ALU.add))
        own.wait()
        own.done(v.reciprocal(self.inv[:], self.total[:]))
        own.wait()
        own.done(v.tensor_tensor(self.w[:], self.e[:, :, 0:2], self.inv[:].rearrange("p (t o) -> p t o", o=1).broadcast_to(full), ALU.mult))
        own.wait()

    def dve_first(self, dve, own, h, came, b, x):
        v = self.nc.vector
        own.wait()
        own.done(v.tensor_copy(self.wh[:, h], self.w[:, bass.ds(b * NT, NT), :]))
        gate(dve, self.came[h], came, self.ticks_dve)
        self.plus(own, h, 0, x, self.y[:, h, 0], None)

    def dve_second(self, own, h, b, out):
        self.plus(own, h, 1, self.y[:, h, 0], out, (self.taken, b + (self.ways + 1)))

    def plus(self, own, h, k, x, out, last):
        own.wait()
        for t in range(NT):
            ins = self.nc.vector.scalar_tensor_tensor(out=out[:, t], in0=self.y[:, h, k, t], scalar=self.wh[:, h, t, k:k + 1], in1=x[:, t], op0=ALU.mult, op1=ALU.add)
            own.tell(ins, *last) if last and t == NT - 1 else own.done(ins)


R_ = 4
PARTS = 3


def relations(nc, x1_d, adjT_d, y_d, weight, bias, identf, route, x2_d, base, gaps, many):
    with ExitStack() as c:
        sb = lambda n, s, d: c.enter_context(nc.sbuf_tensor("g_" + n, s, d))
        pb = lambda n, s, d: c.enter_context(nc.psum_tensor("g_" + n, s, d))
        fresh = Semaphores(c, nc)
        sem = lambda n: fresh("g_" + n)
        xg = sb("xg", [P, WAYS, NT, D], F32)
        x1 = sb("x1", [P, WAYS, NT, D], F32)
        xn = sb("xn", [P, WAYS, NT, D], F32)
        xo = sb("xo", [P, WAYS, NT, TAGGED], F32)
        aT = sb("aT", [P, WAYS, NT, N], BF16)
        mask = sb("mask", [P, 2, R_, NT, N], BF16)
        wr = sb("wr", [P, R_ * D], F32)
        bc = sb("bc", [P, 1], F32)
        eps = sb("eps", [P, 1], F32)
        xT = sb("xT", [P, WAYS, N], F32)
        part = sb("part", [P, WAYS, PARTS, NT, R_ * D], BF16)
        rest = sb("rest", [P, NT, R_ * D], F32)
        oT = sb("oT", [P, WAYS, N], F32)
        banks = [[pb(f"b{h}{n}", [P, N], F32) for n in range(2)] for h in range(WAYS)]
        weights_in, consts = sem("weights_in"), sem("consts")
        x_in, a_in, x2_out = ([sem(f"{n}{h}") for h in range(WAYS)] for n in ("x_in", "a_in", "x2_out"))
        xn_ready, xT_ps, xT_sb, xw_ps, high_sb, rest_sb, mid_sb, parts_sb = (
            sem(n) for n in ("xn_ready", "xT_ps", "xT_sb", "xw_ps", "high_sb", "rest_sb", "mid_sb", "parts_sb"))
        masks, oT_ps, oT_sb, o_ps, x2_ready, xo_ready = (sem(n) for n in ("masks", "oT_ps", "oT_sb", "o_ps", "x2_ready", "xo_ready"))
        dve_own, dve_ticks, sp_ticks, pool_ticks = (sem(n) for n in ("dve_own", "dve_ticks", "sp_ticks", "pool_ticks"))
        n1, n2 = (Norm(c, nc, fresh, f"g_n{k}", WAYS) for k in range(2))
        new_gaps = gaps[1]
        r = Router(c, nc, fresh, "g_r", WAYS, *route, identf)
        q = Results(c, nc, fresh, "g_q", WAYS, y_d, gaps[0], E_)
        r.ticks_dve = q.ticks_dve = dve_ticks

        def by_kinds(eng, program):
            several = eng.value_load(many[0:1, 0:1], min_val=0, max_val=1)
            with eng.If(several == 0):
                program(1)
            with eng.Else():
                program(R_)

        with nc.Block() as block:
            @block.sync
            def _(sp):
                def load(h, b):
                    sp.dma_start(xg[:, h], x1_d[b].rearrange("(t p) d -> p t d", p=P)).then_inc(x_in[h], 16)
                    q.load(sp, h, b)
                    sp.dma_start(aT[:, h], adjT_d[b]).then_inc(a_in[h], 16)

                def load_next(now):
                    for h in now.hs:
                        gate(sp, q.taken, now.graph(h, WAYS + 1), sp_ticks)
                        gate(sp, masks, now.graph(h, 1), sp_ticks)
                        load(h, now.graph(h, WAYS))

                def store(now):
                    for h in now.hs:
                        gate(sp, x2_ready, now.graph(h, 1), sp_ticks)
                        sp.dma_start(x2_d[now.graph(h)].rearrange("(t p) d -> p t d", p=P), x1[:, h]).then_inc(x2_out[h], 16)

                sp.dma_start(wr[:].rearrange("p (r o) -> p r o", r=R_), weight.rearrange("r d o -> d r o")).then_inc(weights_in, 16)
                sp.dma_start(bc[:], bias.rearrange("(p a) -> p a", a=1), allow_slow_non_contiguous=True).then_inc(weights_in, 16)
                r.load(sp, weights_in)
                for h in range(WAYS):
                    load(h, h)
                with sp.Fori(0, QUADS - 1) as i:
                    load_next(Stage(i, 0, 0))
                    load_next(Stage(i, 1, 0))
                    store(Stage(i, 0, 0))
                    store(Stage(i, 1, 0))
                store(Stage(QUADS - 1, 0, 0))
                store(Stage(QUADS - 1, 1, 0))
                for h in range(WAYS):
                    sp.wait_ge(x2_out[h], 16 * (QUADS + 1))

            @block.gpsimd
            def _(pool):
                nc.gpsimd.memset(eps[:], EPS).then_inc(consts, 1)
                r.pool_start(pool, base)

                def send(third):
                    for h in third.hs:
                        r.pool_send(pool, h, third.graph(h), xo[:, h])
                    r.pool_sent(pool, third.graph(third.hs[-1]))

                def program(kinds):
                    def step(i, first, second, third):
                        if first:
                            for h in first.hs:
                                for t in range(NT):
                                    gate(pool, mid_sb, NT * WAYS * i + (NT * (WAYS * first.off + h) + t + 1), pool_ticks)
                                    nc.gpsimd.tensor_tensor(part[:, h, 2, t, 0:kinds * D], rest[:, t, 0:kinds * D], part[:, h, 1, t, 0:kinds * D],
                                                            ALU.subtract).then_inc(parts_sb, 1)
                        if third:
                            send(third)

                    pipeline(pool, step)

                pool.sem_inc(parts_sb, NT)
                by_kinds(pool, program)

            @block.scalar
            def _(act):
                q.act_start(act)
                act.wait_ge(consts, 1)
                act.wait_ge(weights_in, 16 * 4)

                def program(kinds):
                    def step(i, first, second, third):
                        if third:
                            for h in third.hs:
                                r.act_turn(act, h, third.graph(h), banks[h][0])
                        if first:
                            n1.root(act, first.pair, eps, first.hs)
                            for h in first.hs:
                                n1.act_apply(act, first.pair, x1[:, h], xn[:, h], h, xn_ready)
                        def summed(h):
                            act.wait_ge(oT_ps, second.graph(h, 3))
                            nc.scalar.activation(oT[:, h], banks[h][1][:], ACT.Identity, bias=bc[:], scale=1.0).then_inc(oT_sb, 1)

                        if second:
                            summed(second.hs[0])
                        if first:
                            for h in first.hs:
                                act.wait_ge(xT_ps, first.graph(h, 1))
                                nc.scalar.copy(xT[:, h], banks[h][0][:]).then_inc(xT_sb, 1)

                            def middle(h, t):
                                act.wait_ge(rest_sb, NT * WAYS * i + (NT * (WAYS * first.off + h) + t + 3))
                                nc.scalar.copy(part[:, h, 1, t, 0:kinds * D], rest[:, t, 0:kinds * D]).then_inc(mid_sb, 1)

                            for n in range(2 * NT):
                                h, t = first.hs[n // NT], n % NT
                                act.wait_ge(xw_ps, NT * WAYS * i + (NT * (WAYS * first.off + h) + t + 1))
                                nc.scalar.copy(part[:, h, 0, t, 0:kinds * D], banks[h][t % 2][:, 0:kinds * D]).then_inc(high_sb, 1)
                                if n > 0:
                                    middle(first.hs[(n - 1) // NT], (n - 1) % NT)
                            middle(first.hs[1], NT - 1)
                        if second:
                            summed(second.hs[1])
                            n2.root(act, second.pair, eps, second.hs)
                            for h in second.hs:
                                act.wait_ge(r.gone, second.graph(h, 1))
                                n2.act_apply(act, second.pair, x1[:, h], xo[:, h, :, 0:D], h, xo_ready)

                    pipeline(act, step)

                by_kinds(act, program)

            @block.vector
            def _(dve):
                v = nc.vector
                dve.wait_ge(r.consts, 8)
                dve.wait_ge(weights_in, 16 * 4)
                dve.sem_inc(dve_own, 1)
                dve.sem_inc(r.slots, WAYS)
                dve.sem_inc(rest_sb, 2)
                dve.sem_inc(oT_ps, 2)
                dve.sem_inc(xo_ready, WAYS)
                for h in range(WAYS):
                    dve.sem_inc(x2_out[h], 16)
                start = Own(dve, q.own, 0, 3)
                dve.sem_inc(q.own, 1)
                q.dve_start(dve, start)

                def program(kinds):
                    COUNTS = (34 + 2 * kinds, 20, 42)
                    def step(i, first, second, third):
                        own = own_of(dve, dve_own, i, (first, second, third), COUNTS)

                        def open_masks(h):
                            b = first.graph(h)
                            gate(dve, a_in[h], first.loads(), dve_ticks)
                            gate(dve, oT_ps, b + 1, dve_ticks)
                            for k in range(kinds):
                                ins = v.tensor_scalar(mask[:, h % 2, k], aT[:, h], float(k + 1), None, ALU.is_equal)
                                own.tell(ins, masks, b + 1) if k == kinds - 1 else own.done(ins)

                        if first:
                            for h in first.hs:
                                gate(dve, x_in[h], first.loads(), dve_ticks)
                                q.dve_first(dve, own, h, first.loads(16 * 2), first.graph(h), xg[:, h])
                            for h in first.hs:
                                gate(dve, x2_out[h], first.loads(), dve_ticks)
                                gate(dve, xo_ready, first.graph(h, 1), dve_ticks)
                                q.dve_second(own, h, first.graph(h), x1[:, h])
                                n1.stats_of(own, x1[:, h], h)
                            n1.variance(dve, own, first.pair, dve_ticks, first.hs)
                            n1.inverse(dve, own, first.pair, first.hs, True)
                        if third:
                            r.dve_choose(dve, own, third, lambda h: banks[h][1],
                                         lambda h: new_gaps[:, bass.ds(NT * WAYS * i + NT * (WAYS * third.off + h), NT), :])
                        if first:
                            open_masks(first.hs[0])
                        if third:
                            r.dve_slots(dve, own, third, lambda h: banks[h][1], base, xo)
                        if first:
                            for k in range(2 * NT):
                                h, t = first.hs[k // NT], k % NT
                                n = NT * WAYS * i + (NT * (WAYS * first.off + h) + t)
                                own.wait()
                                dve.wait_ge(high_sb, n + 1)
                                dve.wait_ge(parts_sb, n + 1)
                                own.tell(v.tensor_tensor(rest[:, t, 0:kinds * D], banks[h][t % 2][:, 0:kinds * D], part[:, h, 0, t, 0:kinds * D], ALU.subtract), rest_sb, n + 3)
                            open_masks(first.hs[1])
                        if second:
                            for h in second.hs:
                                b = second.graph(h)
                                dve.wait_ge(o_ps, b + 1)
                                own.tell(v.tensor_tensor(x1[:, h], x1[:, h], banks[h][0][:].rearrange("p (t d) -> p t d", t=NT), ALU.add), x2_ready, b + 1)
                                n2.stats_of(own, x1[:, h], h)
                            n2.variance(dve, own, second.pair, dve_ticks, second.hs)
                            n2.inverse(dve, own, second.pair, second.hs, True)
                        own.end()

                    pipeline(dve, step)

                by_kinds(dve, program)

            @block.tensor
            def _(pe):
                pe.wait_ge(weights_in, 16 * 4)
                pe.wait_ge(r.consts, 8)

                def turned_back(second, h):
                    pe.wait_ge(oT_sb, second.graph(h, 1))
                    for t in range(NT):
                        mm = nc.tensor.transpose(banks[h][0][:, t * P:(t + 1) * P], oT[:, h, t * P:(t + 1) * P], identf[:])
                    mm.then_inc(o_ps, 1)

                def program(kinds):
                    STEPS = [(t, k, s) for t in range(NT) for k in range(kinds) for s in range(PARTS)]
                    EACH = kinds * PARTS

                    def neighbours(second, h, steps):
                        if steps[0] == STEPS[0]:
                            pe.wait_ge(masks, second.graph(h, 1))
                            pe.wait_ge(parts_sb, NT * WAYS * second.i + NT * (WAYS * second.off + h + 2))
                        for t, k, s in steps:
                            mm = nc.tensor.matmul(banks[h][1][:], part[:, h, s, t, k * D:(k + 1) * D], mask[:, h % 2, k, t],
                                                  start=(t, k, s) == STEPS[0], stop=(t, k, s) == STEPS[-1])
                        if steps[-1] == STEPS[-1]:
                            mm.then_inc(oT_ps, 1)

                    def step(i, first, second, third):
                        if second:
                            neighbours(second, second.hs[0], STEPS)
                        if third:
                            for h in third.hs:
                                r.pe_turn(pe, h, third.graph(h), xo[:, h, :, 0:D], xo_ready, third.graph(h, WAYS + 1), banks[h][0])
                            for h in third.hs:
                                r.pe_logits(pe, h, third.graph(h), banks[h][1])
                        if second:
                            neighbours(second, second.hs[1], STEPS[:2 * EACH])
                        if third:
                            for h in third.hs:
                                r.pe_rank(pe, h, third.graph(h), banks[h][1])
                        if second:
                            turned_back(second, second.hs[0])
                            neighbours(second, second.hs[1], STEPS[2 * EACH:3 * EACH] if first else STEPS[2 * EACH:])
                        if first:
                            for h in first.hs:
                                pe.wait_ge(xn_ready, first.graph(h, 1))
                                pe.wait_ge(r.slots, first.graph(h, 1))
                                for t in range(NT):
                                    mm = nc.tensor.transpose(banks[h][0][:, t * P:(t + 1) * P], xn[:, h, t], identf[:])
                                mm.then_inc(xT_ps, 1)
                            for n in range(2 * NT):
                                h, t = first.hs[n // NT], n % NT
                                pe.wait_ge(xT_sb, first.graph(h, 1))
                                pe.wait_ge(rest_sb, NT * WAYS * i + (NT * (WAYS * first.off + h) + t + 1))
                                nc.tensor.matmul(banks[h][t % 2][:, 0:kinds * D], xT[:, h, t * P:(t + 1) * P], wr[:, 0:kinds * D], start=True, stop=True).then_inc(xw_ps, 1)
                                some = STEPS[3 * EACH + EACH * n // (2 * NT):3 * EACH + EACH * (n + 1) // (2 * NT)]
                                if second and some:
                                    neighbours(second, second.hs[1], some)
                        if second:
                            turned_back(second, second.hs[1])

                    pipeline(pe, step)

                by_kinds(pe, program)


def finish(nc, x2_d, y_d, gaps, out):
    with ExitStack() as c:
        fresh = Semaphores(c, nc)
        sem = lambda n: fresh("z_" + n)
        x2 = c.enter_context(nc.sbuf_tensor("z_x2", [P, WAYS, NT, D], F32))
        x3 = c.enter_context(nc.sbuf_tensor("z_x3", [P, WAYS, NT, D], F32))
        x_in, out_done = ([sem(f"{n}{h}") for h in range(WAYS)] for n in ("x_in", "out_done"))
        dve_own, dve_ticks, sp_ticks = sem("dve_own"), sem("dve_ticks"), sem("sp_ticks")
        q = Results(c, nc, fresh, "z_q", WAYS, y_d, gaps, 2)
        q.ticks_dve = dve_ticks
        tiled = lambda a, b: a[b].rearrange("(t p) d -> p t d", p=P)

        with nc.Block() as block:
            @block.sync
            def _(sp):
                def load(b, h):
                    sp.dma_start(x2[:, h], tiled(x2_d, b)).then_inc(x_in[h], 16)
                    q.load(sp, h, b)

                def store(b, h):
                    gate(sp, q.taken, b + (WAYS + 1), sp_ticks)
                    sp.dma_start(tiled(out, b), x3[:, h]).then_inc(out_done[h], 16)

                for h in range(WAYS):
                    load(h, h)
                with sp.Fori(0, QUADS - 1) as i:
                    for h in range(WAYS):
                        store(WAYS * i + h, h)
                        load(WAYS * i + (h + WAYS), h)
                for h in range(WAYS):
                    store(B - WAYS + h, h)
                for h in range(WAYS):
                    sp.wait_ge(out_done[h], 16 * (QUADS + 1))

            @block.scalar
            def _(act):
                q.act_start(act)

            @block.vector
            def _(dve):
                dve.sem_inc(q.own, 1)
                q.dve_start(dve, Own(dve, q.own, 0, 3))
                dve.sem_inc(dve_own, 1)
                for h in range(WAYS):
                    dve.sem_inc(out_done[h], 16)
                with dve.Fori(0, QUADS) as i:
                    own = Own(dve, dve_own, i, WAYS * 2 * NT)
                    for h in range(WAYS):
                        b = WAYS * i + h
                        gate(dve, x_in[h], 16 * i + 16, dve_ticks)
                        q.dve_first(dve, own, h, 32 * i + 32, b, x2[:, h])
                        gate(dve, out_done[h], 16 * i + 16, dve_ticks)
                        q.dve_second(own, h, b, x3[:, h])
                    own.end()


def build(nc, x, adj, wqkv, bqkv, wo, bo, g1, c1, w1, b1, w2, b2, g2, c2, gate0_w, gate0_b, pack0,
          rel_w, rel_b, gate1_w, gate1_b, pack1, out):
    dram = lambda n, s, d=F32: nc.dram_tensor(n, s, d, kind="Internal").ap()
    xn_d, x1_d, x2_d = (dram(n, (B, N, D)) for n in ("xn_d", "x1_d", "x2_d"))
    qk_d = dram("qk_d", (B, P, 2, 2, N))
    v_d = dram("v_d", (B, P, NT, HEADS, 32))
    adjT_d, neg_d = dram("adjT_d", (B, P, NT, N), BF16), dram("neg_d", (B, P, NT, N), BF16)
    ctx_d = dram("ctx_d", (UNITS, P, N))
    xs_d = [dram(f"xs{k}_d", (ROWS, TAGGED)) for k in range(2)]
    y_d = [dram(f"y{k}_d", (RESULTS + MOE_TILES * TILE, D)) for k in range(2)]
    split_d = [dram(f"split{k}_d", (E_, P, 4 * hc * P + hc + 1)) for k, hc in enumerate((2, 4))]
    with ExitStack() as c:
        sb = lambda n, s, d: c.enter_context(nc.sbuf_tensor(n, s, d))
        identf, identb = sb("identf", [P, P], F32), sb("identb", [P, P], BF16)
        base = [sb(f"base{k}", [P, E_], F32) for k in range(2)]
        gaps = [sb(f"gaps{k}", [P, B * NT, E_], F32) for k in range(2)]
        many = sb("many", [P, 1], I32)
        made = c.enter_context(nc.semaphore("made"))
        with nc.Block() as block:
            @block.gpsimd
            def _(pool):
                nc.gpsimd.memset(identf[:], 0.0).then_inc(made, 1)
                nc.gpsimd.memset(identb[:], 0.0).then_inc(made, 1)
                pool.wait_ge(made, 2)
                for m in (identf, identb):
                    nc.gpsimd.affine_select(out=m[:], in_=m[:], compare_op=ALU.not_equal, fill=1.0,
                                            base=0, pattern=[[-1, P]], channel_multiplier=1).then_inc(made, 1)
                pool.wait_ge(made, 4)
        prepare(nc, x, adj, wqkv, bqkv, identf, identb, xn_d, qk_d, v_d, adjT_d, neg_d, many)
        attend(nc, identf, identb, qk_d, v_d, neg_d, ctx_d, ((pack0, split_d[0], 2), (pack1, split_d[1], 4)))
        after_attention(nc, x, xn_d, ctx_d, wo, bo, g1, c1, w1, b1, w2, b2, g2, c2, identf,
                        (gate0_w, gate0_b, xs_d[0]), x1_d, base[0], gaps[0])
        experts(nc, "e0_", 2, ACT.Gelu, base[0], xs_d[0], split_d[0], y_d[0], identf)
        relations(nc, x1_d, adjT_d, y_d[0], rel_w, rel_b, identf, (gate1_w, gate1_b, xs_d[1]), x2_d, base[1], gaps, many)
        experts(nc, "e1_", 4, ACT.Relu, base[1], xs_d[1], split_d[1], y_d[1], identf)
        finish(nc, x2_d, y_d[1], gaps[1], out)


def kernel(**inputs):
    import numpy as np
    import concourse.bacc as bacc
    from concourse.bass_utils import run_bass_kernel_spmd

    a = {k: np.asarray(v) for k, v in inputs.items()}

    def pack(w1, b1, w2, b2):
        e, d, h = w1.shape
        c = h // P
        return np.concatenate([w1, w2.reshape(e, c, P, d).transpose(0, 2, 1, 3).reshape(e, P, h),
                               b1.reshape(e, c, P).transpose(0, 2, 1), b2[:, :, None]], axis=-1)

    arrays = {
        "x": a["x"], "adj": a["adj"],
        "wqkv": a["L0_gnn_Wqkv"].T, "bqkv": a["L0_gnn_bqkv"], "wo": a["L0_gnn_Wo"].T, "bo": a["L0_gnn_bo"],
        "g1": a["L0_gnn_ln1_g"], "c1": a["L0_gnn_ln1_b"], "w1": a["L0_gnn_W1"].T, "b1": a["L0_gnn_b1"],
        "w2": a["L0_gnn_W2"].T.reshape(4, P, D).transpose(1, 0, 2), "b2": a["L0_gnn_b2"],
        "g2": a["L0_gnn_ln2_g"], "c2": a["L0_gnn_ln2_b"],
        "gate0_w": a["L0_ffn_gate_w"], "gate0_b": a["L0_ffn_gate_b"],
        "pack0": pack(a["L0_ffn_W1"], a["L0_ffn_b1"], a["L0_ffn_W2"], a["L0_ffn_b2"]),
        "rel_w": a["L1_gnn_weight"], "rel_b": a["L1_gnn_bias"],
        "gate1_w": a["L1_ffn_Wg"].T, "gate1_b": a["L1_ffn_bg"],
        "pack1": pack(a["L1_ffn_W1"].transpose(0, 2, 1), a["L1_ffn_b1"], a["L1_ffn_W2"].transpose(0, 2, 1), a["L1_ffn_b2"]),
    }
    nc = bacc.Bacc("TRN2", target_bir_lowering=False, num_devices=1)
    given, args = {}, []
    for name, v in arrays.items():
        given[name] = np.ascontiguousarray(v)
        args.append(nc.dram_tensor(name, v.shape, mybir.dt.from_np(v.dtype), kind="ExternalInput").ap())
    out = nc.dram_tensor("out", (B, N, D), F32, kind="ExternalOutput").ap()
    build(nc, *args, out)
    result = run_bass_kernel_spmd(nc, [given], core_ids=[0])
    return result.results[0]["out"]
```
